# Optimizing a Trainium2 kernel written in Bass

```python
import numpy as np
import jax
import jax.numpy as jnp

def _softmax(x, axis=-1):
    return jax.nn.softmax(x, axis=axis)

def _gelu(x):
    return jax.nn.gelu(x, approximate=True)

def _silu(x):
    return jax.nn.silu(x)

def _sigmoid(x):
    return jax.nn.sigmoid(x)

def _layernorm(x, axis=-1, eps=1e-05):
    m = jnp.mean(x, axis=axis, keepdims=True)
    v = jnp.var(x, axis=axis, keepdims=True)
    return (x - m) / jnp.sqrt(v + eps)

def _scatter_add(tgt, idx, src, axis=0):
    return tgt.at[idx].add(src)

def _segment_sum(src, seg, n):
    return jax.ops.segment_sum(src, seg, n)
kernel_name = 'mk_vit_tower_cls_d4_tok_img768_r4_870944'

def setup_inputs(seed: int=0):
    np.random.seed(seed)
    _w = jnp.asarray

    def _rec_inputs():
        import jax
        import jax.numpy as jnp
        _rk = jax.random.key(seed)
        x = -0.00016672 + 0.999947 * jax.random.normal(jax.random.fold_in(_rk, 1), (64, 3, 96, 96), jnp.float32)
        cls_tok = 0.02 * jax.random.normal(jax.random.fold_in(_rk, 5), (1, 1, 192), jnp.float32)
        return (x, cls_tok)
    x, cls_tok = _rec_inputs()

    def _L0_tok_setup():
        import jax, jax.numpy as jnp
        import numpy as np
        IMAGE_SIZE = 96
        PATCH = 16
        EMBED = 192
        NUM_PATCHES = (IMAGE_SIZE // PATCH) ** 2
        PATCH_DIM = PATCH * PATCH * 3

        def _patchify(x, patch):
            b, c, h, w = x.shape
            nh, nw = (h // patch, w // patch)
            x = x.reshape(b, c, nh, patch, nw, patch)
            x = x.transpose(0, 2, 4, 1, 3, 5)
            return x.reshape(b, nh * nw, c * patch * patch)
        key = jax.random.key(seed)
        k1, k2, k3, k4, k5 = jax.random.split(key, 5)
        x = jax.random.normal(k1, (64, 3, IMAGE_SIZE, IMAGE_SIZE), dtype=jnp.float32)
        W_emb = jax.random.normal(k2, (PATCH_DIM, EMBED), dtype=jnp.float32) * 0.02
        b_emb = jnp.zeros((EMBED,), dtype=jnp.float32)
        pos_embedding = jax.random.normal(k3, (1, NUM_PATCHES + 1, EMBED), dtype=jnp.float32) * 0.02
        cls_token = jax.random.normal(k4, (1, 1, EMBED), dtype=jnp.float32) * 0.02
        return {'x': x, 'W_emb': W_emb, 'b_emb': b_emb, 'pos_embedding': pos_embedding, 'cls_token': cls_token}
    _L0_tok_all = _L0_tok_setup()
    _L0_tok_in = {k: v for k, v in _L0_tok_all.items() if k in ('W_emb', 'b_emb', 'pos_embedding', 'cls_token')}
    del _L0_tok_all

    def _L0_attn_setup():
        import jax, jax.numpy as jnp
        import numpy as np
        import math
        B, S, E = (2, 512, 192)
        H = 12
        V = 50257
        EPS = 1e-05

        def _layernorm(x, w):
            mu = jnp.mean(x, axis=-1, keepdims=True)
            var = jnp.mean(jnp.square(x - mu), axis=-1, keepdims=True)
            return (x - mu) * jax.lax.rsqrt(var + EPS) * w
        key = jax.random.key(seed)
        ks = jax.random.split(key, 7)
        x = jax.random.normal(ks[0], (B, S, E), dtype=jnp.float32)
        e = jax.random.normal(ks[1], (B, S, E), dtype=jnp.float32)
        p = jax.random.normal(ks[2], (B, S, E), dtype=jnp.float32)
        ln_w = jnp.ones((E,), dtype=jnp.float32)
        W_qk = 0.02 * jax.random.normal(ks[3], (H, E), dtype=jnp.float32)
        W_o = 0.02 / math.sqrt(2 * 12) * jax.random.normal(ks[4], (E, H * E), dtype=jnp.float32)
        wte = 0.02 * jax.random.normal(ks[5], (V, E), dtype=jnp.float32)
        return {'x': x, 'e': e, 'p': p, 'ln_w': ln_w, 'W_qk': W_qk, 'W_o': W_o, 'wte': wte}
    _L0_attn_all = _L0_attn_setup()
    _L0_attn_in = {k: v for k, v in _L0_attn_all.items() if k in ('e', 'p', 'ln_w', 'W_qk', 'W_o', 'wte')}
    del _L0_attn_all

    def _L0_ffn_setup():
        import jax, jax.numpy as jnp
        import numpy as np
        ACT_SCALE = 0.02
        W_SCALE = 0.01
        EFF_SCALE = ACT_SCALE * W_SCALE
        B, S, D, M = (8, 1024, 192, 192)
        key = jax.random.key(seed)
        kx, kw, kb = jax.random.split(key, 3)
        x = jax.random.normal(kx, (B, S, D), dtype=jnp.float32)
        weight_t = jax.random.randint(kw, (D, M), -128, 128, dtype=jnp.int32).astype(jnp.int8)
        bias = jax.random.normal(kb, (M,), dtype=jnp.float32)
        return {'x': x, 'weight_t': weight_t, 'bias': bias}
    _L0_ffn_all = _L0_ffn_setup()
    _L0_ffn_in = {k: v for k, v in _L0_ffn_all.items() if k in ('weight_t', 'bias')}
    del _L0_ffn_all

    def _L1_attn_setup():
        import jax, jax.numpy as jnp
        import numpy as np
        B, L, D, H = (2, 512, 192, 12)
        HD = D // H
        ROPE_BASE = 10000.0

        def apply_rope(x):
            d = x.shape[-1]
            pos = jnp.arange(x.shape[2], dtype=jnp.float32)
            inv_freq = 1.0 / ROPE_BASE ** (jnp.arange(0, d, 2, dtype=jnp.float32) / d)
            ang = pos[:, None] * inv_freq[None, :]
            cos = jnp.concatenate([jnp.cos(ang), jnp.cos(ang)], axis=-1)
            sin = jnp.concatenate([jnp.sin(ang), jnp.sin(ang)], axis=-1)
            x1, x2 = jnp.split(x, 2, axis=-1)
            rot = jnp.concatenate([-x2, x1], axis=-1)
            return x * cos[None, None, :, :].astype(x.dtype) + rot * sin[None, None, :, :].astype(x.dtype)
        key = jax.random.key(seed)
        ks = jax.random.split(key, 9)
        s = 1.0 / np.sqrt(D)
        return {'query': jax.random.normal(ks[0], (B, L, D), dtype=jnp.float32), 'Wq': jax.random.uniform(ks[1], (D, D), jnp.float32, -s, s), 'bq': jax.random.uniform(ks[2], (D,), jnp.float32, -s, s), 'Wk': jax.random.uniform(ks[3], (D, D), jnp.float32, -s, s), 'bk': jax.random.uniform(ks[4], (D,), jnp.float32, -s, s), 'Wv': jax.random.uniform(ks[5], (D, D), jnp.float32, -s, s), 'bv': jax.random.uniform(ks[6], (D,), jnp.float32, -s, s), 'Wo': jax.random.uniform(ks[7], (D, D), jnp.float32, -s, s), 'bo': jax.random.uniform(ks[8], (D,), jnp.float32, -s, s)}
    _L1_attn_all = _L1_attn_setup()
    _L1_attn_in = {k: v for k, v in _L1_attn_all.items() if k in ('Wq', 'bq', 'Wk', 'bk', 'Wv', 'bv', 'Wo', 'bo')}
    del _L1_attn_all

    def _L1_ffn_setup():
        import jax, jax.numpy as jnp
        import numpy as np
        B, S, H, F, E, TOP_K = (4, 512, 192, 768, 8, 2)
        key = jax.random.key(seed)
        ks = jax.random.split(key, 6)
        x = jax.random.normal(ks[0], (B, S, H), dtype=jnp.float32)
        Wr = jax.random.normal(ks[1], (E, H), dtype=jnp.float32) * 0.02
        Wi = jax.random.normal(ks[2], (E, F, H), dtype=jnp.float32) * 0.02
        bi = jnp.zeros((E, F), dtype=jnp.float32)
        Wo = jax.random.normal(ks[3], (E, H, F), dtype=jnp.float32) * 0.02
        bo = jnp.zeros((E, H), dtype=jnp.float32)
        return {'x': x, 'Wr': Wr, 'Wi': Wi, 'bi': bi, 'Wo': Wo, 'bo': bo}
    _L1_ffn_all = _L1_ffn_setup()
    _L1_ffn_in = {k: v for k, v in _L1_ffn_all.items() if k in ('Wr', 'Wi', 'bi', 'Wo', 'bo')}
    del _L1_ffn_all

    def _L2_attn_setup():
        import jax, jax.numpy as jnp
        import numpy as np
        BETA, ALPHA, NS_STEPS = (0.9, 1.0, 1)
        D_MODEL, D_STATE, D_CONV, EXPAND = (192, 16, 4, 2)
        D_INNER = EXPAND * D_MODEL
        DT_RANK = -(-D_MODEL // 16)
        B, L = (2, 256)

        def _newton_schulz(G, steps):
            a, b, c = (3.4445, -4.775, 2.0315)
            X = G / (jnp.linalg.norm(G, axis=(-2, -1), keepdims=True) + 1e-07)
            X = X.swapaxes(-2, -1)
            for _ in range(steps):
                A = X @ X.swapaxes(-2, -1)
                Bm = b * A + c * (A @ A)
                X = a * X + Bm @ X
            return X.swapaxes(-2, -1)
        key = jax.random.key(seed)
        ks = jax.random.split(key, 8)
        s = lambda k, shape, sc=0.02: jax.random.normal(k, shape, jnp.float32) * sc
        return {'hidden_states': jax.random.normal(ks[0], (B, L, D_MODEL), jnp.float32), 'in_proj_w': s(ks[1], (2 * D_INNER, D_MODEL)), 'conv_w': s(ks[2], (D_INNER, 1, D_CONV), 0.2), 'conv_b': jnp.zeros((D_INNER,), jnp.float32), 'x_proj_w': s(ks[3], (DT_RANK + 2 * D_STATE, D_INNER)), 'dt_head_w': s(ks[4], (D_INNER, DT_RANK)), 'dt_head_b': s(ks[5], (D_INNER,), 0.1), 'out_proj_w': s(ks[6], (D_MODEL, D_INNER)), 'D': jnp.ones((D_INNER,), jnp.float32)}
    _L2_attn_all = _L2_attn_setup()
    _L2_attn_in = {k: v for k, v in _L2_attn_all.items() if k in ('in_proj_w', 'conv_w', 'conv_b', 'x_proj_w', 'dt_head_w', 'dt_head_b', 'out_proj_w', 'D')}
    del _L2_attn_all

    def _L2_ffn_setup():
        import jax, jax.numpy as jnp
        import numpy as np
        NUM_EXPERTS = 8
        TOP_K = 2
        CAPACITY_FACTOR = 1.25
        MAX_GROUP_SIZE = 1024
        MIN_EXPERT_CAPACITY = 4

        def _moe_forward(x, w_router, wi, wo):
            B, T, D = x.shape
            E = NUM_EXPERTS
            num_tokens = B * T
            G = max(num_tokens // MAX_GROUP_SIZE, E)
            while num_tokens % G != 0 or G % E != 0:
                G += 1
            S = num_tokens // G
            C = max(int(TOP_K * CAPACITY_FACTOR * S / E), MIN_EXPERT_CAPACITY)
            xg = x.reshape(G, S, D)
            logits = jnp.einsum('gsd,de->gse', xg.astype(jnp.float32), w_router.astype(jnp.float32))
            probs = jax.nn.softmax(logits, axis=-1)
            gate, idx = jax.lax.top_k(probs, TOP_K)
            idx_kf = jnp.swapaxes(idx, 1, 2).reshape(G, TOP_K * S)
            mask = jax.nn.one_hot(idx_kf, E, dtype=jnp.int32)
            prio = jnp.cumsum(mask, axis=1) * mask - 1
            prio = jnp.swapaxes(prio.reshape(G, TOP_K, S, E), 1, 2)
            prio_se = prio.max(axis=2)
            gate_se = jnp.einsum('gsk,gske->gse', gate, jax.nn.one_hot(idx, E, dtype=gate.dtype))
            dispatch = jax.nn.one_hot(prio_se, C, dtype=x.dtype)
            combine = dispatch * gate_se[..., None].astype(x.dtype)
            expert_in = jnp.einsum('gsec,gsd->egcd', dispatch, xg)
            h = jax.nn.relu(jnp.einsum('egcd,edf->egcf', expert_in, wi))
            expert_out = jnp.einsum('egcf,efd->egcd', h, wo)
            out = jnp.einsum('gsec,egcd->gsd', combine, expert_out)
            return out.reshape(B, T, D)
        key = jax.random.key(seed)
        k1, k2, k3, k4 = jax.random.split(key, 4)
        B, T, D, F = (8, 256, 192, 768)
        x = jax.random.normal(k1, (B, T, D), jnp.float32)
        w_router = jax.random.normal(k2, (D, NUM_EXPERTS), jnp.float32) * D ** (-0.5)
        wi = jax.random.normal(k3, (NUM_EXPERTS, D, F), jnp.float32) * D ** (-0.5)
        wo = jax.random.normal(k4, (NUM_EXPERTS, F, D), jnp.float32) * F ** (-0.5)
        return {'x': x, 'w_router': w_router, 'wi': wi, 'wo': wo}
    _L2_ffn_all = _L2_ffn_setup()
    _L2_ffn_in = {k: v for k, v in _L2_ffn_all.items() if k in ('w_router', 'wi', 'wo')}
    del _L2_ffn_all

    def _L3_attn_setup():
        import jax, jax.numpy as jnp
        import numpy as np
        NUM_HEADS = 8

        def _attn(q, k, v, scale):
            a = jax.nn.softmax(jnp.einsum('bhqd,bhkd->bhqk', q, k) * scale, axis=-1)
            return jnp.einsum('bhqk,bhkd->bhqd', a, v)
        key = jax.random.key(seed)
        k1, k2, k3 = jax.random.split(key, 3)
        B, N, C = (8, 256, 192)
        x = jax.random.normal(k1, (B, N, C), dtype=jnp.float32)
        w_qkv = jax.random.normal(k2, (3 * C, C), dtype=jnp.float32) * 0.02
        w_proj = jax.random.normal(k3, (C, C), dtype=jnp.float32) * 0.02
        b_proj = jnp.zeros((C,), dtype=jnp.float32)
        return {'x': x, 'w_qkv': w_qkv, 'w_proj': w_proj, 'b_proj': b_proj}
    _L3_attn_all = _L3_attn_setup()
    _L3_attn_in = {k: v for k, v in _L3_attn_all.items() if k in ('w_qkv', 'w_proj', 'b_proj')}
    del _L3_attn_all

    def _L3_ffn_setup():
        import jax, jax.numpy as jnp
        import numpy as np
        B, N, DIM, HEADS = (4, 256, 192, 12)
        HIDDEN, E, TOPK = (768, 8, 2)
        EPS = 1e-05

        def _layernorm(x, g, b):
            mu = jnp.mean(x, axis=-1, keepdims=True)
            var = jnp.var(x, axis=-1, keepdims=True)
            return (x - mu) * jax.lax.rsqrt(var + EPS) * g + b
        key = jax.random.key(seed)
        ks = jax.random.split(key, 10)
        s = 0.02
        return {'x': jax.random.normal(ks[0], (B, N, DIM), dtype=jnp.float32), 'ln1_g': jnp.ones((DIM,), jnp.float32), 'ln1_b': jnp.zeros((DIM,), jnp.float32), 'qkv_w': jax.random.normal(ks[1], (3 * DIM, DIM), jnp.float32) * s, 'proj_w': jax.random.normal(ks[2], (DIM, DIM), jnp.float32) * s, 'proj_b': jnp.zeros((DIM,), jnp.float32), 'ln2_g': jnp.ones((DIM,), jnp.float32), 'ln2_b': jnp.zeros((DIM,), jnp.float32), 'gate_w': jax.random.normal(ks[3], (E, DIM), jnp.float32) * s, 'gate_b': jnp.zeros((E,), jnp.float32), 'w1': jax.random.normal(ks[4], (E, HIDDEN, DIM), jnp.float32) * s, 'b1': jnp.zeros((E, HIDDEN), jnp.float32), 'w2': jax.random.normal(ks[5], (E, DIM, HIDDEN), jnp.float32) * s, 'b2': jnp.zeros((E, DIM), jnp.float32)}
    _L3_ffn_all = _L3_ffn_setup()
    _L3_ffn_in = {k: v for k, v in _L3_ffn_all.items() if k in ('ln1_g', 'ln1_b', 'qkv_w', 'proj_w', 'proj_b', 'ln2_g', 'ln2_b', 'gate_w', 'gate_b', 'w1', 'b1', 'w2', 'b2')}
    del _L3_ffn_all
    return {'x': x, 'cls_tok': cls_tok, 'L0_tok_W_emb': _L0_tok_in['W_emb'], 'L0_tok_b_emb': _L0_tok_in['b_emb'], 'L0_tok_pos_embedding': _L0_tok_in['pos_embedding'], 'L0_tok_cls_token': _L0_tok_in['cls_token'], 'L0_attn_e': _L0_attn_in['e'], 'L0_attn_p': _L0_attn_in['p'], 'L0_attn_ln_w': _L0_attn_in['ln_w'], 'L0_attn_W_qk': _L0_attn_in['W_qk'], 'L0_attn_W_o': _L0_attn_in['W_o'], 'L0_attn_wte': _L0_attn_in['wte'], 'L0_ffn_weight_t': _L0_ffn_in['weight_t'], 'L0_ffn_bias': _L0_ffn_in['bias'], 'L1_attn_Wq': _L1_attn_in['Wq'], 'L1_attn_bq': _L1_attn_in['bq'], 'L1_attn_Wk': _L1_attn_in['Wk'], 'L1_attn_bk': _L1_attn_in['bk'], 'L1_attn_Wv': _L1_attn_in['Wv'], 'L1_attn_bv': _L1_attn_in['bv'], 'L1_attn_Wo': _L1_attn_in['Wo'], 'L1_attn_bo': _L1_attn_in['bo'], 'L1_ffn_Wr': _L1_ffn_in['Wr'], 'L1_ffn_Wi': _L1_ffn_in['Wi'], 'L1_ffn_bi': _L1_ffn_in['bi'], 'L1_ffn_Wo': _L1_ffn_in['Wo'], 'L1_ffn_bo': _L1_ffn_in['bo'], 'L2_attn_in_proj_w': _L2_attn_in['in_proj_w'], 'L2_attn_conv_w': _L2_attn_in['conv_w'], 'L2_attn_conv_b': _L2_attn_in['conv_b'], 'L2_attn_x_proj_w': _L2_attn_in['x_proj_w'], 'L2_attn_dt_head_w': _L2_attn_in['dt_head_w'], 'L2_attn_dt_head_b': _L2_attn_in['dt_head_b'], 'L2_attn_out_proj_w': _L2_attn_in['out_proj_w'], 'L2_attn_D': _L2_attn_in['D'], 'L2_ffn_w_router': _L2_ffn_in['w_router'], 'L2_ffn_wi': _L2_ffn_in['wi'], 'L2_ffn_wo': _L2_ffn_in['wo'], 'L3_attn_w_qkv': _L3_attn_in['w_qkv'], 'L3_attn_w_proj': _L3_attn_in['w_proj'], 'L3_attn_b_proj': _L3_attn_in['b_proj'], 'L3_ffn_ln1_g': _L3_ffn_in['ln1_g'], 'L3_ffn_ln1_b': _L3_ffn_in['ln1_b'], 'L3_ffn_qkv_w': _L3_ffn_in['qkv_w'], 'L3_ffn_proj_w': _L3_ffn_in['proj_w'], 'L3_ffn_proj_b': _L3_ffn_in['proj_b'], 'L3_ffn_ln2_g': _L3_ffn_in['ln2_g'], 'L3_ffn_ln2_b': _L3_ffn_in['ln2_b'], 'L3_ffn_gate_w': _L3_ffn_in['gate_w'], 'L3_ffn_gate_b': _L3_ffn_in['gate_b'], 'L3_ffn_w1': _L3_ffn_in['w1'], 'L3_ffn_b1': _L3_ffn_in['b1'], 'L3_ffn_w2': _L3_ffn_in['w2'], 'L3_ffn_b2': _L3_ffn_in['b2']}

def reference(x, cls_tok, L0_tok_W_emb, L0_tok_b_emb, L0_tok_pos_embedding, L0_tok_cls_token, L0_attn_e, L0_attn_p, L0_attn_ln_w, L0_attn_W_qk, L0_attn_W_o, L0_attn_wte, L0_ffn_weight_t, L0_ffn_bias, L1_attn_Wq, L1_attn_bq, L1_attn_Wk, L1_attn_bk, L1_attn_Wv, L1_attn_bv, L1_attn_Wo, L1_attn_bo, L1_ffn_Wr, L1_ffn_Wi, L1_ffn_bi, L1_ffn_Wo, L1_ffn_bo, L2_attn_in_proj_w, L2_attn_conv_w, L2_attn_conv_b, L2_attn_x_proj_w, L2_attn_dt_head_w, L2_attn_dt_head_b, L2_attn_out_proj_w, L2_attn_D, L2_ffn_w_router, L2_ffn_wi, L2_ffn_wo, L3_attn_w_qkv, L3_attn_w_proj, L3_attn_b_proj, L3_ffn_ln1_g, L3_ffn_ln1_b, L3_ffn_qkv_w, L3_ffn_proj_w, L3_ffn_proj_b, L3_ffn_ln2_g, L3_ffn_ln2_b, L3_ffn_gate_w, L3_ffn_gate_b, L3_ffn_w1, L3_ffn_b1, L3_ffn_w2, L3_ffn_b2):
    import jax
    import jax.numpy as jnp

    def _L0_tok_ref(x, W_emb, b_emb, pos_embedding, cls_token):
        import jax, jax.numpy as jnp
        import numpy as np
        IMAGE_SIZE = 96
        PATCH = 16
        EMBED = 192
        NUM_PATCHES = (IMAGE_SIZE // PATCH) ** 2
        PATCH_DIM = PATCH * PATCH * 3

        def _patchify(x, patch):
            b, c, h, w = x.shape
            nh, nw = (h // patch, w // patch)
            x = x.reshape(b, c, nh, patch, nw, patch)
            x = x.transpose(0, 2, 4, 1, 3, 5)
            return x.reshape(b, nh * nw, c * patch * patch)
        b = x.shape[0]
        patches = _patchify(x, PATCH)
        tok = jnp.einsum('bnd,de->bne', patches, W_emb) + b_emb
        cls = jnp.broadcast_to(cls_token, (b, 1, EMBED))
        tok = jnp.concatenate([cls, tok], axis=1)
        return tok + pos_embedding[:, :tok.shape[1], :]

    def _L0_attn_ref(x, e, p, ln_w, W_qk, W_o, wte):
        import jax, jax.numpy as jnp
        import numpy as np
        import math
        B, S, E = (2, 512, 192)
        H = 12
        V = 50257
        EPS = 1e-05

        def _layernorm(x, w):
            mu = jnp.mean(x, axis=-1, keepdims=True)
            var = jnp.mean(jnp.square(x - mu), axis=-1, keepdims=True)
            return (x - mu) * jax.lax.rsqrt(var + EPS) * w
        xb, sb, eb = x.shape
        xn = _layernorm(x, ln_w)
        avg_wte = jnp.mean(wte, axis=0)
        Q = xn[:, None, :, :] * W_qk[None, :, None, :]
        attn = jnp.einsum('bhse,bhte->bhst', Q, Q) / math.sqrt(eb)
        causal = jnp.tril(jnp.ones((sb, sb), dtype=bool))
        attn = jnp.where(causal[None, None], attn, -jnp.inf)
        attn = jax.nn.softmax(attn, axis=-1)
        Vv = xn[:, None, :, :] - avg_wte[None, None, None, :]
        out = jnp.einsum('bhst,bhte->bhse', attn, Vv)
        N_reg = 1.0 / jnp.arange(1, sb + 1, dtype=jnp.float32)
        out = out * N_reg[None, None, :, None]
        out = out.transpose(0, 2, 1, 3).reshape(xb, sb, H * eb)
        out = out @ W_o.T
        return out

    def _L0_ffn_ref(x, weight_t, bias):
        import jax, jax.numpy as jnp
        import numpy as np
        ACT_SCALE = 0.02
        W_SCALE = 0.01
        EFF_SCALE = ACT_SCALE * W_SCALE
        B, S, D, M = (8, 1024, 192, 192)
        orig_shape = x.shape
        x_flat = x.reshape(-1, orig_shape[-1])
        x_int8 = jnp.clip(jnp.round(x_flat / ACT_SCALE), -128, 127).astype(jnp.int8)
        acc_i32 = jnp.matmul(x_int8, weight_t, preferred_element_type=jnp.int32)
        out = acc_i32.astype(jnp.float32) * jnp.float32(EFF_SCALE) + bias
        return out.reshape(orig_shape[:-1] + (M,))

    def _L1_attn_ref(query, Wq, bq, Wk, bk, Wv, bv, Wo, bo):
        import jax, jax.numpy as jnp
        import numpy as np
        B, L, D, H = (2, 512, 192, 12)
        HD = D // H
        ROPE_BASE = 10000.0

        def apply_rope(x):
            d = x.shape[-1]
            pos = jnp.arange(x.shape[2], dtype=jnp.float32)
            inv_freq = 1.0 / ROPE_BASE ** (jnp.arange(0, d, 2, dtype=jnp.float32) / d)
            ang = pos[:, None] * inv_freq[None, :]
            cos = jnp.concatenate([jnp.cos(ang), jnp.cos(ang)], axis=-1)
            sin = jnp.concatenate([jnp.sin(ang), jnp.sin(ang)], axis=-1)
            x1, x2 = jnp.split(x, 2, axis=-1)
            rot = jnp.concatenate([-x2, x1], axis=-1)
            return x * cos[None, None, :, :].astype(x.dtype) + rot * sin[None, None, :, :].astype(x.dtype)
        b, l, _ = query.shape
        q = (query @ Wq.T + bq).reshape(b, l, H, HD).transpose(0, 2, 1, 3)
        k = (query @ Wk.T + bk).reshape(b, l, H, HD).transpose(0, 2, 1, 3)
        v = (query @ Wv.T + bv).reshape(b, l, H, HD).transpose(0, 2, 1, 3)
        q = apply_rope(q)
        k = apply_rope(k)
        scores = jnp.einsum('bhqd,bhkd->bhqk', q, k) / np.sqrt(HD).astype(np.float32)
        causal = jnp.triu(jnp.ones((l, l), dtype=bool), k=1)
        scores = jnp.where(causal[None, None, :, :], -jnp.inf, scores)
        attn = jax.nn.softmax(scores, axis=-1)
        out = jnp.einsum('bhqk,bhkd->bhqd', attn, v)
        out = out.transpose(0, 2, 1, 3).reshape(b, l, D)
        return out @ Wo.T + bo

    def _L1_ffn_ref(x, Wr, Wi, bi, Wo, bo):
        import jax, jax.numpy as jnp
        import numpy as np
        B, S, H, F, E, TOP_K = (4, 512, 192, 768, 8, 2)
        xf = x.reshape(-1, x.shape[-1])
        router_logits = jnp.einsum('th,eh->te', xf, Wr)
        topk_vals, topk_idx = jax.lax.top_k(router_logits, TOP_K)
        routing_weights = jax.nn.softmax(topk_vals, axis=-1)
        h = jnp.einsum('th,efh->etf', xf, Wi) + bi[:, None, :]
        h = jax.nn.gelu(h, approximate=False)
        expert_out = jnp.einsum('etf,ehf->eth', h, Wo) + bo[:, None, :]
        expert_out = jnp.transpose(expert_out, (1, 0, 2))
        gathered = jnp.take_along_axis(expert_out, topk_idx[:, :, None], axis=1)
        out = jnp.einsum('tk,tkh->th', routing_weights, gathered)
        return out.reshape(x.shape)

    def _L2_attn_ref(hidden_states, in_proj_w, conv_w, conv_b, x_proj_w, dt_head_w, dt_head_b, out_proj_w, D):
        import jax, jax.numpy as jnp
        import numpy as np
        BETA, ALPHA, NS_STEPS = (0.9, 1.0, 1)
        D_MODEL, D_STATE, D_CONV, EXPAND = (192, 16, 4, 2)
        D_INNER = EXPAND * D_MODEL
        DT_RANK = -(-D_MODEL // 16)
        B, L = (2, 256)

        def _newton_schulz(G, steps):
            a, b, c = (3.4445, -4.775, 2.0315)
            X = G / (jnp.linalg.norm(G, axis=(-2, -1), keepdims=True) + 1e-07)
            X = X.swapaxes(-2, -1)
            for _ in range(steps):
                A = X @ X.swapaxes(-2, -1)
                Bm = b * A + c * (A @ A)
                X = a * X + Bm @ X
            return X.swapaxes(-2, -1)
        Bz, Lz, _ = hidden_states.shape
        dtype = hidden_states.dtype
        xz = jnp.einsum('bld,ed->ble', hidden_states, in_proj_w)
        x, z = jnp.split(xz, 2, axis=-1)
        xc = jax.lax.conv_general_dilated(x.swapaxes(1, 2), conv_w, (1,), [(D_CONV - 1, 0)], dimension_numbers=('NCH', 'OIH', 'NCH'), feature_group_count=D_INNER)
        x = jax.nn.silu(xc.swapaxes(1, 2) + conv_b)
        x_dbl = jnp.einsum('bld,ed->ble', x, x_proj_w)
        dt_low, k, q = jnp.split(x_dbl, [DT_RANK, DT_RANK + D_STATE], axis=-1)
        dt = jnp.einsum('blr,dr->bld', dt_low, dt_head_w)

        def step(carry, inp):
            v, h = carry
            x_t, dt_t, k_t, q_t = inp
            dt_t = jax.nn.sigmoid(dt_t + dt_head_b)
            dt_t = dt_t / (1.0 + dt_t * jnp.sum(k_t * k_t, axis=-1, keepdims=True))
            dA = 1.0 - dt_t[:, :, None] * (k_t * k_t)[:, None, :]
            G = (dt_t * x_t)[:, :, None] * k_t[:, None, :]
            v = BETA * v + ALPHA * _newton_schulz(G, NS_STEPS)
            h = dA * h + v
            y_t = jnp.einsum('bdn,bn->bd', h, q_t) + D * x_t
            return ((v, h), y_t)
        init = (jnp.zeros((Bz, D_INNER, D_STATE), dtype), jnp.zeros((Bz, D_INNER, D_STATE), dtype))
        xs = (x.swapaxes(0, 1), dt.swapaxes(0, 1), k.swapaxes(0, 1), q.swapaxes(0, 1))
        _, y = jax.lax.scan(step, init, xs)
        y = y.swapaxes(0, 1) * jax.nn.silu(z)
        return jnp.einsum('bld,od->blo', y, out_proj_w)

    def _L2_ffn_ref(x, w_router, wi, wo):
        import jax, jax.numpy as jnp
        import numpy as np
        NUM_EXPERTS = 8
        TOP_K = 2
        CAPACITY_FACTOR = 1.25
        MAX_GROUP_SIZE = 1024
        MIN_EXPERT_CAPACITY = 4

        def _moe_forward(x, w_router, wi, wo):
            B, T, D = x.shape
            E = NUM_EXPERTS
            num_tokens = B * T
            G = max(num_tokens // MAX_GROUP_SIZE, E)
            while num_tokens % G != 0 or G % E != 0:
                G += 1
            S = num_tokens // G
            C = max(int(TOP_K * CAPACITY_FACTOR * S / E), MIN_EXPERT_CAPACITY)
            xg = x.reshape(G, S, D)
            logits = jnp.einsum('gsd,de->gse', xg.astype(jnp.float32), w_router.astype(jnp.float32))
            probs = jax.nn.softmax(logits, axis=-1)
            gate, idx = jax.lax.top_k(probs, TOP_K)
            idx_kf = jnp.swapaxes(idx, 1, 2).reshape(G, TOP_K * S)
            mask = jax.nn.one_hot(idx_kf, E, dtype=jnp.int32)
            prio = jnp.cumsum(mask, axis=1) * mask - 1
            prio = jnp.swapaxes(prio.reshape(G, TOP_K, S, E), 1, 2)
            prio_se = prio.max(axis=2)
            gate_se = jnp.einsum('gsk,gske->gse', gate, jax.nn.one_hot(idx, E, dtype=gate.dtype))
            dispatch = jax.nn.one_hot(prio_se, C, dtype=x.dtype)
            combine = dispatch * gate_se[..., None].astype(x.dtype)
            expert_in = jnp.einsum('gsec,gsd->egcd', dispatch, xg)
            h = jax.nn.relu(jnp.einsum('egcd,edf->egcf', expert_in, wi))
            expert_out = jnp.einsum('egcf,efd->egcd', h, wo)
            out = jnp.einsum('gsec,egcd->gsd', combine, expert_out)
            return out.reshape(B, T, D)
        return _moe_forward(x, w_router, wi, wo)

    def _L3_attn_ref(x, w_qkv, w_proj, b_proj):
        import jax, jax.numpy as jnp
        import numpy as np
        NUM_HEADS = 8

        def _attn(q, k, v, scale):
            a = jax.nn.softmax(jnp.einsum('bhqd,bhkd->bhqk', q, k) * scale, axis=-1)
            return jnp.einsum('bhqk,bhkd->bhqd', a, v)
        B, N, C = x.shape
        H = NUM_HEADS
        hd = C // H
        g = hd // 3
        scale = hd ** (-0.5)
        qkv = (x @ w_qkv.T).reshape(B, N, 3, H, hd).transpose(2, 0, 3, 1, 4)
        q, k, v = (qkv[0], qkv[1], qkv[2])
        q3, q4, q5 = (q[..., :g], q[..., g:2 * g], q[..., 2 * g:])
        k3, k4, k5 = (k[..., :g], k[..., g:2 * g], k[..., 2 * g:])
        v3, v4, v5 = (v[..., :g], v[..., g:2 * g], v[..., 2 * g:])

        def merge(o):
            return o.transpose(0, 2, 1, 3).reshape(B, N, C // 3)
        x3 = merge(_attn(q4, jnp.concatenate([k3, k4], axis=2), jnp.concatenate([v3, v4], axis=2), scale))
        x4 = merge(_attn(q5, jnp.concatenate([k3, k5], axis=2), jnp.concatenate([v3, v5], axis=2), scale))
        x5 = merge(_attn(q5, jnp.concatenate([k4, k5], axis=2), jnp.concatenate([v4, v5], axis=2), scale))
        out = jnp.concatenate([x3, x4, x5], axis=2)
        return out @ w_proj.T + b_proj

    def _L3_ffn_ref(x, ln1_g, ln1_b, qkv_w, proj_w, proj_b, ln2_g, ln2_b, gate_w, gate_b, w1, b1, w2, b2):
        import jax, jax.numpy as jnp
        import numpy as np
        B, N, DIM, HEADS = (4, 256, 192, 12)
        HIDDEN, E, TOPK = (768, 8, 2)
        EPS = 1e-05

        def _layernorm(x, g, b):
            mu = jnp.mean(x, axis=-1, keepdims=True)
            var = jnp.var(x, axis=-1, keepdims=True)
            return (x - mu) * jax.lax.rsqrt(var + EPS) * g + b
        b, n, d = x.shape
        hd = d // HEADS
        scale = hd ** (-0.5)
        h = _layernorm(x, ln1_g, ln1_b)
        qkv = h @ qkv_w.T
        qkv = qkv.reshape(b, n, 3, HEADS, hd).transpose(2, 0, 3, 1, 4)
        q, k, v = (qkv[0], qkv[1], qkv[2])
        attn = jax.nn.softmax(jnp.einsum('bhnd,bhmd->bhnm', q, k) * scale, axis=-1)
        a = jnp.einsum('bhnm,bhmd->bhnd', attn, v)
        a = a.transpose(0, 2, 1, 3).reshape(b, n, d)
        a = a @ proj_w.T + proj_b
        x = x + a
        h2 = _layernorm(x, ln2_g, ln2_b)
        t = h2.reshape(-1, d)
        T = t.shape[0]
        logits = t @ gate_w.T + gate_b
        top_val, top_idx = jax.lax.top_k(logits, TOPK)
        score = jax.nn.softmax(top_val, axis=-1)
        cw = jnp.zeros((T, E), t.dtype).at[jnp.arange(T)[:, None], top_idx].add(score)
        out = jnp.zeros_like(t)
        for e in range(E):
            he = jax.nn.gelu(t @ w1[e].T + b1[e], approximate=False)
            ye = he @ w2[e].T + b2[e]
            out = out + cw[:, e:e + 1] * ye
        return x + out.reshape(b, n, d)
    h = _L0_tok_ref(x, L0_tok_W_emb, L0_tok_b_emb, L0_tok_pos_embedding, L0_tok_cls_token)
    h = jnp.concatenate([jnp.broadcast_to(cls_tok, (h.shape[0], 1, h.shape[2])), h], axis=1)
    h = h + _L0_attn_ref(_layernorm(h, axis=-1), L0_attn_e, L0_attn_p, L0_attn_ln_w, L0_attn_W_qk, L0_attn_W_o, L0_attn_wte)
    h = h + _L0_ffn_ref(_layernorm(h, axis=-1), L0_ffn_weight_t, L0_ffn_bias)
    h = h + _L1_attn_ref(_layernorm(h, axis=-1), L1_attn_Wq, L1_attn_bq, L1_attn_Wk, L1_attn_bk, L1_attn_Wv, L1_attn_bv, L1_attn_Wo, L1_attn_bo)
    h = h + _L1_ffn_ref(_layernorm(h, axis=-1), L1_ffn_Wr, L1_ffn_Wi, L1_ffn_bi, L1_ffn_Wo, L1_ffn_bo)
    h = h + _L2_attn_ref(_layernorm(h, axis=-1), L2_attn_in_proj_w, L2_attn_conv_w, L2_attn_conv_b, L2_attn_x_proj_w, L2_attn_dt_head_w, L2_attn_dt_head_b, L2_attn_out_proj_w, L2_attn_D)
    h = h + _L2_ffn_ref(_layernorm(h, axis=-1), L2_ffn_w_router, L2_ffn_wi, L2_ffn_wo)
    h = h + _L3_attn_ref(_layernorm(h, axis=-1), L3_attn_w_qkv, L3_attn_w_proj, L3_attn_b_proj)
    h = h + _L3_ffn_ref(_layernorm(h, axis=-1), L3_ffn_ln1_g, L3_ffn_ln1_b, L3_ffn_qkv_w, L3_ffn_proj_w, L3_ffn_proj_b, L3_ffn_ln2_g, L3_ffn_ln2_b, L3_ffn_gate_w, L3_ffn_gate_b, L3_ffn_w1, L3_ffn_b1, L3_ffn_w2, L3_ffn_b2)
    return h

_drawn_inputs = setup_inputs


def setup_inputs(seed=0):
    import zlib

    import numpy as np

    out = dict(_drawn_inputs(seed))
    spreads = {'L0_tok_b_emb': (0.0, 0.1),
     'L0_attn_ln_w': (1.0, 0.2),
     'L1_ffn_bi': (0.0, 0.8),
     'L1_ffn_bo': (0.0, 0.8),
     'L2_attn_conv_b': (0.0, 0.8),
     'L2_attn_D': (1.0, 0.6),
     'L3_attn_b_proj': (0.0, 2.0),
     'L3_ffn_ln1_g': (1.0, 0.6),
     'L3_ffn_ln1_b': (0.0, 0.8),
     'L3_ffn_proj_b': (0.0, 2.0),
     'L3_ffn_ln2_g': (1.0, 0.6),
     'L3_ffn_ln2_b': (0.0, 0.8),
     'L3_ffn_gate_b': (0.0, 0.8),
     'L3_ffn_b1': (0.0, 2.0),
     'L3_ffn_b2': (0.0, 2.0)}
    factors = {'L0_attn_W_qk': 8.0,
     'L0_attn_wte': 29.732,
     'L1_attn_Wq': 8.0,
     'L1_attn_bq': 8.0,
     'L1_attn_Wk': 8.0,
     'L1_attn_bk': 8.0,
     'L1_attn_Wv': 4.203,
     'L1_attn_bv': 8.0,
     'L1_attn_Wo': 4.041,
     'L1_attn_bo': 8.0,
     'L1_ffn_Wr': 6.974,
     'L1_ffn_Wi': 8.0,
     'L1_ffn_Wo': 8.0,
     'L2_attn_in_proj_w': 8.0,
     'L2_attn_conv_w': 8.0,
     'L2_attn_x_proj_w': 8.0,
     'L2_attn_dt_head_w': 8.0,
     'L2_attn_dt_head_b': 8.0,
     'L2_attn_out_proj_w': 8.0,
     'L3_attn_w_qkv': 8.0,
     'L3_attn_w_proj': 8.0,
     'L3_ffn_qkv_w': 8.0,
     'L3_ffn_proj_w': 8.0,
     'L3_ffn_gate_w': 7.863,
     'L3_ffn_w1': 8.0,
     'L3_ffn_w2': 8.0,
     'L2_ffn_w_router': 8.0,
     'L2_ffn_wi': 8.0,
     'L2_ffn_wo': 8.0}
    for name, (base, spread) in spreads.items():
        noise = np.random.default_rng([zlib.crc32(name.encode()), seed]).standard_normal(out[name].shape)
        drawn = base * np.exp(spread * noise) if base else spread * noise
        out[name] = jnp.asarray(drawn.astype(out[name].dtype))
    for name, factor in factors.items():
        out[name] = (out[name] * factor).astype(out[name].dtype)
    return out
```

```python
from contextlib import ExitStack, contextmanager

import numpy as np

import concourse.bass as bass
from concourse import mybir

F32 = mybir.dt.float32
BF16 = mybir.dt.bfloat16
I8 = mybir.dt.int8
I32 = mybir.dt.int32
ALU = mybir.AluOpType
ACT = mybir.ActivationFunctionType
AX_X = mybir.AxisListType.X
ds = bass.ds

P = 128
IMAGES, SEQ, DIM = 64, 38, 192
TOKENS = IMAGES * SEQ
TILES = TOKENS // P
KT = 2
KD = DIM // KT
GROUPS = 8
GI = IMAGES // GROUPS
GT = GI * SEQ
GPAD = GT + 64
PAIRS = GI // 2
SLOT = 64
HEADS = 12
HPK = HEADS // KT
HD = DIM // HEADS
G3 = 3 * SEQ
PATCH_K = 6
INNER, CI, STATE, RANK = 384, 3, 16, 12
EXPERTS, HIDDEN, FT = 8, 768, 6
CAPACITY = 95
WTE_ROWS = 50257
WTE_R = 4
WTE_CH = WTE_ROWS // P // WTE_R
WTE_TAIL = WTE_ROWS - WTE_CH * WTE_R * P
PARTS, NH3, HD3, KF = 8, 8, 8, 64
EPS = 1e-5
MASKED = -1e30
MAGIC = 12582912.0
TGROUPS = [(s, min(512, TOKENS - s)) for s in range(0, TOKENS, 512)]
CREDITS = 2


class Count:

    def __init__(self, sem, base=0):
        self.sem, self.base = sem, base

    def at(self, base):
        return Count(self.sem, base)

    def done(self, k):
        return self.base + k + 1 + CREDITS

    def freed(self, k):
        return self.base + k + 1


class Chain:

    def __init__(self, eng, sem):
        self.eng, self.sem, self.n, self.reg = eng, sem, 0, 0

    def step(self, ins):
        ins.then_inc(self.sem, 1)
        self.n += 1

    def settle(self):
        self.eng.wait_ge(self.sem, self.reg + self.n)

    @contextmanager
    def loop(self, count, per):
        start, outer = self.n, self.reg
        with self.eng.Fori(0, count) as i:
            self.reg = outer + i * per
            yield i
            assert self.n - start == per, f"{self.n - start} steps in a loop body, not {per}"
        self.reg = outer
        self.n = start + per * count


def ring(eng, n, chain=None, per=0):
    with (chain.loop(n // 2, 2 * per) if chain and per else eng.Fori(0, n // 2)) as i:
        yield 2 * i, 0
        yield 2 * i + 1, 1
    if n % 2:
        yield n - 1, 0
BASES = {
    "L0": (0, (0, 0), (0, 0)),
    "L1": (8, (32, 32), (128, 128)),
    "L3": (16, (64, 64), (160, 160)),
    "L3f": (24, (160, 96), (160, 192)),
}
PJ_BASE = {"L1": 0, "L3": 64, "L3f": 104}
HALVES = [(0, 1), (0, 2), (1, 2)]
QUERY = [0, 1, 1]
TURNING = [False, True, True, True, True, True, True, True, False, True, True]
TURNS = [TILES * sum(TURNING[:i]) for i in range(len(TURNING))]
ARENA = 21600
EARLY_LOADS = 6
EXTRA = {"mixed": 4, "h_ready": 4, "y_sum": 20}
PROJ = {"L0": 0, "L0f": 1, "L1": 2, "L2": 3, "L3": 4, "L3f": 5}
SSM_STEPS = 35
SLOW_FROM = 3


def build(nc, spec, t_in, out):
    with ExitStack() as ctx:
        def sb(name, shape, dt=F32):
            return ctx.enter_context(nc.sbuf_tensor(name, shape, dt))

        def sem(name):
            return ctx.enter_context(nc.semaphore(name))

        h = sb("h", [P, TILES * DIM])
        kept = sb("kept", [P, TILES * DIM])
        xT = sb("xT", [KD, KT, TOKENS])
        zT = sb("zT", [P, CI, TOKENS])
        resident = sb("resident", [P, spec["resident"]])
        normed = sb("normed", [P, 2, DIM])
        ztile = sb("ztile", [P, 2, CI * P])
        stats = sb("stats", [P, TILES * 6])
        mean_var = sb("mean_var", [P, TILES * 2])
        deviation = sb("deviation", [P, TILES])
        rstd = sb("rstd", [P, TILES])
        newton = sb("newton", [P, TILES])
        gates = sb("gates", [P, TILES * EXPERTS])
        wte_sum = sb("wte_sum", [P, WTE_R * DIM])
        avg_wte = sb("avg_wte", [KD, KT])
        w_int8 = sb("w_int8", [KD, KT * DIM // 4], I32)
        arena = sb("arena", [P, ARENA])
        bank = ctx.enter_context(nc.psum_tensor("bank", [P, 8, 512], F32))

        def const(name):
            blob, rows, first, cols = spec[name]
            assert blob == "resident"
            return resident[0:rows, first:first + cols]

        class Carve:
            def __init__(self):
                self.at = 0

            def __call__(self, rows, *dims):
                n = int(np.prod(dims))
                view = arena[0:rows, self.at:self.at + n]
                self.at += n
                assert self.at <= ARENA, self.at
                if len(dims) > 1:
                    names = [f"d{i}" for i in range(len(dims))]
                    view = view.rearrange(f"p ({' '.join(names)}) -> p {' '.join(names)}",
                                          **{n: d for n, d in zip(names[1:], dims[1:])})
                return view

        COUNTS = ("normed_ready turned xT_ready stats_var stats_sd tile_staged proj_sum proj_added rows_ready patch_sum "
                  "patch_taken wte_added prepared pj_sum pj_taken qk_ready kbd_ready scores_ready shifted exped sum_taken "
                  "probs_ready turned_probs probs_in tokens_copied v_sum v_in o_sum o_taken "
                  "wo_sum wo_taken mean_sum mean_in offset_sum h_sum h_ready y_sum y_added "
                  "logit_sum logit_in logit_turned routed exp_in exp_out choice_sum choice_in keep_turned cw_turned cw_in b2_sum b2_added mixed quant "
                  "in_sum in_taken z_gate conv_out conv_gate x_ready low_sum low_in dt_sum dt_gate k2_sum k2_in dx_ready dx_squared dx_sum "
                  "norm_in norm_out w_ready q_sum q_in lists_turned lists_in lists_spread v_expanded a_in scanned weighed reduced").split()
        counts = {n: Count(sem(n)) for n in COUNTS}

        def cnt(name, base=0):
            return counts[name].at(base)

        load_early, load_resident, load_wo = sem("load_early"), sem("load_resident"), sem("load_wo")
        load_tail, stage_ended, stored = sem("load_tail"), sem("stage_ended"), sem("stored")
        patch_loaded = [sem(f"patch_loaded{b}") for b in range(2)]
        wte_loaded = [sem(f"wte_loaded{b}") for b in range(2)]
        expert_loaded = [sem(f"expert_loaded{b}") for b in range(2)]
        chains = {n: sem(f"chain_{n}") for n in ("pe", "dve", "act", "pool")}
        step_apart = sem("step_apart")

        def wait_apart(eng, sem_, value):
            eng.wait_ge(sem_, value)
            eng.sem_inc(step_apart, 1)

        ident = const("ident")
        cols = lambda x, first, n=1: x[:, ds(first, n)]
        tile_h = lambda x, t: x[:, ds(t * DIM, DIM)]

        def ln_dve(dve, ch, i, source, keep=None, turn=True):
            with ch.loop(TILES, 1) as t:
                ch.step(nc.vector.bn_stats(stats[:, ds(6 * t, 6)], tile_h(source, t)))
            ch.settle()
            for t in range(TILES):
                ch.step(nc.vector.bn_aggr(mean_var[:, 2 * t:2 * t + 2], stats[:, 6 * t:6 * t + 6]))
            ch.settle()
            var = mean_var[:, :].rearrange("p (t two) -> p two t", two=2)[:, 1, :]
            nc.vector.tensor_scalar(deviation[:, :], var, EPS, None, ALU.add).then_inc(cnt("stats_var").sem, 1)
            dve.wait_ge(cnt("stats_sd").sem, cnt("stats_sd", i).done(0))
            ch.step(nc.vector.reciprocal(rstd[:, :], newton[:, :]))
            ch.settle()
            ch.step(nc.vector.tensor_tensor(newton[:, :], rstd[:, :], rstd[:, :], ALU.mult))
            ch.settle()
            ch.step(nc.vector.tensor_tensor(newton[:, :], newton[:, :], deviation[:, :], ALU.mult))
            ch.settle()
            ch.step(nc.vector.tensor_scalar(newton[:, :], newton[:, :], -0.5, 1.5, ALU.mult, ALU.add))
            ch.settle()
            ch.step(nc.vector.tensor_tensor(rstd[:, :], rstd[:, :], newton[:, :], ALU.mult))
            ch.settle()
            if keep is not None:
                with ch.loop(TILES, 1) as t:
                    ch.step(nc.vector.tensor_scalar(tile_h(keep, t), tile_h(source, t), cols(mean_var, 2 * t),
                                                    cols(rstd, t), ALU.subtract, ALU.mult))
            if turn:
                ready, turned = cnt("normed_ready", TURNS[i]), cnt("turned", TURNS[i])
                for t, b in ring(dve, TILES):
                    dve.wait_ge(turned.sem, turned.freed(t))
                    nc.vector.tensor_scalar(normed[:, b, :], tile_h(source, t), cols(mean_var, 2 * t),
                                            cols(rstd, t), ALU.subtract, ALU.mult).then_inc(ready.sem, 1)

        def ln_pe(pe, i):
            ready, turned, taken = (cnt(n, TURNS[i]) for n in ("normed_ready", "turned", "xT_ready"))
            for t, b in ring(pe, TILES):
                pe.wait_ge(ready.sem, ready.done(t))
                pe.wait_ge(taken.sem, taken.freed(t))
                for k in range(KT):
                    last = nc.tensor.transpose(bank[0:KD, b, k * P:(k + 1) * P], normed[:, b, k * KD:(k + 1) * KD], ident)
                last.then_inc(turned.sem, 1)

        def ln_act(act, i, turn=True, gain=None, shift=None, scale=1.0):
            var = cnt("stats_var", i)
            act.wait_ge(var.sem, var.done(0))
            nc.scalar.activation(newton[:, :], deviation[:, :], ACT.Sqrt).then_inc(cnt("stats_sd").sem, 1)
            if not turn:
                return
            turned, taken = cnt("turned", TURNS[i]), cnt("xT_ready", TURNS[i])
            for t, b in ring(act, TILES):
                act.wait_ge(turned.sem, turned.done(t))
                if gain is None:
                    nc.scalar.activation(xT[:, :, ds(t * P, P)], bank[0:KD, b, 0:KT * P].rearrange("p (k n) -> p k n", k=KT),
                                         ACT.Copy, scale=scale).then_inc(taken.sem, 1)
                else:
                    for k in range(KT):
                        last = nc.scalar.activation(xT[:, k, ds(t * P, P)], bank[0:KD, b, k * P:(k + 1) * P],
                                                    ACT.Identity, scale=gain[:, k:k + 1],
                                                    bias=shift[:, k:k + 1] if shift is not None else 0.0)
                    last.then_inc(taken.sem, 1)

        def proj_pool(pool, i, z, rows, kt):
            staged, done = cnt("tile_staged", TILES * (i - (i > 1))), cnt("proj_sum", TILES * i)
            for t, b in ring(pool, TILES):
                pool.wait_ge(done.sem, done.freed(t))
                nc.gpsimd.tensor_copy(ztile[0:rows, b, 0:kt * P].rearrange("p (k n) -> p k n", k=kt),
                                      z[0:rows, 0:kt, ds(t * P, P)]).then_inc(staged.sem, 1)

        def proj_pe(pe, i, weight, rows, kt, bias=None):
            staged, done, added = cnt("tile_staged", TILES * (i - (i > 1))), cnt("proj_sum", TILES * i), cnt("proj_added", TILES * i)
            for t, b in ring(pe, TILES):
                pe.wait_ge(staged.sem, staged.done(t))
                pe.wait_ge(added.sem, added.freed(t))
                if bias is not None:
                    nc.tensor.matmul(bank[:, b, 0:DIM], ones_row, bias, start=True, stop=False)
                for k in range(kt):
                    last = nc.tensor.matmul(bank[:, b, 0:DIM], ztile[0:rows, b, k * P:(k + 1) * P], weight[:, k, :],
                                            start=(k == 0 and bias is None), stop=(k == kt - 1))
                last.then_inc(done.sem, 1)

        def turn_pe(pe, i):
            staged, done, added = cnt("tile_staged", TILES * (i - (i > 1))), cnt("proj_sum", TILES * i), cnt("proj_added", TILES * i)
            for t, b in ring(pe, TILES):
                pe.wait_ge(staged.sem, staged.done(t))
                pe.wait_ge(added.sem, added.freed(t))
                for k in range(KT):
                    last = nc.tensor.transpose(bank[:, b, k * KD:(k + 1) * KD], ztile[0:KD, b, k * P:(k + 1) * P],
                                               ident[0:KD, 0:KD])
                last.then_inc(done.sem, 1)

        def proj_dve(dve, i, acc):
            done, added = cnt("proj_sum", TILES * i), cnt("proj_added", TILES * i)
            for t, b in ring(dve, TILES):
                dve.wait_ge(done.sem, done.done(t))
                nc.vector.tensor_tensor(tile_h(acc, t), tile_h(acc, t), bank[:, b, 0:DIM], ALU.add).then_inc(added.sem, 1)

        ones_row = const("ones")[0:1, 0:P]
        ones = const("ones")

        early = Carve()
        w_emb = early(P, PATCH_K, DIM)
        select38 = early(SEQ, TOKENS)
        rows_a, rows_b, rows_sum = early(SEQ, DIM), early(SEQ, DIM), early(SEQ, DIM)
        patch_buf = [early(P, PATCH_K, P) for _ in range(2)]

        def patch_load(sp, t, b):
            summed = cnt("patch_sum")
            sp.wait_ge(summed.sem, summed.freed(t))
            sp.dma_start(patch_buf[b], t_in["patches"][ds(t, 1)].rearrange("a p k n -> (a p) k n")).then_inc(patch_loaded[b], 16)

        def patch_dve(dve, ch):
            ch.step(nc.vector.memset(rows_b[0:1, :], 0.0))
            ch.settle()
            dve.wait_ge(load_early, 16 * EARLY_LOADS)
            nc.vector.tensor_tensor(rows_sum, rows_a, rows_b, ALU.add).then_inc(cnt("rows_ready").sem, 1)
            summed, taken = cnt("patch_sum"), cnt("patch_taken")
            for t, b in ring(dve, TILES):
                dve.wait_ge(summed.sem, summed.done(t))
                nc.vector.tensor_copy(tile_h(h, t), bank[:, b, 0:DIM]).then_inc(taken.sem, 1)

        def patch_pe(pe):
            pe.wait_ge(load_early, 16 * EARLY_LOADS)
            pe.wait_ge(cnt("rows_ready").sem, cnt("rows_ready").done(0))
            summed, taken = cnt("patch_sum"), cnt("patch_taken")

            for t in range(TILES):
                b = t % 2
                pe.wait_ge(patch_loaded[b], 16 * (t // 2 + 1))
                pe.wait_ge(taken.sem, taken.freed(t))
                for k in range(PATCH_K):
                    nc.tensor.matmul(bank[:, b, 0:DIM], patch_buf[b][:, k, :], w_emb[:, k, :], start=(k == 0), stop=False)
                nc.tensor.matmul(bank[:, b, 0:DIM], select38[:, t * P:(t + 1) * P], rows_sum, start=False,
                                 stop=True).then_inc(summed.sem, 1)

        wte_buf = [zT[:, CI - 1, b * WTE_R * DIM:(b + 1) * WTE_R * DIM] for b in range(2)]
        wte_tail = zT[0:WTE_TAIL, CI - 1, 2 * WTE_R * DIM:(2 * WTE_R + 1) * DIM]

        def wte_load(sp, c, b):
            added = cnt("wte_added")
            view = t_in["wte"][0:WTE_ROWS - WTE_TAIL, :].rearrange("(c p r) e -> c p (r e)", p=P, r=WTE_R)
            sp.wait_ge(added.sem, added.freed(c))
            sp.dma_start(wte_buf[b], view[ds(c, 1)].rearrange("a p n -> (a p) n")).then_inc(wte_loaded[b], 16)

        def wte_pool(pool, ch):
            added = cnt("wte_added")
            ch.step(nc.gpsimd.memset(wte_sum[:, :], 0.0))
            ch.settle()
            with pool.Fori(0, WTE_CH // 2) as i:
                for b in range(2):
                    pool.wait_ge(wte_loaded[b], 16 * i + 16)
                    pool.wait_ge(added.sem, 2 * i + b + CREDITS)
                    nc.gpsimd.tensor_tensor(wte_sum[:, :], wte_sum[:, :], wte_buf[b], ALU.add).then_inc(added.sem, 1)
            if WTE_CH % 2:
                pool.wait_ge(wte_loaded[0], 16 * (WTE_CH // 2 + 1))
                pool.wait_ge(added.sem, WTE_CH - 1 + CREDITS)
                nc.gpsimd.tensor_tensor(wte_sum[:, :], wte_sum[:, :], wte_buf[0], ALU.add).then_inc(added.sem, 1)
            pool.wait_ge(added.sem, WTE_CH + CREDITS)
            pool.wait_ge(load_tail, 16)
            ch.step(nc.gpsimd.tensor_tensor(wte_sum[0:WTE_TAIL, 0:DIM], wte_sum[0:WTE_TAIL, 0:DIM], wte_tail, ALU.add))
            ch.settle()
            half = WTE_R // 2
            while half:
                ch.step(nc.gpsimd.tensor_tensor(wte_sum[:, 0:half * DIM], wte_sum[:, 0:half * DIM],
                                                wte_sum[:, half * DIM:2 * half * DIM], ALU.add))
                ch.settle()
                half //= 2

        def soft_shift(ch, psum, work, peak, mask=None):
            src = psum
            if mask is not None:
                ch.step(nc.vector.tensor_tensor(work, psum, mask.unsqueeze(1).broadcast_to(list(work.shape)), ALU.add))
                ch.settle()
                src = work
            ch.step(nc.vector.tensor_reduce(peak, src, AX_X, ALU.max))
            ch.settle()
            return nc.vector.tensor_tensor(work, src, peak.unsqueeze(2).broadcast_to(list(work.shape)), ALU.subtract)

        class Heads16:
            def __init__(self, i, name, rope):
                self.i, self.rope = i, rope
                c = Carve()
                self.q, self.k = c(KD, KT, GPAD), c(KD, KT, GPAD)
                self.rot = [c(KD, GT) for _ in range(2)]
                self.copies = c(KD, KT, GI, 3, SEQ)
                self.kbd = [c(KD, 2, KT, HPK, SEQ) for _ in range(2)]
                self.s = [c(P, HEADS, SEQ) for _ in range(2)]
                self.p = [c(P, HEADS, SEQ) for _ in range(2)]
                self.peak = [c(P, HEADS) for _ in range(2)]
                self.total = [c(P, HEADS) for _ in range(2)]
                self.inverse = [c(P, HEADS) for _ in range(2)]
                self.pt = [c(G3, 4, P) for _ in range(2)]
                self.vw = [c(G3, 2, 4, KD) for _ in range(2)]
                self.rotated = c(KD, KT, 2 * DIM) if rope else None
                self.rot_bias = c(KD, 2, KT)
                if rope:
                    self.w, self.bq, self.bk, self.rbq, self.rbk, self.bv = (const(n) for n in ("qkv1", "bq", "bk", "bq_turned", "bk_turned", "bv"))
                else:
                    self.w = const("qkvf")
                self.w = self.w.rearrange("p (k n) -> p k n", k=KT)
                self.per_group = 8 if rope else 4
                self.pj = PJ_BASE[name]
                self.g0, self.u0, self.o0 = BASES[name]

            def outputs(self):
                for dst, off in ((self.q, 0), (self.k, DIM)):
                    for m in range(KT):
                        yield dst, m, self.w[:, :, off + m * KD:off + (m + 1) * KD], False
                        if self.rope:
                            yield dst, m, self.rotated[:, :, off + m * KD:off + (m + 1) * KD], True

            def pool(self, pool, ch):
                for x in (self.q, self.k):
                    ch.step(nc.gpsimd.memset(x[:, :, GT:GPAD], 0.0))
                if self.rope:
                    for off in (0, DIM):
                        for m in range(KT):
                            src = self.w[:, m, off:off + DIM].rearrange("p (h two d) -> p h two d", two=2, d=HD // 2)
                            dst = self.rotated[:, m, off:off + DIM].rearrange("p (h two d) -> p h two d", two=2, d=HD // 2)
                            ch.step(nc.gpsimd.tensor_scalar(dst[:, :, 0, :], src[:, :, 1, :], -1.0, None, ALU.mult))
                            ch.step(nc.gpsimd.tensor_copy(dst[:, :, 1, :], src[:, :, 0, :]))
                    for n, bias in enumerate((self.rbq, self.rbk)):
                        ch.step(nc.gpsimd.tensor_scalar(self.rot_bias[:, n, :], bias, const("rot_sign"), None, ALU.mult))
                ch.settle()
                pool.sem_inc(cnt("prepared").sem, 1)
                qk, kbd, scored = cnt("qk_ready", self.g0 - GROUPS), cnt("kbd_ready", self.u0[1]), cnt("scores_ready", self.u0[0])
                exped, probs, turned = cnt("sum_taken", self.u0[0] - GROUPS * PAIRS), cnt("probs_ready", self.u0[0]), cnt("turned_probs", self.u0[0])
                hmask = const("hmask").unsqueeze(2).broadcast_to([KD, HPK, SEQ])

                def expand(u, p, b):
                    pool.wait_ge(scored.sem, scored.freed(u))
                    for img in range(2):
                        at = (2 * p + img) * SEQ
                        for m in range(KT):
                            last = nc.gpsimd.tensor_tensor(self.kbd[b][:, img, m], self.k[:, m, at:at + SEQ].unsqueeze(1).broadcast_to([KD, HPK, SEQ]), hmask, ALU.mult)
                    last.then_inc(kbd.sem, 1)

                def norm(u, b):
                    pool.wait_ge(exped.sem, exped.done(u))
                    pool.wait_ge(turned.sem, turned.freed(u))
                    nc.gpsimd.tensor_tensor(self.p[b], self.s[b], self.inverse[b].unsqueeze(2).broadcast_to([P, HEADS, SEQ]), ALU.mult).then_inc(probs.sem, 1)

                with pool.Fori(0, GROUPS) as g:
                    pool.wait_ge(qk.sem, qk.done(g))
                    u = g * PAIRS
                    expand(u, 0, 0)
                    expand(u + 1, 1, 1)
                    for p in range(PAIRS):
                        norm(u + p, p % 2)
                        if p + 2 < PAIRS:
                            expand(u + p + 2, p + 2, p % 2)

            def pe(self, pe):
                pe.wait_ge(cnt("prepared").sem, cnt("prepared", self.i).done(0))
                pj, pj_taken = cnt("pj_sum", self.pj), cnt("pj_taken", self.pj)
                kbd, scored, s_taken = cnt("kbd_ready", self.u0[1]), cnt("scores_ready", self.u0[0]), cnt("shifted", self.u0[0])
                copies, v_sum, v_in = cnt("tokens_copied", self.g0), cnt("v_sum", self.u0[1]), cnt("v_in", self.u0[1])
                probs, turned, p_in = cnt("probs_ready", self.u0[0]), cnt("turned_probs", self.u0[0]), cnt("probs_in", self.u0[0])
                o_sum, o_taken = cnt("o_sum", self.o0[0]), cnt("o_taken", self.o0[1])

                def scores(u, p, b):
                    pe.wait_ge(kbd.sem, kbd.done(u))
                    pe.wait_ge(s_taken.sem, s_taken.freed(u))
                    for img in range(2):
                        at = (2 * p + img) * SEQ
                        for m in range(KT):
                            last = nc.tensor.matmul(bank[img * SLOT:(img + 1) * SLOT, 2 + b, m * HPK * SEQ:(m + 1) * HPK * SEQ],
                                                    self.q[:, m, at:at + SLOT], self.kbd[b][:, img, m].rearrange("p h t -> p (h t)"),
                                                    start=True, stop=True)
                    last.then_inc(scored.sem, 1)

                def values(u, p):
                    pe.wait_ge(v_in.sem, v_in.done(u - 1))
                    for img in range(2):
                        for m in range(KT):
                            last = nc.tensor.matmul(bank[0:G3, 6, img * DIM:(img + 1) * DIM],
                                                    self.copies[:, m, 2 * p + img].rearrange("p c t -> p (c t)"),
                                                    self.w[:, m, 2 * DIM:3 * DIM], start=(m == 0), stop=(m == KT - 1))
                    last.then_inc(v_sum.sem, 1)

                def turn(u, b):
                    pe.wait_ge(probs.sem, probs.done(u))
                    pe.wait_ge(p_in.sem, p_in.freed(u))
                    flat = self.p[b].rearrange("p h t -> p (h t)")
                    for j in range(4):
                        last = nc.tensor.transpose(bank[0:G3, 4 + b, j * P:(j + 1) * P], flat[:, j * G3:(j + 1) * G3], ident)
                    last.then_inc(turned.sem, 1)

                def mix(u, b):
                    pe.wait_ge(p_in.sem, p_in.done(u))
                    pe.wait_ge(v_in.sem, v_in.done(u))
                    pe.wait_ge(o_taken.sem, o_taken.done(u - 1))
                    for m in range(KT):
                        for img in range(2):
                            for j in range(2):
                                last = nc.tensor.matmul(bank[0:KD, 7, (2 * m + img) * SEQ:(2 * m + img + 1) * SEQ],
                                                        self.vw[b][:, img, 2 * m + j, :],
                                                        self.pt[b][:, 2 * m + j, img * SLOT:img * SLOT + SEQ],
                                                        start=(j == 0), stop=(j == 1))
                    last.then_inc(o_sum.sem, 1)

                with pe.Fori(0, GROUPS) as g:
                    for n, (_, m, w, _) in enumerate(self.outputs()):
                        pe.wait_ge(pj_taken.sem, pj_taken.freed(g * self.per_group + n))
                        for kk in range(KT):
                            last = nc.tensor.matmul(bank[0:KD, n % 2, 0:GT], w[:, kk, :], xT[:, kk, ds(g * GT, GT)],
                                                    start=(kk == 0), stop=(kk == KT - 1))
                        last.then_inc(pj.sem, 1)
                    u = g * PAIRS
                    scores(u, 0, 0)
                    pe.wait_ge(copies.sem, copies.done(g))
                    values(u, 0)
                    for p in range(PAIRS):
                        if p + 1 < PAIRS:
                            scores(u + p + 1, p + 1, (p + 1) % 2)
                        turn(u + p, p % 2)
                        if p + 1 < PAIRS:
                            values(u + p + 1, p + 1)
                        mix(u + p, p % 2)

            def dve(self, dve, ch):
                pj, pj_taken = cnt("pj_sum", self.pj), cnt("pj_taken", self.pj)
                qk = cnt("qk_ready", self.g0 - GROUPS)
                scored, shifted = cnt("scores_ready", self.u0[0]), cnt("shifted", self.u0[0])
                exped, summed, probs = cnt("exped", self.u0[0]), cnt("sum_taken", self.u0[0] - GROUPS * PAIRS), cnt("probs_ready", self.u0[0])
                v_sum, v_in, o_sum = cnt("v_sum", self.u0[1]), cnt("v_in", self.u0[1]), cnt("o_sum", self.o0[0])
                cos, sin = (const(n).unsqueeze(1).broadcast_to([KD, GI, SEQ]) for n in ("cos", "sin"))
                mask = const("causal") if self.rope else None
                images = lambda x: x.rearrange("p (i t) -> p i t", t=SEQ)
                dve.wait_ge(cnt("prepared").sem, cnt("prepared", self.i).done(0))

                def part1(u, b):
                    dve.wait_ge(scored.sem, scored.done(u))
                    dve.wait_ge(probs.sem, probs.freed(u))
                    psum = bank[:, 2 + b, 0:HEADS * SEQ].rearrange("p (h t) -> p h t", t=SEQ)
                    soft_shift(ch, psum, self.s[b], self.peak[b], mask).then_inc(shifted.sem, 1)

                def value(u, b):
                    dve.wait_ge(v_sum.sem, v_sum.done(u))
                    dve.wait_ge(o_sum.sem, o_sum.freed(u))
                    for img in range(2):
                        psum = bank[0:G3, 6, img * DIM:(img + 1) * DIM].rearrange("p (m n) -> p m n", m=KT).unsqueeze(2).broadcast_to([G3, KT, 2, KD])
                        msk = const("vmask").rearrange("p (j n) -> p j n", j=2).unsqueeze(1).broadcast_to([G3, KT, 2, KD])
                        out_ = self.vw[b][:, img].rearrange("p (m j) n -> p m j n", j=2)
                        last = nc.vector.tensor_tensor(out_, psum, msk, ALU.mult)
                    last.then_inc(v_in.sem, 1)

                def part2(u, b):
                    dve.wait_ge(exped.sem, exped.done(u))
                    ch.step(nc.vector.tensor_reduce(self.total[b], self.s[b], AX_X, ALU.add))
                    ch.settle()
                    nc.vector.reciprocal(self.inverse[b], self.total[b]).then_inc(summed.sem, 1)

                with ch.loop(GROUPS, 4 + 3 * PAIRS if self.rope else 2 * PAIRS) as g:
                    for n, (dst, m, _, rotated) in enumerate(self.outputs()):
                        v = g * self.per_group + n
                        dve.wait_ge(pj.sem, pj.done(v))
                        psum = bank[0:KD, n % 2, 0:GT]
                        if not self.rope:
                            nc.vector.tensor_copy(dst[:, m, 0:GT], psum).then_inc(pj_taken.sem, 1)
                            continue
                        bias = {(0, False): self.bq, (0, True): self.rot_bias[:, 0], (1, False): self.bk, (1, True): self.rot_bias[:, 1]}[(0 if dst is self.q else 1, rotated)]
                        if n >= 2:
                            ch.settle()
                        nc.vector.scalar_tensor_tensor(images(self.rot[int(rotated)]), images(psum), bias[:, m:m + 1],
                                                       sin if rotated else cos, ALU.add, ALU.mult).then_inc(pj_taken.sem, 1)
                        if rotated:
                            dve.wait_ge(pj_taken.sem, pj_taken.done(v))
                            ch.step(nc.vector.tensor_tensor(dst[:, m, 0:GT], self.rot[0], self.rot[1], ALU.add))
                    dve.wait_ge(pj_taken.sem, pj_taken.done(g * self.per_group + self.per_group - 1))
                    ch.settle()
                    dve.sem_inc(qk.sem, 1)
                    u = g * PAIRS
                    part1(u, 0)
                    for p in range(PAIRS):
                        if p + 1 < PAIRS:
                            dve.wait_ge(shifted.sem, shifted.done(u + p))
                            part1(u + p + 1, (p + 1) % 2)
                        value(u + p, p % 2)
                        part2(u + p, p % 2)

            def act(self, act):
                copies, v_sum = cnt("tokens_copied", self.g0), cnt("v_sum", self.u0[1])
                shifted, exped = cnt("shifted", self.u0[0]), cnt("exped", self.u0[0])
                turned, p_in, o_sum, o_taken = cnt("turned_probs", self.u0[0]), cnt("probs_in", self.u0[0]), cnt("o_sum", self.o0[0]), cnt("o_taken", self.o0[1])

                def exp(u, b):
                    act.wait_ge(shifted.sem, shifted.done(u))
                    nc.scalar.activation(self.s[b], self.s[b], ACT.Exp, scale=HD ** -0.5).then_inc(exped.sem, 1)

                with act.Fori(0, GROUPS) as g:
                    u = g * PAIRS
                    act.wait_ge(v_sum.sem, v_sum.done(u - 1))
                    for m in range(KT):
                        last = nc.scalar.activation(self.copies[:, m], xT[:, m, ds(g * GT, GT)].rearrange("p (i t) -> p i t", t=SEQ).unsqueeze(2).broadcast_to([KD, GI, 3, SEQ]), ACT.Copy)
                    last.then_inc(copies.sem, 1)
                    exp(u, 0)
                    for p in range(PAIRS):
                        b = p % 2
                        if p + 1 < PAIRS:
                            exp(u + p + 1, (p + 1) % 2)
                        act.wait_ge(turned.sem, turned.done(u + p))
                        act.wait_ge(o_sum.sem, o_sum.freed(u + p))
                        nc.scalar.activation(self.pt[b].rearrange("p j n -> p (j n)"), bank[0:G3, 4 + b, :], ACT.Copy).then_inc(p_in.sem, 1)
                        act.wait_ge(o_sum.sem, o_sum.done(u + p))
                        for m in range(KT):
                            last = nc.scalar.activation(zT[0:KD, m, ds(g * GT + 2 * p * SEQ, 2 * SEQ)],
                                                        bank[0:KD, 7, 2 * m * SEQ:2 * (m + 1) * SEQ], ACT.Identity,
                                                        bias=self.bv[:, m:m + 1] if self.rope else 0.0)
                        last.then_inc(o_taken.sem, 1)

        class Tokens12:
            def __init__(self):
                c = Carve()
                self.wo = c(KD, KT * HEADS, DIM)
                self.a = c(KD, KT, GPAD)
                self.w2 = c(KD, KT, HEADS)
                self.kx = [c(KD, 2, KT, HEADS, SEQ) for _ in range(2)]
                self.s = [c(P, HEADS, SEQ) for _ in range(2)]
                self.p = [c(P, HEADS, SEQ) for _ in range(2)]
                self.peak, self.total, self.inverse = ([c(P, HEADS) for _ in range(2)] for _ in range(3))
                self.pt = [c(SEQ, 2, HEADS, SEQ) for _ in range(2)]
                self.v = [c(SEQ, 2, DIM) for _ in range(2)]
                self.att = [c(KD, KT, HEADS, 4 * SEQ) for _ in range(2)]
                self.offset = c(KD, KT)

            def pe(self, pe):
                kx, scored, shifted = cnt("kbd_ready"), cnt("scores_ready"), cnt("shifted")
                copied, v_sum, v_in = cnt("tokens_copied"), cnt("v_sum"), cnt("v_in")
                probs, turned, p_in = cnt("probs_ready"), cnt("turned_probs"), cnt("probs_in")
                o_sum, o_taken, wo_sum, wo_taken = cnt("o_sum"), cnt("o_taken"), cnt("wo_sum"), cnt("wo_taken")

                def scores(u, p, b):
                    pe.wait_ge(kx.sem, kx.done(u))
                    pe.wait_ge(shifted.sem, shifted.done(u - 1))
                    for img in range(2):
                        at = (2 * p + img) * SEQ
                        for m in range(KT):
                            last = nc.tensor.matmul(bank[img * SLOT:(img + 1) * SLOT, 0, 0:HEADS * SEQ], self.a[:, m, at:at + SLOT],
                                                    self.kx[b][:, img, m].rearrange("p h t -> p (h t)"),
                                                    start=(m == 0), stop=(m == KT - 1))
                    last.then_inc(scored.sem, 1)

                def values(u, p):
                    wait_apart(pe, v_in.sem, v_in.done(u - 1))
                    for img in range(2):
                        at = (2 * p + img) * SEQ
                        for m in range(KT):
                            last = nc.tensor.transpose(bank[0:SEQ, 4, img * DIM + m * KD:img * DIM + (m + 1) * KD],
                                                       self.a[:, m, at:at + SEQ], ident[0:KD, 0:KD])
                    last.then_inc(v_sum.sem, 1)

                def turn(u, b):
                    pe.wait_ge(p_in.sem, p_in.done(u - 1))
                    wait_apart(pe, probs.sem, probs.done(u))
                    for hh in range(HEADS):
                        last = nc.tensor.transpose(bank[0:SEQ, 1 + hh // 4, hh % 4 * P:(hh % 4 + 1) * P], self.p[b][:, hh, :], ident)
                    last.then_inc(turned.sem, 1)

                def mix(u, b):
                    pe.wait_ge(p_in.sem, p_in.done(u))
                    pe.wait_ge(v_in.sem, v_in.done(u))
                    for n in range(4):
                        img, m = divmod(n, 2)
                        pe.wait_ge(o_taken.sem, o_taken.freed(4 * u + n))
                        nc.tensor.matmul(bank[0:KD, 5 + n % 2, 0:HEADS * SEQ], self.v[b][:, img, m * KD:(m + 1) * KD],
                                         self.pt[b][:, img].rearrange("p h t -> p (h t)"), start=True, stop=True).then_inc(o_sum.sem, 1)

                def project(g, quad):
                    q = 2 * g + quad
                    pe.wait_ge(o_taken.sem, o_taken.done(4 * PAIRS * g + 8 * quad + 7))
                    pe.wait_ge(wo_taken.sem, wo_taken.done(q - 1))
                    for mt in range(KT):
                        for n in range(KT * HEADS):
                            last = nc.tensor.matmul(bank[0:KD, 7, mt * 4 * SEQ:(mt + 1) * 4 * SEQ], self.wo[:, n, mt * KD:(mt + 1) * KD],
                                                    self.att[quad][:, n // HEADS, n % HEADS, :], start=(n == 0), stop=(n == KT * HEADS - 1))
                    last.then_inc(wo_sum.sem, 1)

                pe.wait_ge(load_wo, 16)
                with pe.Fori(0, GROUPS) as g:
                    u = g * PAIRS
                    pe.wait_ge(copied.sem, copied.done(g))
                    scores(u, 0, 0)
                    values(u, 0)
                    for p in range(PAIRS):
                        if p + 1 < PAIRS:
                            scores(u + p + 1, p + 1, (p + 1) % 2)
                        turn(u + p, p % 2)
                        if p + 1 < PAIRS:
                            values(u + p + 1, p + 1)
                        mix(u + p, p % 2)
                        if p % 2:
                            project(g, p // 2)

            def dve(self, dve, ch):
                kx, scored, shifted, exped = cnt("kbd_ready"), cnt("scores_ready"), cnt("shifted"), cnt("exped")
                copied, probs, turned = cnt("tokens_copied"), cnt("probs_ready"), cnt("turned_probs")
                o_sum, o_taken, wo_sum = cnt("o_sum"), cnt("o_taken"), cnt("wo_sum")
                wqk = const("wqk").rearrange("p (k h) -> p k h", k=KT)
                ch.step(nc.vector.tensor_tensor(self.w2, wqk, wqk, ALU.mult))
                ch.settle()

                def expand(u, p, b):
                    dve.wait_ge(scored.sem, scored.freed(u))
                    for img in range(2):
                        at = (2 * p + img) * SEQ
                        shape = [KD, KT, HEADS, SEQ]
                        last = nc.vector.tensor_tensor(self.kx[b][:, img], self.a[:, :, at:at + SEQ].unsqueeze(2).broadcast_to(shape),
                                                       self.w2.unsqueeze(3).broadcast_to(shape), ALU.mult)
                    last.then_inc(kx.sem, 1)

                def part1(u, b):
                    dve.wait_ge(scored.sem, scored.done(u))
                    dve.wait_ge(probs.sem, probs.freed(u))
                    soft_shift(ch, bank[:, 0, 0:HEADS * SEQ].rearrange("p (h t) -> p h t", t=SEQ), self.s[b], self.peak[b],
                               const("causal")).then_inc(shifted.sem, 1)

                def part2(u, b):
                    dve.wait_ge(exped.sem, exped.done(u))
                    ch.step(nc.vector.tensor_reduce(self.total[b], self.s[b], AX_X, ALU.add))
                    ch.settle()
                    ch.step(nc.vector.reciprocal(self.inverse[b], self.total[b]))
                    ch.settle()
                    dve.wait_ge(turned.sem, turned.freed(u))
                    nc.vector.tensor_tensor(self.p[b], self.s[b], self.inverse[b].unsqueeze(2).broadcast_to([P, HEADS, SEQ]),
                                            ALU.mult).then_inc(probs.sem, 1)

                def take(u, p, g):
                    nreg = const("nreg").unsqueeze(1).broadcast_to([KD, HEADS, SEQ])
                    if p % 2 == 0:
                        dve.wait_ge(wo_sum.sem, wo_sum.freed(2 * g + p // 2))
                    for n in range(4):
                        img, m = divmod(n, 2)
                        at = (2 * (p % 2) + img) * SEQ
                        dve.wait_ge(o_sum.sem, o_sum.done(4 * u + n))
                        nc.vector.tensor_tensor(self.att[p // 2][:, m, :, at:at + SEQ],
                                                bank[0:KD, 5 + n % 2, 0:HEADS * SEQ].rearrange("p (h t) -> p h t", t=SEQ),
                                                nreg, ALU.mult).then_inc(o_taken.sem, 1)

                with ch.loop(GROUPS, 4 * PAIRS) as g:
                    u = g * PAIRS
                    dve.wait_ge(copied.sem, copied.done(g))
                    expand(u, 0, 0)
                    expand(u + 1, 1, 1)
                    part1(u, 0)
                    for p in range(PAIRS):
                        if p + 1 < PAIRS:
                            dve.wait_ge(shifted.sem, shifted.done(u + p))
                            part1(u + p + 1, (p + 1) % 2)
                        part2(u + p, p % 2)
                        if p + 2 < PAIRS:
                            expand(u + p + 2, p + 2, p % 2)
                        take(u + p, p, g)

            def act(self, act, ch):
                copied, v_sum, v_in, scored = cnt("tokens_copied"), cnt("v_sum"), cnt("v_in"), cnt("scores_ready")
                shifted, exped, turned, p_in = cnt("shifted"), cnt("exped"), cnt("turned_probs"), cnt("probs_in")
                wo_sum, wo_taken, o_sum = cnt("wo_sum"), cnt("wo_taken"), cnt("o_sum")
                ch.step(nc.scalar.activation(self.a[:, :, GT:GPAD], xT[:, :, 0:GPAD - GT], ACT.Copy))
                ch.settle()

                def exp(u, b):
                    act.wait_ge(shifted.sem, shifted.done(u))
                    nc.scalar.activation(self.s[b], self.s[b], ACT.Exp, scale=float(DIM) ** -0.5).then_inc(exped.sem, 1)

                with act.Fori(0, GROUPS) as g:
                    u = g * PAIRS
                    act.wait_ge(v_sum.sem, v_sum.done(u - 1))
                    act.wait_ge(scored.sem, scored.done(u - 1))
                    nc.scalar.activation(self.a[:, :, 0:GT], xT[:, :, ds(g * GT, GT)], ACT.Copy).then_inc(copied.sem, 1)
                    exp(u, 0)
                    act.wait_ge(v_sum.sem, v_sum.done(u))
                    act.wait_ge(o_sum.sem, o_sum.done(4 * u - 1))
                    nc.scalar.activation(self.v[0], bank[0:SEQ, 4, 0:2 * DIM].rearrange("p (i n) -> p i n", i=2), ACT.Copy).then_inc(v_in.sem, 1)
                    for p in range(PAIRS):
                        b = p % 2
                        if p + 1 < PAIRS:
                            exp(u + p + 1, (p + 1) % 2)
                        act.wait_ge(turned.sem, turned.done(u + p))
                        if p:
                            act.wait_ge(o_sum.sem, o_sum.done(4 * (u + p) - 1))
                        for img in range(2):
                            last = nc.scalar.activation(self.pt[b][:, img], bank[0:SEQ, 1:4, :].rearrange("p k (h n) -> p (k h) n", n=P)[:, :, img * SLOT:img * SLOT + SEQ], ACT.Copy)
                        last.then_inc(p_in.sem, 1)
                        if p + 1 < PAIRS:
                            act.wait_ge(v_sum.sem, v_sum.done(u + p + 1))
                            nc.scalar.activation(self.v[1 - b], bank[0:SEQ, 4, 0:2 * DIM].rearrange("p (i n) -> p i n", i=2), ACT.Copy).then_inc(v_in.sem, 1)
                        if p % 2:
                            q = 2 * g + p // 2
                            act.wait_ge(wo_sum.sem, wo_sum.done(q))
                            nc.scalar.activation(zT[0:KD, 0:KT, ds(g * GT + (p - 1) * 2 * SEQ, 4 * SEQ)],
                                                 bank[0:KD, 7, 0:KT * 4 * SEQ].rearrange("p (m n) -> p m n", m=KT), ACT.Copy).then_inc(wo_taken.sem, 1)

            def offset_pe(self, pe):
                for m in range(KT):
                    last = nc.tensor.matmul(bank[0:KD, 0, m:m + 1], wte_sum[:, m * KD:(m + 1) * KD], ones[:, 0:1], start=True, stop=True)
                last.then_inc(cnt("mean_sum").sem, 1)
                pe.wait_ge(cnt("mean_in").sem, cnt("mean_in").done(0))
                for mt in range(KT):
                    for n in range(KT * HEADS):
                        last = nc.tensor.matmul(bank[0:KD, 1, mt:mt + 1], self.wo[:, n, mt * KD:(mt + 1) * KD],
                                                avg_wte[:, n // HEADS:n // HEADS + 1], start=(n == 0), stop=(n == KT * HEADS - 1))
                last.then_inc(cnt("offset_sum").sem, 1)

            def offset_act(self, act):
                act.wait_ge(cnt("mean_sum").sem, cnt("mean_sum").done(0))
                nc.scalar.activation(avg_wte[:, :], bank[0:KD, 0, 0:KT], ACT.Copy, scale=1.0 / WTE_ROWS).then_inc(cnt("mean_in").sem, 1)

            def offset_dve(self, dve, ch):
                dve.wait_ge(cnt("offset_sum").sem, cnt("offset_sum").done(0))
                ch.step(nc.vector.tensor_scalar(self.offset, bank[0:KD, 1, 0:KT], -1.0, None, ALU.mult))
                ch.settle()
                for m in range(KT):
                    z = zT[0:KD, m, :].rearrange("p (i t) -> p i t", t=SEQ)
                    ch.step(nc.vector.scalar_tensor_tensor(z, const("nreg").unsqueeze(1).broadcast_to([KD, IMAGES, SEQ]),
                                                           self.offset[:, m:m + 1], z, ALU.mult, ALU.add))

        class Parts8:
            def __init__(self):
                c = Carve()
                self.qk = c(KF, 5, GPAD)
                self.copies = c(KD, KT, GI, 3, SEQ)
                self.kbd = [c(KF, 2, 3, NH3, SEQ) for _ in range(2)]
                self.s = [c(P, 2, NH3, SEQ) for _ in range(2)]
                self.p = [c(P, 2, NH3 + 1, SEQ) for _ in range(2)]
                self.peak2, self.total2 = ([c(P, 2, NH3) for _ in range(2)] for _ in range(2))
                self.peak, self.total, self.inverse = ([c(P, NH3) for _ in range(2)] for _ in range(3))
                self.pt = [c(G3, 2, 3, P) for _ in range(2)]
                self.vw = [c(G3, 2, 3, 3, KF) for _ in range(2)]
                self.w = const("qkv3").rearrange("p (k n) -> p k n", k=KT)
                (self.g0, (self.w0, self.u0), self.o0), self.pj = BASES["L3"], PJ_BASE["L3"]

            def pool(self, pool, ch):
                ch.step(nc.gpsimd.memset(self.qk[:, :, GT:GPAD], 0.0))
                for b in range(2):
                    ch.step(nc.gpsimd.memset(self.p[b][:, :, NH3, :], 0.0))
                ch.settle()
                pool.sem_inc(cnt("prepared").sem, 1)
                qk, kbd, scored = cnt("qk_ready", self.g0 - GROUPS), cnt("kbd_ready", self.u0), cnt("scores_ready", self.w0)
                probs, turned = (cnt(n, self.w0) for n in ("probs_ready", "turned_probs"))
                summed = cnt("sum_taken", self.w0 - GROUPS * PAIRS)

                def expand(u, p, b):
                    pool.wait_ge(scored.sem, scored.done(3 * u - 4))
                    for img in range(2):
                        at = (2 * p + img) * SEQ
                        shape = [KF, 3, NH3, SEQ]
                        last = nc.gpsimd.tensor_tensor(self.kbd[b][:, img], self.qk[:, 2:5, at:at + SEQ].unsqueeze(2).broadcast_to(shape),
                                                       const("hmask8").unsqueeze(1).unsqueeze(3).broadcast_to(shape), ALU.mult)
                    last.then_inc(kbd.sem, 1)

                with pool.Fori(0, GROUPS) as g:
                    pool.wait_ge(qk.sem, qk.done(g))
                    u = g * PAIRS
                    expand(u, 0, 0)
                    for p in range(PAIRS):
                        if p + 1 < PAIRS:
                            expand(u + p + 1, p + 1, (p + 1) % 2)
                        for j in range(3):
                            w, b = 3 * (u + p) + j, (3 * p + j) % 2
                            pool.wait_ge(summed.sem, summed.done(w))
                            pool.wait_ge(turned.sem, turned.freed(w))
                            shape = [P, 2, NH3, SEQ]
                            nc.gpsimd.tensor_tensor(self.p[b][:, :, 0:NH3, :], self.s[b],
                                                    self.inverse[b].unsqueeze(1).unsqueeze(3).broadcast_to(shape), ALU.mult).then_inc(probs.sem, 1)

            def pe(self, pe):
                pe.wait_ge(cnt("prepared").sem, cnt("prepared", 2).done(0))
                pj, pj_taken = cnt("pj_sum", self.pj), cnt("pj_taken", self.pj)
                kbd, v_sum, v_in = (cnt(n, self.u0) for n in ("kbd_ready", "v_sum", "v_in"))
                copied = cnt("tokens_copied", self.g0)
                scored, shifted, probs, turned, p_in = (cnt(n, self.w0) for n in ("scores_ready", "shifted", "probs_ready", "turned_probs", "probs_in"))
                o_taken, mixed = cnt("o_taken", self.o0[1]), cnt("mixed", EXTRA["mixed"])

                def scores(u, n):
                    p, j = divmod(n, 3)
                    b, w = n % 2, 3 * u + n
                    pe.wait_ge(kbd.sem, kbd.done(u + p))
                    wait_apart(pe, shifted.sem, shifted.freed(w))
                    for img in range(2):
                        at = (2 * p + img) * SEQ
                        for half, part in enumerate(HALVES[j]):
                            last = nc.tensor.matmul(bank[img * SLOT:(img + 1) * SLOT, 2 * b + half, 0:NH3 * SEQ], self.qk[:, QUERY[j], at:at + SLOT],
                                                    self.kbd[p % 2][:, img, part].rearrange("p h t -> p (h t)"), start=True, stop=True)
                    last.then_inc(scored.sem, 1)

                def values(u, p):
                    pe.wait_ge(v_in.sem, v_in.done(u - 1))
                    for img in range(2):
                        for m in range(KT):
                            last = nc.tensor.matmul(bank[0:G3, 6, img * DIM:(img + 1) * DIM],
                                                    self.copies[:, m, 2 * p + img].rearrange("p c t -> p (c t)"),
                                                    self.w[:, m, 5 * KF:8 * KF], start=(m == 0), stop=(m == KT - 1))
                    last.then_inc(v_sum.sem, 1)

                def turn(w, b):
                    pe.wait_ge(probs.sem, probs.done(w))
                    pe.wait_ge(p_in.sem, p_in.done(w - 1))
                    for half in range(2):
                        flat = self.p[b][:, half].rearrange("p h t -> p (h t)")
                        for gr in range(3):
                            last = nc.tensor.transpose(bank[0:G3, 4 + half, gr * P:(gr + 1) * P], flat[:, gr * G3:(gr + 1) * G3], ident)
                    last.then_inc(turned.sem, 1)

                def mix(u, p, j, w, b):
                    pe.wait_ge(p_in.sem, p_in.done(w))
                    if j == 0:
                        pe.wait_ge(v_in.sem, v_in.done(u))
                        pe.wait_ge(o_taken.sem, o_taken.done(u - 1))
                    for img in range(2):
                        for half, part in enumerate(HALVES[j]):
                            for gr in range(3):
                                last = nc.tensor.matmul(bank[0:KF, 7, (2 * j + img) * SEQ:(2 * j + img + 1) * SEQ], self.vw[p % 2][:, img, part, gr, :],
                                                        self.pt[b][:, half, gr, img * SLOT:img * SLOT + SEQ],
                                                        start=(half == 0 and gr == 0), stop=(half == 1 and gr == 2))
                    last.then_inc(mixed.sem, 1)

                with pe.Fori(0, GROUPS) as g:
                    wait_apart(pe, shifted.sem, shifted.done(3 * PAIRS * g - 1))
                    for n in range(5):
                        if n == 4:
                            wait_apart(pe, pj_taken.sem, pj_taken.done(5 * g))
                        for kk in range(KT):
                            last = nc.tensor.matmul(bank[0:KF, n % 4, 0:GT], self.w[:, kk, n * KF:(n + 1) * KF], xT[:, kk, ds(g * GT, GT)],
                                                    start=(kk == 0), stop=(kk == KT - 1))
                        last.then_inc(pj.sem, 1)
                    u = g * PAIRS
                    scores(u, 0)
                    pe.wait_ge(copied.sem, copied.done(g))
                    values(u, 0)
                    for n in range(3 * PAIRS):
                        p, j = divmod(n, 3)
                        if n + 1 < 3 * PAIRS:
                            scores(u, n + 1)
                        turn(3 * u + n, n % 2)
                        mix(u + p, p, j, 3 * u + n, n % 2)
                        if j == 0 and p + 1 < PAIRS:
                            values(u + p + 1, p + 1)

            def dve(self, dve, ch):
                dve.wait_ge(cnt("prepared").sem, cnt("prepared", 2).done(0))
                pj, pj_taken, qk = cnt("pj_sum", self.pj), cnt("pj_taken", self.pj), cnt("qk_ready", self.g0 - GROUPS)
                scored, shifted, exped, probs, p_in = (cnt(n, self.w0) for n in ("scores_ready", "shifted", "exped", "probs_ready", "probs_in"))
                summed = cnt("sum_taken", self.w0 - GROUPS * PAIRS)
                v_sum, v_in, mixed = cnt("v_sum", self.u0), cnt("v_in", self.u0), cnt("mixed", EXTRA["mixed"])

                def part1(w, b):
                    dve.wait_ge(scored.sem, scored.done(w))
                    dve.wait_ge(probs.sem, probs.freed(w))
                    psum = bank[:, 2 * b:2 * b + 2, 0:NH3 * SEQ].rearrange("p k (h t) -> p k h t", t=SEQ)
                    ch.step(nc.vector.tensor_reduce(self.peak2[b], psum, AX_X, ALU.max))
                    ch.settle()
                    ch.step(nc.vector.tensor_tensor(self.peak[b], self.peak2[b][:, 0], self.peak2[b][:, 1], ALU.max))
                    ch.settle()
                    nc.vector.tensor_tensor(self.s[b], psum, self.peak[b].unsqueeze(1).unsqueeze(3).broadcast_to([P, 2, NH3, SEQ]),
                                            ALU.subtract).then_inc(shifted.sem, 1)

                def part2(w, b):
                    dve.wait_ge(exped.sem, exped.done(w))
                    ch.step(nc.vector.tensor_reduce(self.total2[b], self.s[b], AX_X, ALU.add))
                    ch.settle()
                    ch.step(nc.vector.tensor_tensor(self.total[b], self.total2[b][:, 0], self.total2[b][:, 1], ALU.add))
                    ch.settle()
                    nc.vector.reciprocal(self.inverse[b], self.total[b]).then_inc(summed.sem, 1)

                def value(u, b):
                    dve.wait_ge(v_sum.sem, v_sum.done(u))
                    dve.wait_ge(mixed.sem, mixed.done(3 * u - 4))
                    for img in range(2):
                        shape = [G3, 3, 3, KF]
                        last = nc.vector.tensor_tensor(self.vw[b][:, img],
                                                       bank[0:G3, 6, img * DIM:(img + 1) * DIM].rearrange("p (v n) -> p v n", v=3).unsqueeze(2).broadcast_to(shape),
                                                       const("vmask8").rearrange("p (g n) -> p g n", g=3).unsqueeze(1).broadcast_to(shape), ALU.mult)
                    last.then_inc(v_in.sem, 1)

                with ch.loop(GROUPS, 4 * 3 * PAIRS) as g:
                    for n in range(5):
                        dve.wait_ge(pj.sem, pj.done(5 * g + n))
                        nc.vector.tensor_copy(self.qk[:, n, 0:GT], bank[0:KF, n % 4, 0:GT]).then_inc(pj_taken.sem, 1)
                    dve.wait_ge(pj_taken.sem, pj_taken.done(5 * g + 4))
                    dve.sem_inc(qk.sem, 1)
                    u = g * PAIRS
                    part1(3 * u, 0)
                    value(u, 0)
                    for n in range(3 * PAIRS):
                        p, j = divmod(n, 3)
                        if n + 1 < 3 * PAIRS:
                            dve.wait_ge(shifted.sem, shifted.done(3 * u + n))
                            part1(3 * u + n + 1, (n + 1) % 2)
                        part2(3 * u + n, n % 2)
                        if j == 1 and p + 1 < PAIRS:
                            value(u + p + 1, (p + 1) % 2)

            def act(self, act):
                copied, v_sum = cnt("tokens_copied", self.g0), cnt("v_sum", self.u0)
                shifted, exped, turned, p_in = (cnt(n, self.w0) for n in ("shifted", "exped", "turned_probs", "probs_in"))
                o_taken, mixed = cnt("o_taken", self.o0[1]), cnt("mixed", EXTRA["mixed"])

                def exp(w, b):
                    act.wait_ge(shifted.sem, shifted.done(w))
                    nc.scalar.activation(self.s[b], self.s[b], ACT.Exp, scale=float(3 * HD3) ** -0.5).then_inc(exped.sem, 1)

                with act.Fori(0, GROUPS) as g:
                    u = g * PAIRS
                    act.wait_ge(v_sum.sem, v_sum.done(u - 1))
                    for m in range(KT):
                        last = nc.scalar.activation(self.copies[:, m], xT[:, m, ds(g * GT, GT)].rearrange("p (i t) -> p i t", t=SEQ).unsqueeze(2).broadcast_to([KD, GI, 3, SEQ]), ACT.Copy)
                    last.then_inc(copied.sem, 1)
                    exp(3 * u, 0)
                    for n in range(3 * PAIRS):
                        p, j = divmod(n, 3)
                        w, b = 3 * u + n, n % 2
                        if n + 1 < 3 * PAIRS:
                            exp(w + 1, 1 - b)
                        act.wait_ge(turned.sem, turned.done(w))
                        act.wait_ge(mixed.sem, mixed.freed(w))
                        nc.scalar.activation(self.pt[b], bank[0:G3, 4:6, 0:3 * P].rearrange("p k (g n) -> p k g n", n=P), ACT.Copy).then_inc(p_in.sem, 1)
                        if j == 2:
                            act.wait_ge(mixed.sem, mixed.done(w))
                            nc.scalar.activation(zT[0:KF, :, ds(g * GT + 2 * p * SEQ, 2 * SEQ)], bank[0:KF, 7, 0:6 * SEQ].rearrange("p (j n) -> p j n", j=3),
                                                 ACT.Copy).then_inc(o_taken.sem, 1)

        class Experts:

            def __init__(self, r, acc):
                self.r, self.acc = r, acc
                name = ("1", "2", "3f")[r]
                c = Carve()
                self.w1 = [c(KD, KT, HIDDEN) for _ in range(2)]
                self.w2 = [c(P, FT, DIM) for _ in range(2)]
                self.hid = [c(P, FT, 512) for _ in range(2)]
                self.logitsT = c(EXPERTS, TOKENS)
                small = lambda: c(P, TILES, EXPERTS)
                self.lg, self.eq, self.oh1, self.oh2, self.lg2 = (small() for _ in range(5))
                self.m1, self.m2, self.first, self.ex, self.g1, self.g2 = (c(P, TILES) for _ in range(6))
                self.router = const("router" + name).rearrange("p (k e) -> p k e", k=KT)
                self.router_bias = const("gate_b") if r == 2 else None
                self.b1 = const("b1_" + name) if r != 1 else None
                self.b2 = const("b2_" + name) if r != 1 else None
                self.w1_dram, self.w2_dram = t_in["w1_" + name], t_in["w2_" + name]
                self.chosen = zT[0:EXPERTS, 0:2, :]
                self.running = arena[0:EXPERTS, self.hid_at():self.hid_at() + 2 * TOKENS].rearrange("p (k n) -> p k n", k=2)
                self.func = ACT.Relu if r == 1 else ACT.Gelu

            def hid_at(self):
                return 2 * KT * HIDDEN + 2 * FT * DIM

            def load(self, sp, e, b):
                sp.dma_start(self.w1[b], self.w1_dram[ds(e, 1)].rearrange("a p k n -> (a p) k n")).then_inc(expert_loaded[b], 16)
                sp.dma_start(self.w2[b], self.w2_dram[ds(e, 1)].rearrange("a p f n -> (a p) f n")).then_inc(expert_loaded[b], 16)

            def sp_first(self, sp):
                for b in range(2):
                    self.load(sp, b, b)

            def sp_rest(self, sp):
                y_sum = cnt("y_sum", EXTRA["y_sum"] + self.r * EXPERTS * TILES)
                with sp.Fori(1, EXPERTS // 2) as i:
                    for b in range(2):
                        sp.wait_ge(y_sum.sem, y_sum.done((2 * i + b - 1) * TILES - 1))
                        self.load(sp, 2 * i + b, b)

            def route_pe(self, pe):
                r = self.r
                summed, taken = cnt("logit_sum", 5 * r), cnt("logit_in", 5 * r)
                for n, (at, width) in enumerate(TGROUPS):
                    pe.wait_ge(taken.sem, taken.freed(n))
                    for m in range(KT):
                        last = nc.tensor.matmul(bank[0:EXPERTS, n % 2, 0:width], self.router[:, m, :], xT[:, m, at:at + width],
                                                start=(m == 0), stop=(m == KT - 1))
                    last.then_inc(summed.sem, 1)
                pe.wait_ge(taken.sem, taken.done(4))
                for t in range(TILES):
                    last = nc.tensor.transpose(bank[:, 2, t * EXPERTS:(t + 1) * EXPERTS], self.logitsT[:, t * P:(t + 1) * P], ident[0:EXPERTS, 0:EXPERTS])
                last.then_inc(cnt("logit_turned").sem, 1)
                pe.wait_ge(cnt("routed").sem, cnt("routed", r).done(0))
                if r == 1:
                    csum, cin = cnt("choice_sum"), cnt("choice_in")
                    for k, one_hot in enumerate((self.oh1, self.oh2)):
                        for n, (at, width) in enumerate(TGROUPS):
                            v = 5 * k + n
                            pe.wait_ge(cin.sem, cin.freed(v))
                            for t in range(at // P, (at + width) // P):
                                last = nc.tensor.transpose(bank[0:EXPERTS, 4 + v % 2, t * P - at:(t + 1) * P - at], one_hot[:, t, :], ident)
                            last.then_inc(csum.sem, 1)
                    pe.wait_ge(cnt("keep_turned").sem, cnt("keep_turned").done(0))
                    for t in range(TILES):
                        last = nc.tensor.transpose(bank[:, 3, t * EXPERTS:(t + 1) * EXPERTS], self.logitsT[:, t * P:(t + 1) * P], ident[0:EXPERTS, 0:EXPERTS])
                    last.then_inc(cnt("keep_turned").sem, 1)
                    return
                turned, cin = cnt("cw_turned", 5 * (r // 2)), cnt("cw_in", 5 * (r // 2))
                for n, (at, width) in enumerate(TGROUPS):
                    pe.wait_ge(cin.sem, cin.freed(n))
                    for t in range(at // P, (at + width) // P):
                        last = nc.tensor.transpose(bank[0:EXPERTS, 4 + n % 2, t * P - at:(t + 1) * P - at], gates[:, t * EXPERTS:(t + 1) * EXPERTS], ident)
                    last.then_inc(turned.sem, 1)
                pe.wait_ge(cin.sem, cin.done(4))
                b2_sum, b2_added = cnt("b2_sum", TILES * (r // 2)), cnt("b2_added", TILES * (r // 2))
                for t in range(TILES):
                    pe.wait_ge(b2_added.sem, b2_added.freed(t))
                    nc.tensor.matmul(bank[:, 6 + t % 2, 0:DIM], self.logitsT[:, t * P:(t + 1) * P], self.b2, start=True, stop=True).then_inc(b2_sum.sem, 1)

            def route_act(self, act):
                r = self.r
                summed, taken = cnt("logit_sum", 5 * r), cnt("logit_in", 5 * r)
                for n, (at, width) in enumerate(TGROUPS):
                    act.wait_ge(summed.sem, summed.done(n))
                    nc.scalar.activation(self.logitsT[:, at:at + width], bank[0:EXPERTS, n % 2, 0:width], ACT.Identity,
                                         bias=self.router_bias if r == 2 else 0.0).then_inc(taken.sem, 1)
                act.wait_ge(cnt("exp_in").sem, cnt("exp_in", r).done(0))
                x = self.lg if r == 1 else self.ex
                nc.scalar.activation(x, x, ACT.Exp).then_inc(cnt("exp_out").sem, 1)
                if r == 1:
                    csum, cin = cnt("choice_sum"), cnt("choice_in")
                    for k in range(2):
                        for n, (at, width) in enumerate(TGROUPS):
                            v = 5 * k + n
                            act.wait_ge(csum.sem, csum.done(v))
                            nc.scalar.activation(self.chosen[:, k, at:at + width], bank[0:EXPERTS, 4 + v % 2, 0:width], ACT.Copy).then_inc(cin.sem, 1)
                    return
                turned, cin = cnt("cw_turned", 5 * (r // 2)), cnt("cw_in", 5 * (r // 2))
                for n, (at, width) in enumerate(TGROUPS):
                    act.wait_ge(turned.sem, turned.done(n))
                    nc.scalar.activation(self.logitsT[:, at:at + width], bank[0:EXPERTS, 4 + n % 2, 0:width], ACT.Copy).then_inc(cin.sem, 1)

            def route_dve(self, dve, ch):
                r = self.r
                wide = [P, TILES, EXPERTS]
                spread = lambda x: x.unsqueeze(2).broadcast_to(wide)
                order = const("descending").unsqueeze(1).broadcast_to(wide)
                V = nc.vector

                def do(ins):
                    ch.step(ins)
                    ch.settle()

                def choose(values, peak, one_hot):
                    do(V.tensor_reduce(peak, values, AX_X, ALU.max))
                    do(V.tensor_tensor(self.eq, values, spread(peak), ALU.is_equal))
                    do(V.tensor_tensor(self.eq, self.eq, order, ALU.mult))
                    do(V.tensor_reduce(self.first, self.eq, AX_X, ALU.max))
                    do(V.tensor_tensor(one_hot, self.eq, spread(self.first), ALU.is_equal))

                dve.wait_ge(cnt("logit_turned").sem, cnt("logit_turned", r).done(0))
                do(V.tensor_copy(self.lg, bank[:, 2, 0:TILES * EXPERTS].rearrange("p (t e) -> p t e", e=EXPERTS)))
                if r == 1:
                    do(V.tensor_reduce(self.m1, self.lg, AX_X, ALU.max))
                    V.tensor_tensor(self.lg, self.lg, spread(self.m1), ALU.subtract).then_inc(cnt("exp_in").sem, 1)
                    dve.wait_ge(cnt("exp_out").sem, cnt("exp_out", r).done(0))
                    do(V.tensor_reduce(self.m2, self.lg, AX_X, ALU.add))
                    do(V.reciprocal(self.m2, self.m2))
                    do(V.tensor_tensor(self.lg, self.lg, spread(self.m2), ALU.mult))
                choose(self.lg, self.m1, self.oh1)
                do(V.scalar_tensor_tensor(self.lg2, self.oh1, MASKED, self.lg, ALU.mult, ALU.add))
                choose(self.lg2, self.m2, self.oh2)
                if r == 1:
                    g1, g2 = self.m1, self.m2
                else:
                    V.tensor_tensor(self.ex, self.m2, self.m1, ALU.subtract).then_inc(cnt("exp_in").sem, 1)
                    dve.wait_ge(cnt("exp_out").sem, cnt("exp_out", r).done(0))
                    do(V.tensor_scalar(self.g1, self.ex, 1.0, None, ALU.add))
                    do(V.reciprocal(self.g1, self.g1))
                    do(V.tensor_tensor(self.g2, self.ex, self.g1, ALU.mult))
                    g1, g2 = self.g1, self.g2
                gates3 = gates[:, :].rearrange("p (t e) -> p t e", e=EXPERTS)
                do(V.tensor_tensor(gates3, self.oh1, spread(g1), ALU.mult))
                do(V.tensor_tensor(self.eq, self.oh2, spread(g2), ALU.mult))
                do(V.tensor_tensor(gates3, gates3, self.eq, ALU.add))
                dve.sem_inc(cnt("routed").sem, 1)
                if r == 1:
                    dve.wait_ge(cnt("choice_in").sem, cnt("choice_in").done(9))
                    count_on = const("ones")[0:EXPERTS, 0:1].broadcast_to([EXPERTS, GT])
                    for k in range(2):
                        for g in range(GROUPS):
                            start = 0.0 if k == 0 else self.running[:, 0, (g + 1) * GT - 1:(g + 1) * GT]
                            ch.step(V.tensor_tensor_scan(self.running[:, k, g * GT:(g + 1) * GT], count_on,
                                                         self.chosen[:, k, g * GT:(g + 1) * GT], start, ALU.mult, ALU.add))
                        ch.settle()
                    do(V.scalar_tensor_tensor(self.running, self.running, float(CAPACITY), self.chosen, ALU.is_le, ALU.mult))
                    V.tensor_tensor(self.logitsT, self.running[:, 0], self.running[:, 1], ALU.add).then_inc(cnt("keep_turned").sem, 1)
                    dve.wait_ge(cnt("keep_turned").sem, cnt("keep_turned").done(1))
                    do(V.tensor_tensor(gates[:, :], gates[:, :], bank[:, 3, 0:TILES * EXPERTS], ALU.mult))
                    return
                b2_sum, b2_added = cnt("b2_sum", TILES * (r // 2)), cnt("b2_added", TILES * (r // 2))
                for t in range(TILES):
                    dve.wait_ge(b2_sum.sem, b2_sum.done(t))
                    V.tensor_tensor(tile_h(self.acc, t), tile_h(self.acc, t), bank[:, 6 + t % 2, 0:DIM], ALU.add).then_inc(b2_added.sem, 1)

            def pe(self, pe):
                H0, Y0 = self.r * EXPERTS * 5 * FT, self.r * EXPERTS * TILES
                h_sum, h_ready = cnt("h_sum", H0), cnt("h_ready", EXTRA["h_ready"] + H0)
                y_sum, y_added = cnt("y_sum", EXTRA["y_sum"] + Y0), cnt("y_added", Y0)

                def first(e, b, j):
                    at, width = TGROUPS[j]
                    for f in range(FT):
                        n = (5 * FT) * e + FT * j + f
                        pe.wait_ge(h_ready.sem, h_ready.done(n - 4))
                        for m in range(KT):
                            last = nc.tensor.matmul(bank[:, (5 * FT * b + FT * j + f) % 4, 0:width], self.w1[b][:, m, f * P:(f + 1) * P],
                                                    xT[:, m, at:at + width], start=(m == 0), stop=(m == KT - 1))
                        last.then_inc(h_sum.sem, 1)

                def second(e, b, j):
                    at, width = TGROUPS[j]
                    pe.wait_ge(h_ready.sem, h_ready.done((5 * FT) * e + FT * j + FT - 1))
                    for t in range(at // P, (at + width) // P):
                        pe.wait_ge(y_added.sem, y_added.freed(e * TILES + t))
                        for f in range(FT):
                            last = nc.tensor.matmul(bank[:, 4 + (b + t) % 2, 0:DIM], self.hid[(b + j) % 2][:, f, t * P - at:(t + 1) * P - at],
                                                    self.w2[b][:, f, :], start=(f == 0), stop=(f == FT - 1))
                        last.then_inc(y_sum.sem, 1)

                with pe.Fori(0, EXPERTS // 2) as i:
                    for b in range(2):
                        e = 2 * i + b
                        pe.wait_ge(expert_loaded[b], 32 * i + 32 * (1 + self.r * EXPERTS // 2))
                        first(e, b, 0)
                        for j in range(5):
                            if j + 1 < 5:
                                first(e, b, j + 1)
                            second(e, b, j)

            def act(self, act):
                H0, Y0 = self.r * EXPERTS * 5 * FT, self.r * EXPERTS * TILES
                h_sum, h_ready, y_sum = cnt("h_sum", H0), cnt("h_ready", EXTRA["h_ready"] + H0), cnt("y_sum", EXTRA["y_sum"] + Y0)
                for e, b in ring(act, EXPERTS):
                    for j, (at, width) in enumerate(TGROUPS):
                        back, gone = (0, j - 2) if j >= 2 else (1, j + 3)
                        act.wait_ge(y_sum.sem, y_sum.done((e - back) * TILES + sum(TGROUPS[gone]) // P - 1))
                        for f in range(FT):
                            n = 5 * FT * e + FT * j + f
                            wait_apart(act, h_sum.sem, h_sum.done(n))
                            bias = self.b1[:, ds(e * FT + f, 1)] if self.b1 is not None else 0.0
                            nc.scalar.activation(self.hid[(b + j) % 2][:, f, 0:width], bank[:, (5 * FT * b + FT * j + f) % 4, 0:width],
                                                 self.func, bias=bias).then_inc(h_ready.sem, 1)

            def dve(self, dve):
                Y0 = self.r * EXPERTS * TILES
                y_sum, y_added = cnt("y_sum", EXTRA["y_sum"] + Y0), cnt("y_added", Y0)
                for e, b in ring(dve, EXPERTS):
                    for t in range(TILES):
                        n = e * TILES + t
                        dve.wait_ge(y_sum.sem, y_sum.done(n))
                        dve.wait_ge(y_added.sem, y_added.freed(n))
                        nc.vector.scalar_tensor_tensor(tile_h(self.acc, t), bank[:, 4 + (b + t) % 2, 0:DIM], gates[:, ds(e + t * EXPERTS, 1)],
                                                       tile_h(self.acc, t), ALU.mult, ALU.add).then_inc(y_added.sem, 1)

        def quant_dve(dve, ch):
            q = quantised
            half = TOKENS // 2
            for m in range(KT):
                for s in range(2):
                    x = xT[:, m, s * half:(s + 1) * half]
                    ch.step(nc.vector.tensor_scalar(x, x, -128.0, 127.0, ALU.max, ALU.min))
                    ch.settle()
                    ch.step(nc.vector.tensor_scalar(q[:, m, s * half:(s + 1) * half], x, MAGIC, MAGIC, ALU.add, ALU.subtract))
            ch.step(nc.vector.tensor_copy(weight_q, w_int8[:, :].bitcast(I8).rearrange("p (k n) -> p k n", k=KT)))
            ch.settle()
            dve.sem_inc(cnt("quant").sem, 1)
            done, added = cnt("proj_sum", TILES * PROJ["L0f"]), cnt("proj_added", TILES * PROJ["L0f"])
            for t, b in ring(dve, TILES, ch, 1):
                dve.wait_ge(done.sem, done.done(t))
                ch.step(nc.vector.scalar_tensor_tensor(quant_out[b], bank[:, b, 0:DIM], float(np.float32(0.02 * 0.01)), const("bias_int8"), ALU.mult, ALU.add))
                ch.settle()
                nc.vector.tensor_tensor(tile_h(h, t), tile_h(h, t), quant_out[b], ALU.add).then_inc(added.sem, 1)

        def quant_pe(pe):
            pe.wait_ge(cnt("quant").sem, cnt("quant").done(0))
            done, added = cnt("proj_sum", TILES * PROJ["L0f"]), cnt("proj_added", TILES * PROJ["L0f"])
            for t, b in ring(pe, TILES):
                pe.wait_ge(added.sem, added.freed(t))
                for m in range(KT):
                    last = nc.tensor.matmul(bank[:, b, 0:DIM], quantised[:, m, ds(t * P, P)], weight_q[:, m, :], start=(m == 0), stop=(m == KT - 1))
                last.then_inc(done.sem, 1)

        qc = Carve()
        quantised = qc(KD, TOKENS).bitcast(BF16).rearrange("p (k n) -> p k n", k=KT)
        weight_q = qc(KD, DIM).bitcast(BF16).rearrange("p (k n) -> p k n", k=KT)
        quant_out = [qc(P, DIM) for _ in range(2)]

        class StateSpace:
            def __init__(self):
                c = Carve()
                wide = lambda: c(P, CI, GT)
                self.xp = c(P, CI, GI, SEQ + 3)
                self.acc, self.sig = wide(), wide()
                self.x2 = self.sig
                quarter = lambda n: kept[:, n * CI * GT:(n + 1) * CI * GT].rearrange("p (c n) -> p c n", c=CI)
                self.x, self.z, self.dt, self.tmp = (quarter(n) for n in range(4))
                self.w64, self.dt64 = c(P, CI, GI, SLOT), c(P, CI, GI, SLOT)
                self.k64, self.kk64 = c(STATE, GI, SLOT), c(STATE, GI, SLOT)
                self.q, self.low = c(STATE, GT), c(RANK, GT)
                self.kk = c(P, GT)
                self.n1, self.n2, self.n3, self.n4 = (c(P, GT) for _ in range(4))
                self.qb = c(P, STATE, GT)
                self.lists = [c(P, 2 * CI * P + 2 * STATE) for _ in range(2)]
                self.spread_k = [c(P, STATE, SEQ) for _ in range(2)]
                self.spread_kk = [c(P, STATE, SEQ) for _ in range(2)]
                self.decay = [c(P, STATE * SEQ) for _ in range(2)]
                self.state = [c(P, STATE * SEQ) for _ in range(2)]
                self.w_in = const("in_proj").rearrange("p (k n) -> p k n", k=KT)
                self.w_x = const("x_proj").rearrange("p (c n) -> p c n", c=CI)
                self.w_dt = const("dt_head")
                self.conv_w = const("conv_w").rearrange("p (c j) -> p c j", c=CI)
                self.conv_b, self.dt_b, self.d = const("conv_b"), const("dt_b"), const("d")

            def pool(self, pool, ch):
                for x, value in ((self.xp[:, :, :, 0:3], 0.0), (self.w64, 0.0), (self.dt64, 0.0), (self.k64, 0.0), (self.kk64, 0.0)):
                    for n in range(x.shape[1]) if len(x.shape) == 4 else [None]:
                        ch.step(nc.gpsimd.memset(x[:, n] if n is not None else x, value))
                ch.settle()
                for x in [self.dt64[:, n, :, SEQ:SEQ + 1] for n in range(CI)] + [self.kk64[:, :, SEQ:SEQ + 1]]:
                    ch.step(nc.gpsimd.memset(x, 1.0))
                ch.settle()
                pool.sem_inc(cnt("prepared").sem, 1)
                lists_in, spread = cnt("lists_in"), cnt("lists_spread")
                scanned, weighed, q_in = cnt("scanned"), cnt("weighed"), cnt("q_in")
                shape = [P, STATE, SEQ]

                def build(u, p, b):
                    pool.wait_ge(lists_in.sem, lists_in.done(u))
                    at = 2 * CI * P
                    ks = self.lists[b][:, at:at + STATE].unsqueeze(2).broadcast_to(shape)
                    kks = self.lists[b][:, at + STATE:at + 2 * STATE].unsqueeze(2).broadcast_to(shape)
                    nc.gpsimd.tensor_tensor(self.spread_k[b], ks, const("fade").unsqueeze(1).broadcast_to(shape), ALU.mult).then_inc(spread.sem, 1)
                    nc.gpsimd.tensor_tensor(self.spread_kk[b], kks, const("own").unsqueeze(1).broadcast_to(shape), ALU.mult).then_inc(spread.sem, 1)

                with pool.Fori(0, GROUPS) as g:
                    u = g * PAIRS
                    build(u, 0, 0)
                    pool.wait_ge(q_in.sem, q_in.done(STATE * g + STATE - 1))
                    for p in range(PAIRS):
                        for n in range(6):
                            img, c = divmod(n, CI)
                            v, b = 6 * (u + p) + n, n % 2
                            at = (2 * p + img) * SEQ
                            pool.wait_ge(scanned.sem, scanned.done(v))
                            st = self.state[b].rearrange("p (n t) -> p n t", t=SEQ)
                            nc.gpsimd.tensor_tensor(st, st, self.qb[:, :, at:at + SEQ], ALU.mult).then_inc(weighed.sem, 1)
                            if n == 3 and p + 1 < PAIRS:
                                build(u + p + 1, p + 1, (p + 1) % 2)

            def pe(self, pe):
                pe.wait_ge(cnt("prepared").sem, cnt("prepared", 1).done(0))
                C = {n: cnt(n) for n in COUNTS}
                wait = lambda n, k: pe.wait_ge(C[n].sem, C[n].done(k))
                freed = lambda n, k: pe.wait_ge(C[n].sem, C[n].freed(k))
                inc = lambda ins, n: ins.then_inc(C[n].sem, 1)
                flat = lambda x: x.rearrange("p a b -> p (a b)")

                def turn(u, p):
                    wait("lists_in", u - 1)
                    for c in range(CI):
                        nc.tensor.transpose(bank[:, 6, c * P:(c + 1) * P], flat(self.w64[:, c, 2 * p:2 * p + 2, :]), ident)
                    for c in range(CI):
                        nc.tensor.transpose(bank[:, 7, c * P:(c + 1) * P], flat(self.dt64[:, c, 2 * p:2 * p + 2, :]), ident)
                    nc.tensor.transpose(bank[:, 6, CI * P:CI * P + STATE], flat(self.k64[:, 2 * p:2 * p + 2, :]), ident[0:STATE, 0:STATE])
                    last = nc.tensor.transpose(bank[:, 7, CI * P:CI * P + STATE], flat(self.kk64[:, 2 * p:2 * p + 2, :]), ident[0:STATE, 0:STATE])
                    inc(last, "lists_turned")

                with pe.Fori(0, GROUPS) as g:
                    u = g * PAIRS
                    wait("reduced", 6 * PAIRS * g - 1)
                    wait("a_in", 6 * PAIRS * g - 1)
                    for m in range(6):
                        freed("in_taken", 6 * g + m)
                        for kk in range(KT):
                            last = nc.tensor.matmul(bank[:, m % 2, 0:GT], self.w_in[:, kk, m * P:(m + 1) * P], xT[:, kk, ds(g * GT, GT)],
                                                    start=(kk == 0), stop=(kk == KT - 1))
                        inc(last, "in_sum")
                    wait("x_ready", g)
                    for j, (at, rows) in enumerate(((0, RANK), (RANK, STATE), (RANK + STATE, STATE))):
                        for c in range(CI):
                            last = nc.tensor.matmul(bank[0:rows, 2 + j, 0:GT], self.w_x[:, c, at:at + rows], self.x[:, c, :],
                                                    start=(c == 0), stop=(c == CI - 1))
                    inc(last, "low_sum")
                    wait("low_in", g)
                    wait("q_in", STATE * g - 1)
                    for c in range(CI):
                        last = nc.tensor.matmul(bank[:, 5 + c, 0:GT], self.w_dt[:, c * P:(c + 1) * P], self.low, start=True, stop=True)
                    inc(last, "dt_sum")
                    wait("in_taken", 6 * g + 5)
                    for half in range(2):
                        last = nc.tensor.matmul(bank[:, 0, half * GT // 2:(half + 1) * GT // 2], ones[0:STATE, 0:P],
                                                self.kk64[:, half * GI // 2:(half + 1) * GI // 2, 0:SEQ], start=True, stop=True)
                    inc(last, "k2_sum")
                    wait("dt_gate", g)
                    for n in range(STATE):
                        freed("q_in", STATE * g + n)
                        inc(nc.tensor.matmul(bank[:, 6 + n % 2, 0:GT], ident[0:STATE, n:n + 1].broadcast_to([STATE, P]), self.q, start=True, stop=True), "q_sum")
                    wait("dx_squared", g)
                    for c in range(CI):
                        last = nc.tensor.matmul(bank[:, 1, 0:GT], ones[:, 0:P], self.tmp[:, c, :], start=(c == 0), stop=(c == CI - 1))
                    inc(last, "dx_sum")
                    wait("w_ready", g)
                    wait("q_in", STATE * g + STATE - 1)
                    turn(u, 0)
                    for p in range(PAIRS):
                        wait("lists_spread", 2 * (u + p) + 1)
                        for n in range(6):
                            img, c = divmod(n, CI)
                            v, b, r0 = 6 * (u + p) + n, n % 2, img * SLOT
                            wait("scanned", v - 2)
                            wait("a_in", v - 1)
                            for half in range(2):
                                nc.tensor.matmul(bank[:, 2 * b + half, 0:GT], self.lists[p % 2][r0:r0 + SEQ, c * P:(c + 1) * P],
                                                 flat(self.spread_k[p % 2])[r0:r0 + SEQ, half * GT:(half + 1) * GT], start=True, stop=True)
                            for half in range(2):
                                last = nc.tensor.matmul(bank[:, 4 + half, 0:GT], self.lists[p % 2][r0:r0 + SEQ + 1, (CI + c) * P:(CI + c + 1) * P],
                                                        flat(self.spread_kk[p % 2])[r0:r0 + SEQ + 1, half * GT:(half + 1) * GT], start=True, stop=True)
                            inc(last, "v_expanded")
                            if n == 1 and p + 1 < PAIRS:
                                turn(u + p + 1, p + 1)

            def act(self, act):
                act.wait_ge(cnt("prepared").sem, cnt("prepared", 1).done(0))
                C = {n: cnt(n) for n in COUNTS}
                wait = lambda n, k: act.wait_ge(C[n].sem, C[n].done(k))
                inc = lambda ins, n: ins.then_inc(C[n].sem, 1)
                A = nc.scalar.activation
                images = lambda x: x.rearrange("p (i t) -> p i t", t=SEQ)

                def lists(u, b):
                    wait("lists_turned", u)
                    x, n = self.lists[b], CI * P
                    A(x[:, 0:n], bank[:, 6, 0:n], ACT.Copy)
                    A(x[:, n:2 * n], bank[:, 7, 0:n], ACT.Copy)
                    A(x[:, 2 * n:2 * n + STATE], bank[:, 6, n:n + STATE], ACT.Copy)
                    inc(A(x[:, 2 * n + STATE:], bank[:, 7, n:n + STATE], ACT.Copy), "lists_in")

                with act.Fori(0, GROUPS) as g:
                    u = g * PAIRS
                    for m in range(6):
                        wait("in_sum", 6 * g + m)
                        psum = bank[:, m % 2, 0:GT]
                        if m < CI:
                            inc(A(self.xp[:, m, :, 3:], images(psum), ACT.Copy), "in_taken")
                        else:
                            inc(A(self.sig[:, m - CI, :], psum, ACT.Sigmoid), "z_gate")
                    wait("conv_out", g)
                    inc(A(self.sig, self.acc, ACT.Sigmoid), "conv_gate")
                    wait("low_sum", g)
                    A(self.low, bank[0:RANK, 2, 0:GT], ACT.Copy)
                    A(self.k64[:, :, 0:SEQ], images(bank[0:STATE, 3, 0:GT]), ACT.Copy)
                    A(self.kk64[:, :, 0:SEQ], images(bank[0:STATE, 3, 0:GT]), ACT.Square)
                    inc(A(self.q, bank[0:STATE, 4, 0:GT], ACT.Copy), "low_in")
                    wait("dt_sum", g)
                    for c in range(CI):
                        last = A(self.dt[:, c, :], bank[:, 5 + c, 0:GT], ACT.Sigmoid, bias=self.dt_b[:, c:c + 1])
                    inc(last, "dt_gate")
                    wait("k2_sum", g)
                    inc(A(self.kk, bank[:, 0, 0:GT], ACT.Copy), "k2_in")
                    for n in range(STATE):
                        wait("q_sum", STATE * g + n)
                        if n == 0:
                            wait("weighed", 6 * PAIRS * g - 1)
                        inc(A(self.qb[:, n, :], bank[:, 6 + n % 2, 0:GT], ACT.Copy), "q_in")
                    wait("dx_ready", g)
                    inc(A(self.tmp, self.x2, ACT.Square), "dx_squared")
                    wait("norm_in", g)
                    inc(A(self.n2, self.n1, ACT.Sqrt), "norm_out")
                    lists(u, 0)
                    for p in range(PAIRS):
                        for n in range(6):
                            v = 6 * (u + p) + n
                            wait("v_expanded", v)
                            wait("scanned", v - 2)
                            inc(A(self.decay[n % 2].rearrange("p (a n) -> p a n", a=2), bank[:, 4:6, 0:GT], ACT.Copy), "a_in")
                            if n == 2 and p + 1 < PAIRS:
                                lists(u + p + 1, (p + 1) % 2)

            def dve(self, dve, ch):
                dve.wait_ge(cnt("prepared").sem, cnt("prepared", 1).done(0))
                C = {n: cnt(n) for n in COUNTS}
                wait = lambda n, k: dve.wait_ge(C[n].sem, C[n].done(k))
                inc = lambda ins, n: ins.then_inc(C[n].sem, 1)
                V = nc.vector
                images = lambda x: x.rearrange("p (i t) -> p i t", t=SEQ)

                def do(ins):
                    ch.step(ins)
                    ch.settle()

                all_c = lambda x: x.unsqueeze(1).broadcast_to([P, CI, GT])
                with ch.loop(GROUPS, SSM_STEPS) as g:
                    u = g * PAIRS
                    for m in range(CI, 6):
                        wait("z_gate", CI * g + m - CI)
                        inc(V.tensor_tensor(self.z[:, m - CI, :], bank[:, m % 2, 0:GT], self.sig[:, m - CI, :], ALU.mult), "in_taken")
                    wait("in_taken", 6 * g + 5)
                    for j in range(4):
                        for c in range(CI):
                            src, acc, w = self.xp[:, c, :, j:j + SEQ], images(self.acc[:, c, :]), self.conv_w[:, c, j:j + 1]
                            if j == 0:
                                ch.step(V.tensor_scalar(acc, src, w, self.conv_b[:, c:c + 1], ALU.mult, ALU.add))
                            else:
                                ch.step(V.scalar_tensor_tensor(acc, src, w, acc, ALU.mult, ALU.add))
                        ch.settle()
                    dve.sem_inc(C["conv_out"].sem, 1)
                    wait("conv_gate", g)
                    inc(V.tensor_tensor(self.x, self.acc, self.sig, ALU.mult), "x_ready")
                    wait("dt_gate", g)
                    wait("k2_in", g)
                    do(V.tensor_tensor(self.tmp, self.dt, all_c(self.kk), ALU.mult))
                    do(V.tensor_scalar(self.tmp, self.tmp, 1.0, None, ALU.add))
                    do(V.reciprocal(self.tmp, self.tmp))
                    for c in range(CI):
                        ch.step(V.tensor_tensor(self.dt64[:, c, :, 0:SEQ], images(self.dt[:, c, :]), images(self.tmp[:, c, :]), ALU.mult))
                    ch.settle()
                    for c in range(CI):
                        ch.step(V.tensor_tensor(images(self.x2[:, c, :]), self.dt64[:, c, :, 0:SEQ], images(self.x[:, c, :]), ALU.mult))
                    ch.settle()
                    dve.sem_inc(C["dx_ready"].sem, 1)
                    wait("dx_sum", g)
                    inc(V.tensor_tensor(self.n1, bank[:, 1, 0:GT], self.kk, ALU.mult), "norm_in")
                    wait("norm_out", g)
                    do(V.tensor_scalar(self.n3, self.n2, 1e-7, None, ALU.add))
                    do(V.reciprocal(self.n3, self.n3))
                    do(V.tensor_tensor(self.n2, self.n2, self.n3, ALU.mult))
                    do(V.tensor_tensor(self.n2, self.n2, self.n2, ALU.mult))
                    do(V.tensor_scalar(self.n4, self.n2, 2.0315, -4.775, ALU.mult, ALU.add))
                    do(V.tensor_tensor(self.n4, self.n4, self.n2, ALU.mult))
                    do(V.scalar_tensor_tensor(self.n4, self.n4, 3.4445, self.n3, ALU.add, ALU.mult))
                    for c in range(CI):
                        ch.step(V.tensor_tensor(self.w64[:, c, :, 0:SEQ], images(self.x2[:, c, :]), images(self.n4), ALU.mult))
                    ch.settle()
                    dve.sem_inc(C["w_ready"].sem, 1)

                    def reduce(v, p, n):
                        img, c = divmod(n, CI)
                        at = (2 * p + img) * SEQ
                        wait("weighed", v)
                        inc(V.tensor_reduce(self.acc[:, c, at:at + SEQ], self.state[n % 2].rearrange("p (n t) -> p t n", t=SEQ), AX_X, ALU.add), "reduced")

                    for p in range(PAIRS):
                        for n in range(6):
                            v, b = 6 * (u + p) + n, n % 2
                            wait("a_in", v)
                            wait("reduced", v - 2)
                            for half in range(2):
                                last = V.tensor_tensor_scan(self.state[b][:, half * GT:(half + 1) * GT], self.decay[b][:, half * GT:(half + 1) * GT],
                                                            bank[:, 2 * b + half, 0:GT], 0.0, ALU.mult, ALU.add)
                            inc(last, "scanned")
                            if p or n:
                                reduce(v - 1, p if n else p - 1, n - 1 if n else 5)
                    reduce(6 * u + 6 * PAIRS - 1, PAIRS - 1, 5)
                    wait("reduced", 6 * u + 6 * PAIRS - 1)
                    for c in range(CI):
                        ch.step(V.scalar_tensor_tensor(self.acc[:, c, :], self.x[:, c, :], self.d[:, c:c + 1], self.acc[:, c, :], ALU.mult, ALU.add))
                    ch.settle()
                    do(V.tensor_tensor(zT[:, :, ds(g * GT, GT)], self.acc, self.z, ALU.mult))

        layer0, layer1, layer2, layer3 = Tokens12(), Heads16(0, "L1", True), StateSpace(), Parts8()
        layer3f = Heads16(3, "L3f", False)
        experts = [Experts(0, h), Experts(1, h), Experts(2, kept)]
        bias_of = lambda n: const(n)
        weight_of = lambda n, kt: const(n).rearrange("p (k n) -> p k n", k=kt)
        credit_share = {e: COUNTS[i::4] for i, e in enumerate(("sp", "act", "pe", "dve"))}

        def credits(eng, name):
            for n in credit_share[name]:
                eng.sem_inc(counts[n].sem, CREDITS + EXTRA.get(n, 0))

        slow_ended = sem("slow_ended")

        class Stages:

            def __init__(self, eng, slow=False):
                self.eng, self.k, self.slow = eng, 0, slow

            def end(self):
                own, k = (slow_ended if self.slow else stage_ended), self.k
                self.eng.drain().then_inc(own, 1)
                self.eng.wait_ge(stage_ended, 3 * (k + 1))
                if k == 0 or k >= SLOW_FROM:
                    self.eng.wait_ge(slow_ended, 2 if k == 0 else 2 * (k - SLOW_FROM + 2))
                self.k = SLOW_FROM if self.slow and k == 0 else k + 1

            def skip(self, n):
                for _ in range(n):
                    self.end()

        block = ctx.enter_context(nc.Block())

        @block.sync
        def _(sp):
            stage = Stages(sp, slow=True)
            credits(sp, "sp")
            sp.dma_start(w_emb, t_in["w_emb"]).then_inc(load_early, 16)
            sp.dma_start(select38, t_in["select38"]).then_inc(load_early, 16)
            sp.dma_start(rows_a[0:1, :], t_in["cls_tok"]).then_inc(load_early, 16)
            sp.dma_start(rows_a[1:SEQ, :], t_in["pos"]).then_inc(load_early, 16)
            sp.dma_start(rows_b[1:2, :], t_in["cls_token"]).then_inc(load_early, 16)
            sp.dma_start(rows_b[2:SEQ, :], t_in["b_emb"].broadcast_to([SEQ - 2, DIM])).then_inc(load_early, 16)
            stage.end()
            sp.dma_start(wte_tail, t_in["wte"][WTE_ROWS - WTE_TAIL:WTE_ROWS, :]).then_inc(load_tail, 16)
            with sp.Fori(0, TILES // 2) as i:
                for b in range(2):
                    patch_load(sp, 2 * i + b, b)
                    wte_load(sp, 2 * i + b, b)
            patch_load(sp, TILES - 1, 0)
            sp.dma_start(resident[:, :], t_in["resident"]).then_inc(load_resident, 16)
            sp.dma_start(w_int8[:, :], t_in["w_int8"]).then_inc(load_resident, 16)
            sp.wait_ge(cnt("patch_taken").sem, cnt("patch_taken").done(TILES - 1))
            sp.dma_start(layer0.wo.rearrange("p n e -> p (n e)"), t_in["wo0"]).then_inc(load_wo, 16)
            with sp.Fori(TILES // 2, WTE_CH // 2) as i:
                for b in range(2):
                    wte_load(sp, 2 * i + b, b)
            stage.skip(11 - SLOW_FROM)
            experts[0].sp_first(sp)
            stage.skip(2)
            experts[0].sp_rest(sp)
            stage.skip(4)
            experts[1].sp_first(sp)
            stage.skip(2)
            experts[1].sp_rest(sp)
            stage.skip(7)
            experts[2].sp_first(sp)
            stage.skip(2)
            experts[2].sp_rest(sp)
            stage.skip(2)
            sp.dma_start(out.rearrange("i s e -> (i s) e").rearrange("(t p) e -> p t e", p=P),
                         h[:, :].rearrange("p (t e) -> p t e", e=DIM)).then_inc(stored, 16)
            sp.wait_ge(stored, 16)

        @block.gpsimd
        def _(pool):
            ch = Chain(pool, chains["pool"])
            stage = Stages(pool, slow=True)
            stage.end()
            wte_pool(pool, ch)
            stage.skip(2)
            proj_pool(pool, PROJ["L0"], zT, KD, KT)
            stage.skip(4)
            layer1.pool(pool, ch)
            stage.end()
            proj_pool(pool, PROJ["L1"], zT, KD, KT)
            stage.skip(5)
            layer2.pool(pool, ch)
            stage.end()
            proj_pool(pool, PROJ["L2"], zT, P, CI)
            stage.skip(5)
            layer3.pool(pool, ch)
            stage.end()
            proj_pool(pool, PROJ["L3"], zT, KF, 3)
            stage.skip(2)
            layer3f.pool(pool, ch)
            stage.end()
            proj_pool(pool, PROJ["L3f"], zT, KD, KT)
            stage.skip(5)

        @block.scalar
        def _(act):
            ch = Chain(act, chains["act"])
            stage = Stages(act)
            credits(act, "act")
            stage.skip(2)
            act.wait_ge(load_resident, 32)
            ln_act(act, 0, turn=False)
            ln_act(act, 1, gain=const("ln_w"))
            stage.end()
            layer0.act(act, ch)
            stage.end()
            layer0.offset_act(act)
            stage.skip(2)
            ln_act(act, 2, scale=50.0)
            stage.skip(2)
            ln_act(act, 3)
            stage.end()
            layer1.act(act)
            stage.skip(2)
            ln_act(act, 4)
            stage.end()
            experts[0].route_act(act)
            stage.end()
            experts[0].act(act)
            stage.end()
            ln_act(act, 5)
            stage.end()
            layer2.act(act)
            stage.skip(2)
            ln_act(act, 6)
            stage.end()
            experts[1].route_act(act)
            stage.end()
            experts[1].act(act)
            stage.end()
            ln_act(act, 7)
            stage.end()
            layer3.act(act)
            stage.skip(2)
            ln_act(act, 8, turn=False)
            ln_act(act, 9, gain=const("ln1_g"), shift=const("ln1_b"))
            stage.end()
            layer3f.act(act)
            stage.skip(2)
            ln_act(act, 10, gain=const("ln2_g"), shift=const("ln2_b"))
            stage.end()
            experts[2].route_act(act)
            stage.end()
            experts[2].act(act)
            stage.skip(2)

        @block.tensor
        def _(pe):
            stage = Stages(pe)
            credits(pe, "pe")
            stage.end()
            patch_pe(pe)
            stage.end()
            pe.wait_ge(load_resident, 32)
            ln_pe(pe, 1)
            stage.end()
            layer0.pe(pe)
            stage.end()
            layer0.offset_pe(pe)
            stage.end()
            turn_pe(pe, PROJ["L0"])
            stage.end()
            ln_pe(pe, 2)
            stage.end()
            quant_pe(pe)
            stage.end()
            ln_pe(pe, 3)
            stage.end()
            layer1.pe(pe)
            stage.end()
            proj_pe(pe, PROJ["L1"], weight_of("wo1", KT), KD, KT, bias_of("bo1"))
            stage.end()
            ln_pe(pe, 4)
            stage.end()
            experts[0].route_pe(pe)
            stage.end()
            experts[0].pe(pe)
            stage.end()
            ln_pe(pe, 5)
            stage.end()
            layer2.pe(pe)
            stage.end()
            proj_pe(pe, PROJ["L2"], weight_of("out_proj", CI), P, CI)
            stage.end()
            ln_pe(pe, 6)
            stage.end()
            experts[1].route_pe(pe)
            stage.end()
            experts[1].pe(pe)
            stage.end()
            ln_pe(pe, 7)
            stage.end()
            layer3.pe(pe)
            stage.end()
            proj_pe(pe, PROJ["L3"], weight_of("wo3", 3), KF, 3, bias_of("bo3"))
            stage.end()
            ln_pe(pe, 9)
            stage.end()
            layer3f.pe(pe)
            stage.end()
            proj_pe(pe, PROJ["L3f"], weight_of("wof", KT), KD, KT, bias_of("bof"))
            stage.end()
            ln_pe(pe, 10)
            stage.end()
            experts[2].route_pe(pe)
            stage.end()
            experts[2].pe(pe)
            stage.skip(2)

        @block.vector
        def _(dve):
            ch = Chain(dve, chains["dve"])
            stage = Stages(dve)
            credits(dve, "dve")
            stage.end()
            patch_dve(dve, ch)
            stage.end()
            dve.wait_ge(load_resident, 32)
            ln_dve(dve, ch, 0, h, keep=kept, turn=False)
            ch.settle()
            ln_dve(dve, ch, 1, kept)
            stage.end()
            layer0.dve(dve, ch)
            stage.end()
            layer0.offset_dve(dve, ch)
            stage.end()
            proj_dve(dve, PROJ["L0"], h)
            stage.end()
            ln_dve(dve, ch, 2, h)
            stage.end()
            quant_dve(dve, ch)
            stage.end()
            ln_dve(dve, ch, 3, h)
            stage.end()
            layer1.dve(dve, ch)
            stage.end()
            proj_dve(dve, PROJ["L1"], h)
            stage.end()
            ln_dve(dve, ch, 4, h)
            stage.end()
            experts[0].route_dve(dve, ch)
            stage.end()
            experts[0].dve(dve)
            stage.end()
            ln_dve(dve, ch, 5, h)
            stage.end()
            layer2.dve(dve, ch)
            stage.end()
            proj_dve(dve, PROJ["L2"], h)
            stage.end()
            ln_dve(dve, ch, 6, h)
            stage.end()
            experts[1].route_dve(dve, ch)
            stage.end()
            experts[1].dve(dve)
            stage.end()
            ln_dve(dve, ch, 7, h)
            stage.end()
            layer3.dve(dve, ch)
            stage.end()
            proj_dve(dve, PROJ["L3"], h)
            stage.end()
            ln_dve(dve, ch, 8, h, keep=kept, turn=False)
            ch.settle()
            ln_dve(dve, ch, 9, kept)
            stage.end()
            layer3f.dve(dve, ch)
            stage.end()
            proj_dve(dve, PROJ["L3f"], kept)
            stage.end()
            ln_dve(dve, ch, 10, kept)
            stage.end()
            experts[2].route_dve(dve, ch)
            stage.end()
            experts[2].dve(dve)
            stage.end()
            nc.vector.tensor_tensor(h[:, :], h[:, :], kept[:, :], ALU.add)
            stage.end()


def k_major(w, kt):
    w = np.asarray(w).T
    return w.reshape(kt, w.shape[0] // kt, w.shape[1]).transpose(1, 0, 2).reshape(w.shape[0] // kt, -1)


def by_feature(v, kt):
    v = np.asarray(v)
    return v.reshape(kt, -1).T


def constants():
    f = np.float32
    c = {"ident": np.eye(P, dtype=f), "ones": np.ones((P, P), f)}
    s, t = np.arange(P)[:, None] % SLOT, np.arange(SEQ)[None, :]
    c["causal"] = np.where((s < SEQ) & (t > s), f(MASKED), f(0)).astype(f)
    c["nreg"] = np.broadcast_to((f(1) / np.arange(1, SEQ + 1, dtype=f))[None], (KD, SEQ))
    inv = f(1) / f(10000.0) ** (np.arange(0, HD, 2, dtype=f) / f(HD))
    ang = np.arange(SEQ, dtype=f)[None, :] * inv[:, None]
    c["cos"], c["sin"] = (np.tile(np.concatenate([fn(ang)] * 2, 0), (HPK, 1)).astype(f) for fn in (np.cos, np.sin))
    c["hmask"] = (np.arange(KD)[:, None] // HD == np.arange(HPK)[None]).astype(f)
    c["hmask8"] = (np.arange(KF)[:, None] // HD3 == np.arange(NH3)[None]).astype(f)
    row = np.arange(G3)[:, None, None] // SEQ
    c["vmask"] = (np.arange(KD)[None, None] // HD == 3 * np.arange(2)[None, :, None] + row).astype(f).reshape(G3, -1)
    c["vmask8"] = (np.arange(KF)[None, None] // HD3 == 3 * np.arange(3)[None, :, None] + row).astype(f).reshape(G3, -1)
    c["fade"] = np.where((s < SEQ) & (t >= s), f(0.9) ** np.maximum(t - s, 0).astype(f), f(0)).astype(f)
    c["own"] = (-1.0 * ((t == s) & (t > 0)) + 1.0 * ((s == SEQ) & (t > 0))).astype(f)
    c["descending"] = np.broadcast_to(np.arange(EXPERTS, 0, -1, dtype=f)[None], (P, EXPERTS))
    c["rot_sign"] = np.where(np.arange(KD) % HD < HD // 2, f(-1), f(1)).astype(f)[:, None]
    return c


def lay_out(i):
    a = {n: np.asarray(v) for n, v in i.items()}
    rot = np.arange(DIM).reshape(HEADS, 2, HD // 2)[:, ::-1].reshape(-1)
    parts = [w * DIM + np.arange(NH3)[:, None] * 24 + s * HD3 + np.arange(HD3)[None] for w, s in
             ((0, 1), (0, 2), (1, 0), (1, 1), (1, 2), (2, 0), (2, 1), (2, 2))]
    parts = np.concatenate([x.reshape(-1) for x in parts])
    packed = constants()
    packed.update({
        "wqk": k_major(a["L0_attn_W_qk"], KT),
        "ln_w": by_feature(a["L0_attn_ln_w"], KT),
        "bias_int8": np.broadcast_to(a["L0_ffn_bias"][None], (P, DIM)),
        "qkv1": k_major(np.concatenate([a["L1_attn_Wq"], a["L1_attn_Wk"], a["L1_attn_Wv"]], 0), KT),
        "bq": by_feature(a["L1_attn_bq"], KT), "bk": by_feature(a["L1_attn_bk"], KT), "bv": by_feature(a["L1_attn_bv"], KT),
        "bq_turned": by_feature(a["L1_attn_bq"][rot], KT), "bk_turned": by_feature(a["L1_attn_bk"][rot], KT),
        "wo1": k_major(a["L1_attn_Wo"], KT), "bo1": a["L1_attn_bo"][None],
        "router1": k_major(a["L1_ffn_Wr"], KT), "b2_1": a["L1_ffn_bo"],
        "b1_1": a["L1_ffn_bi"].reshape(EXPERTS * FT, P).T,
        "in_proj": k_major(a["L2_attn_in_proj_w"], KT), "x_proj": k_major(a["L2_attn_x_proj_w"], CI),
        "dt_head": a["L2_attn_dt_head_w"].T, "dt_b": by_feature(a["L2_attn_dt_head_b"], CI),
        "conv_w": a["L2_attn_conv_w"].reshape(CI, P, 4).transpose(1, 0, 2).reshape(P, -1),
        "conv_b": by_feature(a["L2_attn_conv_b"], CI), "d": by_feature(a["L2_attn_D"], CI),
        "out_proj": k_major(a["L2_attn_out_proj_w"], CI),
        "router2": k_major(a["L2_ffn_w_router"].T, KT),
        "qkv3": k_major(a["L3_attn_w_qkv"][parts], KT), "wo3": k_major(a["L3_attn_w_proj"], 3), "bo3": a["L3_attn_b_proj"][None],
        "qkvf": k_major(a["L3_ffn_qkv_w"], KT), "wof": k_major(a["L3_ffn_proj_w"], KT), "bof": a["L3_ffn_proj_b"][None],
        "ln1_g": by_feature(a["L3_ffn_ln1_g"], KT), "ln1_b": by_feature(a["L3_ffn_ln1_b"], KT),
        "ln2_g": by_feature(a["L3_ffn_ln2_g"], KT), "ln2_b": by_feature(a["L3_ffn_ln2_b"], KT),
        "router3f": k_major(a["L3_ffn_gate_w"], KT), "gate_b": a["L3_ffn_gate_b"][:, None],
        "b1_3f": a["L3_ffn_b1"].reshape(EXPERTS * FT, P).T, "b2_3f": a["L3_ffn_b2"],
    })
    total = sum(v.shape[1] for v in packed.values())
    resident, spec, at = np.zeros((P, total), np.float32), {"resident": total}, 0
    for n, v in packed.items():
        resident[:v.shape[0], at:at + v.shape[1]] = v
        spec[n] = ("resident", v.shape[0], at, v.shape[1])
        at += v.shape[1]
    patches = a["x"].reshape(IMAGES, 3, 6, 16, 6, 16).transpose(0, 2, 4, 1, 3, 5).reshape(IMAGES, 36, PATCH_K * P)
    padded = np.zeros((IMAGES, SEQ, PATCH_K * P), np.float32)
    padded[:, 2:] = patches
    first = lambda w: np.ascontiguousarray(w.transpose(0, 2, 1).reshape(EXPERTS, KT, KD, HIDDEN).transpose(0, 2, 1, 3))
    second = lambda w: np.ascontiguousarray(w.transpose(0, 2, 1).reshape(EXPERTS, FT, P, DIM).transpose(0, 2, 1, 3))
    swap = lambda w: w.transpose(0, 2, 1)
    wo0 = a["L0_attn_W_o"].reshape(DIM, HEADS, KT, KD).transpose(3, 2, 1, 0)
    arrays = {
        "patches": padded.reshape(TILES, P, PATCH_K, P).transpose(0, 3, 2, 1),
        "w_emb": a["L0_tok_W_emb"].reshape(PATCH_K, P, DIM).transpose(1, 0, 2),
        "select38": np.tile(np.eye(SEQ, dtype=np.float32), (1, IMAGES)),
        "cls_tok": a["cls_tok"].reshape(1, DIM), "cls_token": a["L0_tok_cls_token"].reshape(1, DIM),
        "pos": a["L0_tok_pos_embedding"].reshape(SEQ - 1, DIM), "b_emb": a["L0_tok_b_emb"].reshape(1, DIM),
        "wte": a["L0_attn_wte"],
        "wo0": wo0.reshape(KD, -1),
        "w_int8": np.ascontiguousarray(a["L0_ffn_weight_t"].reshape(KT, KD, DIM).transpose(1, 0, 2).reshape(KD, -1)).view(np.int32),
        "resident": resident,
        "w1_1": first(a["L1_ffn_Wi"]), "w2_1": second(a["L1_ffn_Wo"]),
        "w1_2": first(swap(a["L2_ffn_wi"])), "w2_2": second(swap(a["L2_ffn_wo"])),
        "w1_3f": first(a["L3_ffn_w1"]), "w2_3f": second(a["L3_ffn_w2"]),
    }
    return {n: np.ascontiguousarray(v) for n, v in arrays.items()}, spec


def kernel(**inputs):
    import concourse.bacc as bacc
    from concourse.bass_utils import run_bass_kernel_spmd

    arrays, spec = lay_out(inputs)
    nc = bacc.Bacc("TRN2", target_bir_lowering=False, num_devices=1)
    t_in = {n: nc.dram_tensor(f"in_{n}", v.shape, mybir.dt.from_np(v.dtype), kind="ExternalInput").ap() for n, v in arrays.items()}
    out = nc.dram_tensor("tower_out", (IMAGES, SEQ, DIM), F32, kind="ExternalOutput").ap()
    build(nc, spec, t_in, out)
    r = run_bass_kernel_spmd(nc, [{f"in_{n}": v for n, v in arrays.items()}], core_ids=[0])
    return r.results[0]["tower_out"]
```

```python
from contextlib import ExitStack, contextmanager

import numpy as np

import concourse.bass as bass
from concourse import mybir

F32 = mybir.dt.float32
BF16 = mybir.dt.bfloat16
F32R = mybir.dt.float32r
I8 = mybir.dt.int8
I32 = mybir.dt.int32
ALU = mybir.AluOpType
ACT = mybir.ActivationFunctionType
AX_X = mybir.AxisListType.X
ds = bass.ds

P = 128
IMAGES, SEQ, DIM = 64, 38, 192
TOKENS = IMAGES * SEQ
TILES = TOKENS // P
KT = 2
KD = DIM // KT
GROUPS = 8
GI = IMAGES // GROUPS
GT = GI * SEQ
GPAD = GT + 64
PAIRS = GI // 2
SLOT = 64
HEADS = 12
HPK = HEADS // KT
HD = DIM // HEADS
G3 = 3 * SEQ
PATCH_K = 6
INNER, CI, STATE, RANK = 384, 3, 16, 12
EXPERTS, HIDDEN, FT = 8, 768, 6
CAPACITY = 95
WTE_ROWS = 50257
WTE_R = 4
WTE_CH = WTE_ROWS // P // WTE_R
WTE_TAIL = WTE_ROWS - WTE_CH * WTE_R * P
PARTS, NH3, HD3, KF = 8, 8, 8, 64
EPS = 1e-5
MASKED = -1e30
MAGIC = 12582912.0
TGROUPS = [(s, min(512, TOKENS - s)) for s in range(0, TOKENS, 512)]
CREDITS = 2


class Count:

    def __init__(self, sem, base=0):
        self.sem, self.base = sem, base

    def at(self, base):
        return Count(self.sem, base)

    def done(self, k):
        return self.base + k + 1 + CREDITS

    def freed(self, k):
        return self.base + k + 1


class Chain:

    def __init__(self, eng, sem):
        self.eng, self.sem, self.n, self.reg = eng, sem, 0, 0

    def step(self, ins):
        ins.then_inc(self.sem, 1)
        self.n += 1

    def settle(self):
        self.eng.wait_ge(self.sem, self.reg + self.n)

    @contextmanager
    def loop(self, count, per):
        start, outer = self.n, self.reg
        with self.eng.Fori(0, count) as i:
            self.reg = outer + i * per
            yield i
            assert self.n - start == per, f"{self.n - start} steps in a loop body, not {per}"
        self.reg = outer
        self.n = start + per * count


def ring(eng, n, chain=None, per=0):
    with (chain.loop(n // 2, 2 * per) if chain and per else eng.Fori(0, n // 2)) as i:
        yield 2 * i, 0
        yield 2 * i + 1, 1
    if n % 2:
        yield n - 1, 0
BASES = {
    "L0": (0, (0, 0), (0, 0)),
    "L1": (8, (32, 32), (128, 128)),
    "L3": (16, (64, 64), (160, 160)),
    "L3f": (24, (160, 96), (160, 192)),
}
PJ_BASE = {"L1": 0, "L3": 64, "L3f": 104}
HALVES = [(0, 1), (0, 2), (1, 2)]
QUERY = [0, 1, 1]
TURNING = [False, True, True, True, True, True, True, True, False, True, True]
TURNS = [TILES * sum(TURNING[:i]) for i in range(len(TURNING))]
ARENA, ROUNDED = 17400, 4288
EARLY_LOADS = 6
EXTRA = {"mixed": 4, "h_ready": 4, "y_sum": 20}
PROJ = {"L0": 0, "L0f": 1, "L1": 2, "L2": 3, "L3": 4, "L3f": 5}
SSM_STEPS = 60
STATES = 4
FADE = 0.9
AHEAD = 4
SLOW_FROM = 3


def build(nc, spec, t_in, out):
    with ExitStack() as ctx:
        def sb(name, shape, dt=F32):
            return ctx.enter_context(nc.sbuf_tensor(name, shape, dt))

        def sem(name):
            return ctx.enter_context(nc.semaphore(name))

        h = sb("h", [P, TILES * DIM])
        kept = sb("kept", [P, TILES * DIM])
        xT = sb("xT", [KD, KT, TOKENS])
        zT = sb("zT", [P, CI, TOKENS])
        resident = sb("resident", [P, spec["resident"]])
        normed = sb("normed", [P, 2, DIM])
        ztile = sb("ztile", [P, 2, CI * P])
        stats = sb("stats", [P, TILES * 6])
        mean_var = sb("mean_var", [P, TILES * 2])
        deviation = sb("deviation", [P, TILES])
        rstd = sb("rstd", [P, TILES])
        newton = sb("newton", [P, TILES])
        gates = sb("gates", [P, TILES * EXPERTS])
        wte_sum = sb("wte_sum", [P, WTE_R * DIM])
        avg_wte = sb("avg_wte", [KD, KT])
        w_int8 = sb("w_int8", [KD, KT * DIM // 4], I32)
        arena = sb("arena", [P, ARENA])
        rounded = sb("rounded", [P, ROUNDED])
        bank = ctx.enter_context(nc.psum_tensor("bank", [P, 8, 512], F32))

        def const(name):
            blob, rows, first, cols = spec[name]
            assert blob == "resident"
            return resident[0:rows, first:first + cols]

        class Carve:
            def __init__(self, memory=None):
                self.memory, self.at = arena if memory is None else memory, 0

            def __call__(self, rows, *dims):
                n = int(np.prod(dims))
                view = self.memory[0:rows, self.at:self.at + n]
                self.at += n
                assert self.at <= self.memory.shape[1], self.at
                if len(dims) > 1:
                    names = [f"d{i}" for i in range(len(dims))]
                    view = view.rearrange(f"p ({' '.join(names)}) -> p {' '.join(names)}",
                                          **{n: d for n, d in zip(names[1:], dims[1:])})
                return view

        COUNTS = ("normed_ready turned xT_ready stats_var stats_sd tile_staged proj_sum proj_added rows_ready patch_sum "
                  "patch_taken wte_added prepared pj_sum pj_taken qk_ready kbd_ready scores_ready shifted exped sum_taken "
                  "probs_ready turned_probs probs_in tokens_copied v_sum v_in o_sum o_taken "
                  "wo_sum wo_taken mean_sum mean_in offset_sum h_sum h_ready y_sum y_added "
                  "logit_sum logit_in logit_turned routed exp_in exp_out choice_sum choice_in keep_turned cw_turned cw_in b2_sum b2_added mixed quant "
                  "in_sum in_taken z_gate conv_out conv_gate x_ready low_sum low_in dt_sum dt_gate k2_sum k2_in dx_ready dx_squared dx_sum "
                  "norm_in norm_out w_ready q_split q_sum q_in lists_turned lists_in lists_spread v_expanded a_in scanned weighed reduced").split()
        counts = {n: Count(sem(n)) for n in COUNTS}

        def cnt(name, base=0):
            return counts[name].at(base)

        load_early, load_resident, load_wo = sem("load_early"), sem("load_resident"), sem("load_wo")
        load_tail, stage_ended, stored = sem("load_tail"), sem("stage_ended"), sem("stored")
        patch_loaded = [sem(f"patch_loaded{b}") for b in range(2)]
        wte_loaded = [sem(f"wte_loaded{b}") for b in range(2)]
        expert_loaded = [sem(f"expert_loaded{b}") for b in range(2)]
        chains = {n: sem(f"chain_{n}") for n in ("pe", "dve", "act", "pool")}
        step_apart = sem("step_apart")

        def wait_apart(eng, sem_, value):
            eng.wait_ge(sem_, value)
            eng.sem_inc(step_apart, 1)

        ident = const("ident")
        cols = lambda x, first, n=1: x[:, ds(first, n)]
        tile_h = lambda x, t: x[:, ds(t * DIM, DIM)]

        def ln_dve(dve, ch, i, source, keep=None, turn=True):
            with ch.loop(TILES, 1) as t:
                ch.step(nc.vector.bn_stats(stats[:, ds(6 * t, 6)], tile_h(source, t)))
            ch.settle()
            for t in range(TILES):
                ch.step(nc.vector.bn_aggr(mean_var[:, 2 * t:2 * t + 2], stats[:, 6 * t:6 * t + 6]))
            ch.settle()
            var = mean_var[:, :].rearrange("p (t two) -> p two t", two=2)[:, 1, :]
            nc.vector.tensor_scalar(deviation[:, :], var, EPS, None, ALU.add).then_inc(cnt("stats_var").sem, 1)
            dve.wait_ge(cnt("stats_sd").sem, cnt("stats_sd", i).done(0))
            ch.step(nc.vector.reciprocal(rstd[:, :], newton[:, :]))
            ch.settle()
            ch.step(nc.vector.tensor_tensor(newton[:, :], rstd[:, :], rstd[:, :], ALU.mult))
            ch.settle()
            ch.step(nc.vector.tensor_tensor(newton[:, :], newton[:, :], deviation[:, :], ALU.mult))
            ch.settle()
            ch.step(nc.vector.tensor_scalar(newton[:, :], newton[:, :], -0.5, 1.5, ALU.mult, ALU.add))
            ch.settle()
            ch.step(nc.vector.tensor_tensor(rstd[:, :], rstd[:, :], newton[:, :], ALU.mult))
            ch.settle()
            if keep is not None:
                with ch.loop(TILES, 1) as t:
                    ch.step(nc.vector.tensor_scalar(tile_h(keep, t), tile_h(source, t), cols(mean_var, 2 * t),
                                                    cols(rstd, t), ALU.subtract, ALU.mult))
            if turn:
                ready, turned = cnt("normed_ready", TURNS[i]), cnt("turned", TURNS[i])
                for t, b in ring(dve, TILES):
                    dve.wait_ge(turned.sem, turned.freed(t))
                    nc.vector.tensor_scalar(normed[:, b, :], tile_h(source, t), cols(mean_var, 2 * t),
                                            cols(rstd, t), ALU.subtract, ALU.mult).then_inc(ready.sem, 1)

        def ln_pe(pe, i):
            ready, turned, taken = (cnt(n, TURNS[i]) for n in ("normed_ready", "turned", "xT_ready"))
            for t, b in ring(pe, TILES):
                pe.wait_ge(ready.sem, ready.done(t))
                pe.wait_ge(taken.sem, taken.freed(t))
                for k in range(KT):
                    last = nc.tensor.transpose(bank[0:KD, b, k * P:(k + 1) * P], normed[:, b, k * KD:(k + 1) * KD], ident)
                last.then_inc(turned.sem, 1)

        def ln_act(act, i, turn=True, gain=None, shift=None, scale=1.0):
            var = cnt("stats_var", i)
            act.wait_ge(var.sem, var.done(0))
            nc.scalar.activation(newton[:, :], deviation[:, :], ACT.Sqrt).then_inc(cnt("stats_sd").sem, 1)
            if not turn:
                return
            turned, taken = cnt("turned", TURNS[i]), cnt("xT_ready", TURNS[i])
            for t, b in ring(act, TILES):
                act.wait_ge(turned.sem, turned.done(t))
                if gain is None:
                    nc.scalar.activation(xT[:, :, ds(t * P, P)], bank[0:KD, b, 0:KT * P].rearrange("p (k n) -> p k n", k=KT),
                                         ACT.Copy, scale=scale).then_inc(taken.sem, 1)
                else:
                    for k in range(KT):
                        last = nc.scalar.activation(xT[:, k, ds(t * P, P)], bank[0:KD, b, k * P:(k + 1) * P],
                                                    ACT.Identity, scale=gain[:, k:k + 1],
                                                    bias=shift[:, k:k + 1] if shift is not None else 0.0)
                    last.then_inc(taken.sem, 1)

        def proj_pool(pool, i, z, rows, kt):
            staged, done = cnt("tile_staged", TILES * (i - (i > 1))), cnt("proj_sum", TILES * i)
            for t, b in ring(pool, TILES):
                pool.wait_ge(done.sem, done.freed(t))
                nc.gpsimd.tensor_copy(ztile[0:rows, b, 0:kt * P].rearrange("p (k n) -> p k n", k=kt),
                                      z[0:rows, 0:kt, ds(t * P, P)]).then_inc(staged.sem, 1)

        def proj_pe(pe, i, weight, rows, kt, bias=None):
            staged, done, added = cnt("tile_staged", TILES * (i - (i > 1))), cnt("proj_sum", TILES * i), cnt("proj_added", TILES * i)
            for t, b in ring(pe, TILES):
                pe.wait_ge(staged.sem, staged.done(t))
                pe.wait_ge(added.sem, added.freed(t))
                if bias is not None:
                    nc.tensor.matmul(bank[:, b, 0:DIM], ones_row, bias, start=True, stop=False)
                for k in range(kt):
                    last = nc.tensor.matmul(bank[:, b, 0:DIM], ztile[0:rows, b, k * P:(k + 1) * P], weight[:, k, :],
                                            start=(k == 0 and bias is None), stop=(k == kt - 1))
                last.then_inc(done.sem, 1)

        def turn_pe(pe, i):
            staged, done, added = cnt("tile_staged", TILES * (i - (i > 1))), cnt("proj_sum", TILES * i), cnt("proj_added", TILES * i)
            for t, b in ring(pe, TILES):
                pe.wait_ge(staged.sem, staged.done(t))
                pe.wait_ge(added.sem, added.freed(t))
                for k in range(KT):
                    last = nc.tensor.transpose(bank[:, b, k * KD:(k + 1) * KD], ztile[0:KD, b, k * P:(k + 1) * P],
                                               ident[0:KD, 0:KD])
                last.then_inc(done.sem, 1)

        def proj_dve(dve, i, acc):
            done, added = cnt("proj_sum", TILES * i), cnt("proj_added", TILES * i)
            for t, b in ring(dve, TILES):
                dve.wait_ge(done.sem, done.done(t))
                nc.vector.tensor_tensor(tile_h(acc, t), tile_h(acc, t), bank[:, b, 0:DIM], ALU.add).then_inc(added.sem, 1)

        ones_row = const("ones")[0:1, 0:P]
        ones = const("ones")

        early = Carve()
        w_emb = early(P, PATCH_K, DIM)
        select38 = early(SEQ, TOKENS)
        rows_a, rows_b, rows_sum = early(SEQ, DIM), early(SEQ, DIM), early(SEQ, DIM)
        patch_buf = [early(P, PATCH_K, P) for _ in range(2)]

        def patch_load(sp, t, b):
            summed = cnt("patch_sum")
            sp.wait_ge(summed.sem, summed.freed(t))
            sp.dma_start(patch_buf[b], t_in["patches"][ds(t, 1)].rearrange("a p k n -> (a p) k n")).then_inc(patch_loaded[b], 16)

        def patch_dve(dve, ch):
            ch.step(nc.vector.memset(rows_b[0:1, :], 0.0))
            ch.settle()
            dve.wait_ge(load_early, 16 * EARLY_LOADS)
            nc.vector.tensor_tensor(rows_sum, rows_a, rows_b, ALU.add).then_inc(cnt("rows_ready").sem, 1)
            summed, taken = cnt("patch_sum"), cnt("patch_taken")
            for t, b in ring(dve, TILES):
                dve.wait_ge(summed.sem, summed.done(t))
                nc.vector.tensor_copy(tile_h(h, t), bank[:, b, 0:DIM]).then_inc(taken.sem, 1)

        def patch_pe(pe):
            pe.wait_ge(load_early, 16 * EARLY_LOADS)
            pe.wait_ge(cnt("rows_ready").sem, cnt("rows_ready").done(0))
            summed, taken = cnt("patch_sum"), cnt("patch_taken")

            for t in range(TILES):
                b = t % 2
                pe.wait_ge(patch_loaded[b], 16 * (t // 2 + 1))
                pe.wait_ge(taken.sem, taken.freed(t))
                for k in range(PATCH_K):
                    nc.tensor.matmul(bank[:, b, 0:DIM], patch_buf[b][:, k, :], w_emb[:, k, :], start=(k == 0), stop=False)
                nc.tensor.matmul(bank[:, b, 0:DIM], select38[:, t * P:(t + 1) * P], rows_sum, start=False,
                                 stop=True).then_inc(summed.sem, 1)

        wte_buf = [zT[:, CI - 1, b * WTE_R * DIM:(b + 1) * WTE_R * DIM] for b in range(2)]
        wte_tail = zT[0:WTE_TAIL, CI - 1, 2 * WTE_R * DIM:(2 * WTE_R + 1) * DIM]

        def wte_load(sp, c, b):
            added = cnt("wte_added")
            view = t_in["wte"][0:WTE_ROWS - WTE_TAIL, :].rearrange("(c p r) e -> c p (r e)", p=P, r=WTE_R)
            sp.wait_ge(added.sem, added.freed(c))
            sp.dma_start(wte_buf[b], view[ds(c, 1)].rearrange("a p n -> (a p) n")).then_inc(wte_loaded[b], 16)

        def wte_pool(pool, ch):
            added = cnt("wte_added")
            ch.step(nc.gpsimd.memset(wte_sum[:, :], 0.0))
            ch.settle()
            with pool.Fori(0, WTE_CH // 2) as i:
                for b in range(2):
                    pool.wait_ge(wte_loaded[b], 16 * i + 16)
                    pool.wait_ge(added.sem, 2 * i + b + CREDITS)
                    nc.gpsimd.tensor_tensor(wte_sum[:, :], wte_sum[:, :], wte_buf[b], ALU.add).then_inc(added.sem, 1)
            if WTE_CH % 2:
                pool.wait_ge(wte_loaded[0], 16 * (WTE_CH // 2 + 1))
                pool.wait_ge(added.sem, WTE_CH - 1 + CREDITS)
                nc.gpsimd.tensor_tensor(wte_sum[:, :], wte_sum[:, :], wte_buf[0], ALU.add).then_inc(added.sem, 1)
            pool.wait_ge(added.sem, WTE_CH + CREDITS)
            pool.wait_ge(load_tail, 16)
            ch.step(nc.gpsimd.tensor_tensor(wte_sum[0:WTE_TAIL, 0:DIM], wte_sum[0:WTE_TAIL, 0:DIM], wte_tail, ALU.add))
            ch.settle()
            half = WTE_R // 2
            while half:
                ch.step(nc.gpsimd.tensor_tensor(wte_sum[:, 0:half * DIM], wte_sum[:, 0:half * DIM],
                                                wte_sum[:, half * DIM:2 * half * DIM], ALU.add))
                ch.settle()
                half //= 2

        def soft_shift(ch, psum, work, peak, mask=None):
            src = psum
            if mask is not None:
                ch.step(nc.vector.tensor_tensor(work, psum, mask.unsqueeze(1).broadcast_to(list(work.shape)), ALU.add))
                ch.settle()
                src = work
            ch.step(nc.vector.tensor_reduce(peak, src, AX_X, ALU.max))
            ch.settle()
            return nc.vector.tensor_tensor(work, src, peak.unsqueeze(2).broadcast_to(list(work.shape)), ALU.subtract)

        class Heads16:
            def __init__(self, i, name, rope):
                self.i, self.rope = i, rope
                c = Carve()
                self.q, self.k = c(KD, KT, GPAD), c(KD, KT, GPAD)
                self.rot = [c(KD, GT) for _ in range(2)]
                self.copies = c(KD, KT, GI, 3, SEQ)
                self.kbd = [c(KD, 2, KT, HPK, SEQ) for _ in range(2)]
                self.s = [c(P, HEADS, SEQ) for _ in range(PAIRS)]
                self.p = [c(P, HEADS, SEQ) for _ in range(2)]
                self.peak = [c(P, HEADS) for _ in range(PAIRS)]
                self.total = [c(P, HEADS) for _ in range(PAIRS)]
                self.inverse = [c(P, HEADS) for _ in range(PAIRS)]
                self.pt = [c(G3, 4, P) for _ in range(2)]
                self.vw = [c(G3, 2, 4, KD) for _ in range(PAIRS)]
                self.rotated = c(KD, KT, 2 * DIM) if rope else None
                self.rot_bias = c(KD, 2, KT)
                if rope:
                    self.w, self.bq, self.bk, self.rbq, self.rbk, self.bv = (const(n) for n in ("qkv1", "bq", "bk", "bq_turned", "bk_turned", "bv"))
                else:
                    self.w = const("qkvf")
                self.w = self.w.rearrange("p (k n) -> p k n", k=KT)
                self.per_group = 8 if rope else 4
                self.pj = PJ_BASE[name]
                self.g0, self.u0, self.o0 = BASES[name]

            def outputs(self):
                for dst, off in ((self.q, 0), (self.k, DIM)):
                    for m in range(KT):
                        yield dst, m, self.w[:, :, off + m * KD:off + (m + 1) * KD], False
                        if self.rope:
                            yield dst, m, self.rotated[:, :, off + m * KD:off + (m + 1) * KD], True

            def pool(self, pool, ch):
                for x in (self.q, self.k):
                    ch.step(nc.gpsimd.memset(x[:, :, GT:GPAD], 0.0))
                if self.rope:
                    for off in (0, DIM):
                        for m in range(KT):
                            src = self.w[:, m, off:off + DIM].rearrange("p (h two d) -> p h two d", two=2, d=HD // 2)
                            dst = self.rotated[:, m, off:off + DIM].rearrange("p (h two d) -> p h two d", two=2, d=HD // 2)
                            ch.step(nc.gpsimd.tensor_scalar(dst[:, :, 0, :], src[:, :, 1, :], -1.0, None, ALU.mult))
                            ch.step(nc.gpsimd.tensor_copy(dst[:, :, 1, :], src[:, :, 0, :]))
                    for n, bias in enumerate((self.rbq, self.rbk)):
                        ch.step(nc.gpsimd.tensor_scalar(self.rot_bias[:, n, :], bias, const("rot_sign"), None, ALU.mult))
                ch.settle()
                pool.sem_inc(cnt("prepared").sem, 1)
                qk, kbd, scored = cnt("qk_ready", self.g0 - GROUPS), cnt("kbd_ready", self.u0[1]), cnt("scores_ready", self.u0[0])
                exped, probs, turned = cnt("sum_taken", self.u0[0] - GROUPS * PAIRS), cnt("probs_ready", self.u0[0]), cnt("turned_probs", self.u0[0])
                hmask = const("hmask").unsqueeze(2).broadcast_to([KD, HPK, SEQ])

                def expand(u, p, b):
                    pool.wait_ge(scored.sem, scored.freed(u))
                    for img in range(2):
                        at = (2 * p + img) * SEQ
                        for m in range(KT):
                            last = nc.gpsimd.tensor_tensor(self.kbd[b][:, img, m], self.k[:, m, at:at + SEQ].unsqueeze(1).broadcast_to([KD, HPK, SEQ]), hmask, ALU.mult)
                    last.then_inc(kbd.sem, 1)

                def norm(u, p):
                    pool.wait_ge(exped.sem, exped.done(u))
                    pool.wait_ge(turned.sem, turned.freed(u))
                    nc.gpsimd.tensor_tensor(self.p[p % 2], self.s[p], self.inverse[p].unsqueeze(2).broadcast_to([P, HEADS, SEQ]), ALU.mult).then_inc(probs.sem, 1)

                with pool.Fori(0, GROUPS) as g:
                    pool.wait_ge(qk.sem, qk.done(g))
                    u = g * PAIRS
                    for p in range(3):
                        expand(u + p, p, p % 2)
                    for p in range(PAIRS):
                        norm(u + p, p)
                        if p + 3 < PAIRS:
                            expand(u + p + 3, p + 3, (p + 3) % 2)

            def pe(self, pe):
                pe.wait_ge(cnt("prepared").sem, cnt("prepared", self.i).done(0))
                pj, pj_taken = cnt("pj_sum", self.pj), cnt("pj_taken", self.pj)
                kbd, scored, s_taken = cnt("kbd_ready", self.u0[1]), cnt("scores_ready", self.u0[0]), cnt("shifted", self.u0[0])
                copies, v_sum, v_in = cnt("tokens_copied", self.g0), cnt("v_sum", self.u0[1]), cnt("v_in", self.u0[1])
                probs, turned, p_in = cnt("probs_ready", self.u0[0]), cnt("turned_probs", self.u0[0]), cnt("probs_in", self.u0[0])
                o_sum, o_taken = cnt("o_sum", self.o0[0]), cnt("o_taken", self.o0[1])

                def scores(u, p, b):
                    pe.wait_ge(kbd.sem, kbd.done(u))
                    pe.wait_ge(s_taken.sem, s_taken.freed(u))
                    for img in range(2):
                        at = (2 * p + img) * SEQ
                        for m in range(KT):
                            last = nc.tensor.matmul(bank[img * SLOT:(img + 1) * SLOT, 2 + b, m * HPK * SEQ:(m + 1) * HPK * SEQ],
                                                    self.q[:, m, at:at + SLOT], self.kbd[b][:, img, m].rearrange("p h t -> p (h t)"),
                                                    start=True, stop=True)
                    last.then_inc(scored.sem, 1)

                def values(u, p):
                    pe.wait_ge(v_in.sem, v_in.done(u - 1))
                    for img in range(2):
                        for m in range(KT):
                            last = nc.tensor.matmul(bank[0:G3, 6, img * DIM:(img + 1) * DIM],
                                                    self.copies[:, m, 2 * p + img].rearrange("p c t -> p (c t)"),
                                                    self.w[:, m, 2 * DIM:3 * DIM], start=(m == 0), stop=(m == KT - 1))
                    last.then_inc(v_sum.sem, 1)

                def turn(u, b):
                    pe.wait_ge(probs.sem, probs.done(u))
                    pe.wait_ge(p_in.sem, p_in.freed(u))
                    flat = self.p[b].rearrange("p h t -> p (h t)")
                    for j in range(4):
                        last = nc.tensor.transpose(bank[0:G3, 4 + b, j * P:(j + 1) * P], flat[:, j * G3:(j + 1) * G3], ident)
                    last.then_inc(turned.sem, 1)

                def mix(u, p):
                    b = p % 2
                    pe.wait_ge(p_in.sem, p_in.done(u))
                    pe.wait_ge(v_in.sem, v_in.done(u))
                    pe.wait_ge(o_taken.sem, o_taken.done(u - 1))
                    for m in range(KT):
                        for img in range(2):
                            for j in range(2):
                                last = nc.tensor.matmul(bank[0:KD, 7, (2 * m + img) * SEQ:(2 * m + img + 1) * SEQ],
                                                        self.vw[p][:, img, 2 * m + j, :],
                                                        self.pt[b][:, 2 * m + j, img * SLOT:img * SLOT + SEQ],
                                                        start=(j == 0), stop=(j == 1))
                    last.then_inc(o_sum.sem, 1)

                with pe.Fori(0, GROUPS) as g:
                    for n, (_, m, w, _) in enumerate(self.outputs()):
                        pe.wait_ge(pj_taken.sem, pj_taken.freed(g * self.per_group + n))
                        for kk in range(KT):
                            last = nc.tensor.matmul(bank[0:KD, n % 2, 0:GT], w[:, kk, :], xT[:, kk, ds(g * GT, GT)],
                                                    start=(kk == 0), stop=(kk == KT - 1))
                        last.then_inc(pj.sem, 1)
                    u = g * PAIRS
                    scores(u, 0, 0)
                    scores(u + 1, 1, 1)
                    pe.wait_ge(copies.sem, copies.done(g))
                    values(u, 0)
                    scores(u + 2, 2, 0)
                    for p in range(PAIRS):
                        turn(u + p, p % 2)
                        if p + 3 < PAIRS:
                            scores(u + p + 3, p + 3, (p + 3) % 2)
                        if p + 1 < PAIRS:
                            values(u + p + 1, p + 1)
                        if p:
                            mix(u + p - 1, p - 1)
                    mix(u + PAIRS - 1, PAIRS - 1)

            def dve(self, dve, ch):
                pj, pj_taken = cnt("pj_sum", self.pj), cnt("pj_taken", self.pj)
                qk = cnt("qk_ready", self.g0 - GROUPS)
                scored, shifted = cnt("scores_ready", self.u0[0]), cnt("shifted", self.u0[0])
                exped, summed, probs = cnt("exped", self.u0[0]), cnt("sum_taken", self.u0[0] - GROUPS * PAIRS), cnt("probs_ready", self.u0[0])
                v_sum, v_in, o_sum = cnt("v_sum", self.u0[1]), cnt("v_in", self.u0[1]), cnt("o_sum", self.o0[0])
                cos, sin = (const(n).unsqueeze(1).broadcast_to([KD, GI, SEQ]) for n in ("cos", "sin"))
                mask = const("causal") if self.rope else None
                images = lambda x: x.rearrange("p (i t) -> p i t", t=SEQ)
                dve.wait_ge(cnt("prepared").sem, cnt("prepared", self.i).done(0))

                def part1(u, b):
                    dve.wait_ge(scored.sem, scored.done(u))
                    dve.wait_ge(probs.sem, probs.done(u - PAIRS))
                    psum = bank[:, 2 + b % 2, 0:HEADS * SEQ].rearrange("p (h t) -> p h t", t=SEQ)
                    soft_shift(ch, psum, self.s[b], self.peak[b], mask).then_inc(shifted.sem, 1)

                def value(u, b):
                    dve.wait_ge(v_sum.sem, v_sum.done(u))
                    dve.wait_ge(o_sum.sem, o_sum.done(u - PAIRS))
                    for img in range(2):
                        psum = bank[0:G3, 6, img * DIM:(img + 1) * DIM].rearrange("p (m n) -> p m n", m=KT).unsqueeze(2).broadcast_to([G3, KT, 2, KD])
                        msk = const("vmask").rearrange("p (j n) -> p j n", j=2).unsqueeze(1).broadcast_to([G3, KT, 2, KD])
                        out_ = self.vw[b][:, img].rearrange("p (m j) n -> p m j n", j=2)
                        last = nc.vector.tensor_tensor(out_, psum, msk, ALU.mult)
                    last.then_inc(v_in.sem, 1)

                def part2(u, b):
                    dve.wait_ge(exped.sem, exped.done(u))
                    ch.step(nc.vector.tensor_reduce(self.total[b], self.s[b], AX_X, ALU.add))
                    ch.settle()
                    nc.vector.reciprocal(self.inverse[b], self.total[b]).then_inc(summed.sem, 1)

                with ch.loop(GROUPS, 4 + 3 * PAIRS if self.rope else 2 * PAIRS) as g:
                    for n, (dst, m, _, rotated) in enumerate(self.outputs()):
                        v = g * self.per_group + n
                        dve.wait_ge(pj.sem, pj.done(v))
                        psum = bank[0:KD, n % 2, 0:GT]
                        if not self.rope:
                            nc.vector.tensor_copy(dst[:, m, 0:GT], psum).then_inc(pj_taken.sem, 1)
                            continue
                        bias = {(0, False): self.bq, (0, True): self.rot_bias[:, 0], (1, False): self.bk, (1, True): self.rot_bias[:, 1]}[(0 if dst is self.q else 1, rotated)]
                        if n >= 2:
                            ch.settle()
                        nc.vector.scalar_tensor_tensor(images(self.rot[int(rotated)]), images(psum), bias[:, m:m + 1],
                                                       sin if rotated else cos, ALU.add, ALU.mult).then_inc(pj_taken.sem, 1)
                        if rotated:
                            dve.wait_ge(pj_taken.sem, pj_taken.done(v))
                            ch.step(nc.vector.tensor_tensor(dst[:, m, 0:GT], self.rot[0], self.rot[1], ALU.add))
                    dve.wait_ge(pj_taken.sem, pj_taken.done(g * self.per_group + self.per_group - 1))
                    ch.settle()
                    dve.sem_inc(qk.sem, 1)
                    u = g * PAIRS
                    part1(u, 0)
                    part1(u + 1, 1)
                    value(u, 0)
                    part2(u, 0)
                    part1(u + 2, 2)
                    for p in range(1, PAIRS):
                        part2(u + p, p)
                        if p + 2 < PAIRS:
                            part1(u + p + 2, p + 2)
                        value(u + p, p)

            def act(self, act):
                copies, v_sum = cnt("tokens_copied", self.g0), cnt("v_sum", self.u0[1])
                shifted, exped = cnt("shifted", self.u0[0]), cnt("exped", self.u0[0])
                turned, p_in, o_sum, o_taken = cnt("turned_probs", self.u0[0]), cnt("probs_in", self.u0[0]), cnt("o_sum", self.o0[0]), cnt("o_taken", self.o0[1])

                def exp(u, b):
                    act.wait_ge(shifted.sem, shifted.done(u))
                    nc.scalar.activation(self.s[b], self.s[b], ACT.Exp, scale=HD ** -0.5).then_inc(exped.sem, 1)

                with act.Fori(0, GROUPS) as g:
                    u = g * PAIRS
                    act.wait_ge(v_sum.sem, v_sum.done(u - 1))
                    for m in range(KT):
                        last = nc.scalar.activation(self.copies[:, m], xT[:, m, ds(g * GT, GT)].rearrange("p (i t) -> p i t", t=SEQ).unsqueeze(2).broadcast_to([KD, GI, 3, SEQ]), ACT.Copy)
                    last.then_inc(copies.sem, 1)
                    for p in range(3):
                        exp(u + p, p)
                    for p in range(PAIRS + 1):
                        b = p % 2
                        if p < PAIRS:
                            act.wait_ge(turned.sem, turned.done(u + p))
                            act.wait_ge(o_sum.sem, o_sum.freed(u + p))
                            nc.scalar.activation(self.pt[b].rearrange("p j n -> p (j n)"), bank[0:G3, 4 + b, :], ACT.Copy).then_inc(p_in.sem, 1)
                        if p + 3 < PAIRS:
                            exp(u + p + 3, p + 3)
                        if p == 0:
                            continue
                        act.wait_ge(o_sum.sem, o_sum.done(u + p - 1))
                        for m in range(KT):
                            last = nc.scalar.activation(zT[0:KD, m, ds(g * GT + 2 * (p - 1) * SEQ, 2 * SEQ)],
                                                        bank[0:KD, 7, 2 * m * SEQ:2 * (m + 1) * SEQ], ACT.Identity,
                                                        bias=self.bv[:, m:m + 1] if self.rope else 0.0)
                        last.then_inc(o_taken.sem, 1)

        class Tokens12:
            def __init__(self):
                c = Carve()
                self.wo = c(KD, KT * HEADS, DIM)
                self.a = c(KD, KT, GPAD)
                self.w2 = c(KD, KT, HEADS)
                self.kx = [c(KD, 2, KT, HEADS, SEQ) for _ in range(2)]
                self.s = [c(P, HEADS, SEQ) for _ in range(2)]
                self.p = [c(P, HEADS, SEQ) for _ in range(2)]
                self.peak, self.total, self.inverse = ([c(P, HEADS) for _ in range(2)] for _ in range(3))
                self.pt = [c(SEQ, 2, HEADS, SEQ) for _ in range(2)]
                self.v = [c(SEQ, 2, DIM) for _ in range(2)]
                self.att = [kept[0:KD, :].rearrange("p (m h n) -> p m h n", m=KT, h=HEADS), c(KD, KT, HEADS, 4 * SEQ)]
                self.offset = c(KD, KT)

            def pe(self, pe):
                kx, scored, shifted = cnt("kbd_ready"), cnt("scores_ready"), cnt("shifted")
                copied, v_sum, v_in = cnt("tokens_copied"), cnt("v_sum"), cnt("v_in")
                probs, turned, p_in = cnt("probs_ready"), cnt("turned_probs"), cnt("probs_in")
                o_sum, o_taken, wo_sum, wo_taken = cnt("o_sum"), cnt("o_taken"), cnt("wo_sum"), cnt("wo_taken")

                def scores(u, p, b):
                    pe.wait_ge(kx.sem, kx.done(u))
                    pe.wait_ge(shifted.sem, shifted.done(u - 1))
                    for img in range(2):
                        at = (2 * p + img) * SEQ
                        for m in range(KT):
                            last = nc.tensor.matmul(bank[img * SLOT:(img + 1) * SLOT, 0, 0:HEADS * SEQ], self.a[:, m, at:at + SLOT],
                                                    self.kx[b][:, img, m].rearrange("p h t -> p (h t)"),
                                                    start=(m == 0), stop=(m == KT - 1))
                    last.then_inc(scored.sem, 1)

                def values(u, p):
                    wait_apart(pe, v_in.sem, v_in.done(u - 1))
                    for img in range(2):
                        at = (2 * p + img) * SEQ
                        for m in range(KT):
                            last = nc.tensor.transpose(bank[0:SEQ, 4, img * DIM + m * KD:img * DIM + (m + 1) * KD],
                                                       self.a[:, m, at:at + SEQ], ident[0:KD, 0:KD])
                    last.then_inc(v_sum.sem, 1)

                def turn(u, b):
                    pe.wait_ge(p_in.sem, p_in.done(u - 1))
                    wait_apart(pe, probs.sem, probs.done(u))
                    for hh in range(HEADS):
                        last = nc.tensor.transpose(bank[0:SEQ, 1 + hh // 4, hh % 4 * P:(hh % 4 + 1) * P], self.p[b][:, hh, :], ident)
                    last.then_inc(turned.sem, 1)

                def mix(u, b):
                    pe.wait_ge(p_in.sem, p_in.done(u))
                    pe.wait_ge(v_in.sem, v_in.done(u))
                    for n in range(4):
                        img, m = divmod(n, 2)
                        pe.wait_ge(o_taken.sem, o_taken.freed(4 * u + n))
                        nc.tensor.matmul(bank[0:KD, 5 + n % 2, 0:HEADS * SEQ], self.v[b][:, img, m * KD:(m + 1) * KD],
                                         self.pt[b][:, img].rearrange("p h t -> p (h t)"), start=True, stop=True).then_inc(o_sum.sem, 1)

                def project(g, quad):
                    q = 2 * g + quad
                    pe.wait_ge(o_taken.sem, o_taken.done(4 * PAIRS * g + 8 * quad + 7))
                    pe.wait_ge(wo_taken.sem, wo_taken.done(q - 1))
                    for mt in range(KT):
                        for n in range(KT * HEADS):
                            last = nc.tensor.matmul(bank[0:KD, 7, mt * 4 * SEQ:(mt + 1) * 4 * SEQ], self.wo[:, n, mt * KD:(mt + 1) * KD],
                                                    self.att[quad][:, n // HEADS, n % HEADS, :], start=(n == 0), stop=(n == KT * HEADS - 1))
                    last.then_inc(wo_sum.sem, 1)

                pe.wait_ge(load_wo, 16)
                with pe.Fori(0, GROUPS) as g:
                    u = g * PAIRS
                    pe.wait_ge(copied.sem, copied.done(g))
                    scores(u, 0, 0)
                    values(u, 0)
                    scores(u + 1, 1, 1)
                    for p in range(PAIRS):
                        turn(u + p, p % 2)
                        if p + 2 < PAIRS:
                            scores(u + p + 2, p + 2, p % 2)
                        if p + 1 < PAIRS:
                            values(u + p + 1, p + 1)
                        if p:
                            mix(u + p - 1, (p - 1) % 2)
                    project(g, 0)
                    mix(u + PAIRS - 1, (PAIRS - 1) % 2)
                    project(g, 1)

            def dve(self, dve, ch):
                kx, scored, shifted, exped = cnt("kbd_ready"), cnt("scores_ready"), cnt("shifted"), cnt("exped")
                copied, probs, turned = cnt("tokens_copied"), cnt("probs_ready"), cnt("turned_probs")
                wqk = const("wqk").rearrange("p (k h) -> p k h", k=KT)
                ch.step(nc.vector.tensor_tensor(self.w2, wqk, wqk, ALU.mult))
                ch.settle()

                def expand(u, p, b):
                    dve.wait_ge(scored.sem, scored.freed(u))
                    for img in range(2):
                        at = (2 * p + img) * SEQ
                        shape = [KD, KT, HEADS, SEQ]
                        last = nc.vector.tensor_tensor(self.kx[b][:, img], self.a[:, :, at:at + SEQ].unsqueeze(2).broadcast_to(shape),
                                                       self.w2.unsqueeze(3).broadcast_to(shape), ALU.mult)
                    last.then_inc(kx.sem, 1)

                def part1(u, b):
                    dve.wait_ge(scored.sem, scored.done(u))
                    dve.wait_ge(probs.sem, probs.freed(u))
                    soft_shift(ch, bank[:, 0, 0:HEADS * SEQ].rearrange("p (h t) -> p h t", t=SEQ), self.s[b], self.peak[b],
                               const("causal")).then_inc(shifted.sem, 1)

                def part2(u, b):
                    dve.wait_ge(exped.sem, exped.done(u))
                    ch.step(nc.vector.tensor_reduce(self.total[b], self.s[b], AX_X, ALU.add))
                    ch.settle()
                    ch.step(nc.vector.reciprocal(self.inverse[b], self.total[b]))
                    ch.settle()
                    dve.wait_ge(turned.sem, turned.freed(u))
                    nc.vector.scalar_tensor_tensor(self.p[b], self.s[b], const("nreg_row"), self.inverse[b].unsqueeze(2).broadcast_to([P, HEADS, SEQ]),
                                                   ALU.mult, ALU.mult).then_inc(probs.sem, 1)

                with ch.loop(GROUPS, 4 * PAIRS) as g:
                    u = g * PAIRS
                    dve.wait_ge(copied.sem, copied.done(g))
                    expand(u, 0, 0)
                    expand(u + 1, 1, 1)
                    part1(u, 0)
                    part1(u + 1, 1)
                    part2(u, 0)
                    for p in range(1, PAIRS):
                        if p + 1 < PAIRS:
                            expand(u + p + 1, p + 1, (p + 1) % 2)
                        part2(u + p, p % 2)
                        if p + 1 < PAIRS:
                            part1(u + p + 1, (p + 1) % 2)

            def act(self, act, ch):
                copied, v_sum, v_in, scored = cnt("tokens_copied"), cnt("v_sum"), cnt("v_in"), cnt("scores_ready")
                shifted, exped, turned, p_in = cnt("shifted"), cnt("exped"), cnt("turned_probs"), cnt("probs_in")
                wo_sum, wo_taken, o_sum, o_taken = cnt("wo_sum"), cnt("wo_taken"), cnt("o_sum"), cnt("o_taken")
                ch.step(nc.scalar.activation(self.a[:, :, GT:GPAD], xT[:, :, 0:GPAD - GT], ACT.Copy))
                ch.settle()

                def exp(u, b):
                    act.wait_ge(shifted.sem, shifted.done(u))
                    nc.scalar.activation(self.s[b], self.s[b], ACT.Exp, scale=float(DIM) ** -0.5).then_inc(exped.sem, 1)

                def value(u, b):
                    act.wait_ge(v_sum.sem, v_sum.done(u))
                    nc.scalar.activation(self.v[b], bank[0:SEQ, 4, 0:2 * DIM].rearrange("p (i n) -> p i n", i=2), ACT.Copy).then_inc(v_in.sem, 1)

                def take(u, p, g):
                    if p % 2 == 0:
                        act.wait_ge(wo_sum.sem, wo_sum.freed(2 * g + p // 2))
                    for n in range(4):
                        img, m = divmod(n, 2)
                        at = (2 * (p % 2) + img) * SEQ
                        act.wait_ge(o_sum.sem, o_sum.done(4 * u + n))
                        nc.scalar.activation(self.att[p // 2][:, m, :, at:at + SEQ],
                                             bank[0:KD, 5 + n % 2, 0:HEADS * SEQ].rearrange("p (h t) -> p h t", t=SEQ), ACT.Copy).then_inc(o_taken.sem, 1)

                def output(g, quad):
                    q = 2 * g + quad
                    act.wait_ge(wo_sum.sem, wo_sum.done(q))
                    nc.scalar.activation(zT[0:KD, 0:KT, ds(g * GT + quad * 4 * SEQ, 4 * SEQ)],
                                         bank[0:KD, 7, 0:KT * 4 * SEQ].rearrange("p (m n) -> p m n", m=KT), ACT.Copy).then_inc(wo_taken.sem, 1)

                with act.Fori(0, GROUPS) as g:
                    u = g * PAIRS
                    act.wait_ge(v_sum.sem, v_sum.done(u - 1))
                    act.wait_ge(scored.sem, scored.done(u - 1))
                    nc.scalar.activation(self.a[:, :, 0:GT], xT[:, :, ds(g * GT, GT)], ACT.Copy).then_inc(copied.sem, 1)
                    exp(u, 0)
                    value(u, 0)
                    exp(u + 1, 1)
                    for p in range(PAIRS):
                        b = p % 2
                        act.wait_ge(turned.sem, turned.done(u + p))
                        if p >= 2:
                            act.wait_ge(o_sum.sem, o_sum.done(4 * (u + p) - 5))
                        for img in range(2):
                            last = nc.scalar.activation(self.pt[b][:, img], bank[0:SEQ, 1:4, :].rearrange("p k (h n) -> p (k h) n", n=P)[:, :, img * SLOT:img * SLOT + SEQ], ACT.Copy)
                        last.then_inc(p_in.sem, 1)
                        if p + 2 < PAIRS:
                            exp(u + p + 2, b)
                        if p:
                            take(u + p - 1, p - 1, g)
                        if p + 1 < PAIRS:
                            value(u + p + 1, (p + 1) % 2)
                    output(g, 0)
                    take(u + PAIRS - 1, PAIRS - 1, g)
                    output(g, 1)

            def offset_pe(self, pe):
                for m in range(KT):
                    last = nc.tensor.matmul(bank[0:KD, 0, m:m + 1], wte_sum[:, m * KD:(m + 1) * KD], ones[:, 0:1], start=True, stop=True)
                last.then_inc(cnt("mean_sum").sem, 1)
                pe.wait_ge(cnt("mean_in").sem, cnt("mean_in").done(0))
                for mt in range(KT):
                    for n in range(KT * HEADS):
                        last = nc.tensor.matmul(bank[0:KD, 1, mt:mt + 1], self.wo[:, n, mt * KD:(mt + 1) * KD],
                                                avg_wte[:, n // HEADS:n // HEADS + 1], start=(n == 0), stop=(n == KT * HEADS - 1))
                last.then_inc(cnt("offset_sum").sem, 1)

            def offset_act(self, act):
                act.wait_ge(cnt("mean_sum").sem, cnt("mean_sum").done(0))
                nc.scalar.activation(avg_wte[:, :], bank[0:KD, 0, 0:KT], ACT.Copy, scale=1.0 / WTE_ROWS).then_inc(cnt("mean_in").sem, 1)

            def offset_dve(self, dve, ch):
                dve.wait_ge(cnt("offset_sum").sem, cnt("offset_sum").done(0))
                ch.step(nc.vector.tensor_scalar(self.offset, bank[0:KD, 1, 0:KT], -1.0, None, ALU.mult))
                ch.settle()
                for m in range(KT):
                    z = zT[0:KD, m, :].rearrange("p (i t) -> p i t", t=SEQ)
                    ch.step(nc.vector.scalar_tensor_tensor(z, const("nreg").unsqueeze(1).broadcast_to([KD, IMAGES, SEQ]),
                                                           self.offset[:, m:m + 1], z, ALU.mult, ALU.add))

        class Parts8:
            def __init__(self):
                c = Carve()
                self.qk = c(KF, 5, GPAD)
                self.copies = c(KD, KT, GI, 3, SEQ)
                self.kbd = [c(KF, 2, 3, NH3, SEQ) for _ in range(2)]
                self.s = [c(P, 2, NH3, SEQ) for _ in range(AHEAD)]
                self.p = [c(P, 2, NH3 + 1, SEQ) for _ in range(2)]
                self.peak2, self.total2 = ([c(P, 2, NH3) for _ in range(AHEAD)] for _ in range(2))
                self.peak, self.total, self.inverse = ([c(P, NH3) for _ in range(AHEAD)] for _ in range(3))
                self.pt = [c(G3, 2, 3, P) for _ in range(2)]
                self.vw = [c(G3, 2, 3, 3, KF) for _ in range(2)]
                self.w = const("qkv3").rearrange("p (k n) -> p k n", k=KT)
                (self.g0, (self.w0, self.u0), self.o0), self.pj = BASES["L3"], PJ_BASE["L3"]

            def pool(self, pool, ch):
                ch.step(nc.gpsimd.memset(self.qk[:, :, GT:GPAD], 0.0))
                for b in range(2):
                    ch.step(nc.gpsimd.memset(self.p[b][:, :, NH3, :], 0.0))
                ch.settle()
                pool.sem_inc(cnt("prepared").sem, 1)
                qk, kbd, scored = cnt("qk_ready", self.g0 - GROUPS), cnt("kbd_ready", self.u0), cnt("scores_ready", self.w0)
                probs, turned = (cnt(n, self.w0) for n in ("probs_ready", "turned_probs"))
                summed = cnt("sum_taken", self.w0 - GROUPS * PAIRS)

                def expand(u, p, b):
                    pool.wait_ge(scored.sem, scored.done(3 * u - 4))
                    for img in range(2):
                        at = (2 * p + img) * SEQ
                        shape = [KF, 3, NH3, SEQ]
                        last = nc.gpsimd.tensor_tensor(self.kbd[b][:, img], self.qk[:, 2:5, at:at + SEQ].unsqueeze(2).broadcast_to(shape),
                                                       const("hmask8").unsqueeze(1).unsqueeze(3).broadcast_to(shape), ALU.mult)
                    last.then_inc(kbd.sem, 1)

                with pool.Fori(0, GROUPS) as g:
                    pool.wait_ge(qk.sem, qk.done(g))
                    u = g * PAIRS
                    expand(u, 0, 0)
                    for p in range(PAIRS):
                        if p + 1 < PAIRS:
                            expand(u + p + 1, p + 1, (p + 1) % 2)
                        for j in range(3):
                            w, b, a = 3 * (u + p) + j, (3 * p + j) % 2, (3 * p + j) % AHEAD
                            pool.wait_ge(summed.sem, summed.done(w))
                            pool.wait_ge(turned.sem, turned.freed(w))
                            shape = [P, 2, NH3, SEQ]
                            nc.gpsimd.tensor_tensor(self.p[b][:, :, 0:NH3, :], self.s[a],
                                                    self.inverse[a].unsqueeze(1).unsqueeze(3).broadcast_to(shape), ALU.mult).then_inc(probs.sem, 1)

            def pe(self, pe):
                pe.wait_ge(cnt("prepared").sem, cnt("prepared", 2).done(0))
                pj, pj_taken = cnt("pj_sum", self.pj), cnt("pj_taken", self.pj)
                kbd, v_sum, v_in = (cnt(n, self.u0) for n in ("kbd_ready", "v_sum", "v_in"))
                copied = cnt("tokens_copied", self.g0)
                scored, shifted, probs, turned, p_in = (cnt(n, self.w0) for n in ("scores_ready", "shifted", "probs_ready", "turned_probs", "probs_in"))
                o_taken, mixed = cnt("o_taken", self.o0[1]), cnt("mixed", EXTRA["mixed"])

                def scores(u, n):
                    p, j = divmod(n, 3)
                    b, w = n % 2, 3 * u + n
                    pe.wait_ge(kbd.sem, kbd.done(u + p))
                    wait_apart(pe, shifted.sem, shifted.freed(w))
                    for img in range(2):
                        at = (2 * p + img) * SEQ
                        for half, part in enumerate(HALVES[j]):
                            last = nc.tensor.matmul(bank[img * SLOT:(img + 1) * SLOT, 2 * b + half, 0:NH3 * SEQ], self.qk[:, QUERY[j], at:at + SLOT],
                                                    self.kbd[p % 2][:, img, part].rearrange("p h t -> p (h t)"), start=True, stop=True)
                    last.then_inc(scored.sem, 1)

                def values(u, p):
                    pe.wait_ge(v_in.sem, v_in.done(u - 1))
                    for img in range(2):
                        for m in range(KT):
                            last = nc.tensor.matmul(bank[0:G3, 6, img * DIM:(img + 1) * DIM],
                                                    self.copies[:, m, 2 * p + img].rearrange("p c t -> p (c t)"),
                                                    self.w[:, m, 5 * KF:8 * KF], start=(m == 0), stop=(m == KT - 1))
                    last.then_inc(v_sum.sem, 1)

                def turn(w, b):
                    pe.wait_ge(probs.sem, probs.done(w))
                    pe.wait_ge(p_in.sem, p_in.done(w - 1))
                    for half in range(2):
                        flat = self.p[b][:, half].rearrange("p h t -> p (h t)")
                        for gr in range(3):
                            last = nc.tensor.transpose(bank[0:G3, 4 + half, gr * P:(gr + 1) * P], flat[:, gr * G3:(gr + 1) * G3], ident)
                    last.then_inc(turned.sem, 1)

                def mix(u, p, j, w, b):
                    pe.wait_ge(p_in.sem, p_in.done(w))
                    if j == 0:
                        pe.wait_ge(v_in.sem, v_in.done(u))
                        pe.wait_ge(o_taken.sem, o_taken.done(u - 1))
                    for img in range(2):
                        for half, part in enumerate(HALVES[j]):
                            for gr in range(3):
                                last = nc.tensor.matmul(bank[0:KF, 7, (2 * j + img) * SEQ:(2 * j + img + 1) * SEQ], self.vw[p % 2][:, img, part, gr, :],
                                                        self.pt[b][:, half, gr, img * SLOT:img * SLOT + SEQ],
                                                        start=(half == 0 and gr == 0), stop=(half == 1 and gr == 2))
                    last.then_inc(mixed.sem, 1)

                def mix_unit(u, n):
                    p, j = divmod(n, 3)
                    mix(u + p, p, j, 3 * u + n, n % 2)

                with pe.Fori(0, GROUPS) as g:
                    wait_apart(pe, shifted.sem, shifted.done(3 * PAIRS * g - 1))
                    for n in range(5):
                        if n == 4:
                            wait_apart(pe, pj_taken.sem, pj_taken.done(5 * g))
                        for kk in range(KT):
                            last = nc.tensor.matmul(bank[0:KF, n % 4, 0:GT], self.w[:, kk, n * KF:(n + 1) * KF], xT[:, kk, ds(g * GT, GT)],
                                                    start=(kk == 0), stop=(kk == KT - 1))
                        last.then_inc(pj.sem, 1)
                    u = g * PAIRS
                    scores(u, 0)
                    scores(u, 1)
                    pe.wait_ge(copied.sem, copied.done(g))
                    values(u, 0)
                    scores(u, 2)
                    for n in range(3 * PAIRS):
                        p, j = divmod(n, 3)
                        turn(3 * u + n, n % 2)
                        if n + 3 < 3 * PAIRS:
                            scores(u, n + 3)
                        if n:
                            mix_unit(u, n - 1)
                        if j == 0 and p + 1 < PAIRS:
                            values(u + p + 1, p + 1)
                    mix_unit(u, 3 * PAIRS - 1)

            def dve(self, dve, ch):
                dve.wait_ge(cnt("prepared").sem, cnt("prepared", 2).done(0))
                pj, pj_taken, qk = cnt("pj_sum", self.pj), cnt("pj_taken", self.pj), cnt("qk_ready", self.g0 - GROUPS)
                scored, shifted, exped, probs, p_in = (cnt(n, self.w0) for n in ("scores_ready", "shifted", "exped", "probs_ready", "probs_in"))
                summed = cnt("sum_taken", self.w0 - GROUPS * PAIRS)
                v_sum, v_in, mixed = cnt("v_sum", self.u0), cnt("v_in", self.u0), cnt("mixed", EXTRA["mixed"])

                def part1(w, n):
                    b = n % AHEAD
                    dve.wait_ge(scored.sem, scored.done(w))
                    dve.wait_ge(probs.sem, probs.done(w - AHEAD))
                    psum = bank[:, 2 * (n % 2):2 * (n % 2) + 2, 0:NH3 * SEQ].rearrange("p k (h t) -> p k h t", t=SEQ)
                    ch.step(nc.vector.tensor_reduce(self.peak2[b], psum, AX_X, ALU.max))
                    ch.settle()
                    ch.step(nc.vector.tensor_tensor(self.peak[b], self.peak2[b][:, 0], self.peak2[b][:, 1], ALU.max))
                    ch.settle()
                    nc.vector.tensor_tensor(self.s[b], psum, self.peak[b].unsqueeze(1).unsqueeze(3).broadcast_to([P, 2, NH3, SEQ]),
                                            ALU.subtract).then_inc(shifted.sem, 1)

                def part2(w, n):
                    b = n % AHEAD
                    dve.wait_ge(exped.sem, exped.done(w))
                    ch.step(nc.vector.tensor_reduce(self.total2[b], self.s[b], AX_X, ALU.add))
                    ch.settle()
                    ch.step(nc.vector.tensor_tensor(self.total[b], self.total2[b][:, 0], self.total2[b][:, 1], ALU.add))
                    ch.settle()
                    nc.vector.reciprocal(self.inverse[b], self.total[b]).then_inc(summed.sem, 1)

                def value(u, b):
                    dve.wait_ge(v_sum.sem, v_sum.done(u))
                    dve.wait_ge(mixed.sem, mixed.done(3 * u - 4))
                    for img in range(2):
                        shape = [G3, 3, 3, KF]
                        last = nc.vector.tensor_tensor(self.vw[b][:, img],
                                                       bank[0:G3, 6, img * DIM:(img + 1) * DIM].rearrange("p (v n) -> p v n", v=3).unsqueeze(2).broadcast_to(shape),
                                                       const("vmask8").rearrange("p (g n) -> p g n", g=3).unsqueeze(1).broadcast_to(shape), ALU.mult)
                    last.then_inc(v_in.sem, 1)

                with ch.loop(GROUPS, 4 * 3 * PAIRS) as g:
                    for n in range(5):
                        dve.wait_ge(pj.sem, pj.done(5 * g + n))
                        nc.vector.tensor_copy(self.qk[:, n, 0:GT], bank[0:KF, n % 4, 0:GT]).then_inc(pj_taken.sem, 1)
                    dve.wait_ge(pj_taken.sem, pj_taken.done(5 * g + 4))
                    dve.sem_inc(qk.sem, 1)
                    u = g * PAIRS
                    part1(3 * u, 0)
                    part1(3 * u + 1, 1)
                    value(u, 0)
                    part2(3 * u, 0)
                    part1(3 * u + 2, 2)
                    for n in range(1, 3 * PAIRS):
                        p, j = divmod(n, 3)
                        part2(3 * u + n, n)
                        if n + 2 < 3 * PAIRS:
                            part1(3 * u + n + 2, n + 2)
                        if j == 1 and p + 1 < PAIRS:
                            value(u + p + 1, (p + 1) % 2)

            def act(self, act):
                copied, v_sum = cnt("tokens_copied", self.g0), cnt("v_sum", self.u0)
                shifted, exped, turned, p_in = (cnt(n, self.w0) for n in ("shifted", "exped", "turned_probs", "probs_in"))
                o_taken, mixed = cnt("o_taken", self.o0[1]), cnt("mixed", EXTRA["mixed"])

                def exp(w, n):
                    b = n % AHEAD
                    act.wait_ge(shifted.sem, shifted.done(w))
                    nc.scalar.activation(self.s[b], self.s[b], ACT.Exp, scale=float(3 * HD3) ** -0.5).then_inc(exped.sem, 1)

                with act.Fori(0, GROUPS) as g:
                    u = g * PAIRS
                    act.wait_ge(v_sum.sem, v_sum.done(u - 1))
                    for m in range(KT):
                        last = nc.scalar.activation(self.copies[:, m], xT[:, m, ds(g * GT, GT)].rearrange("p (i t) -> p i t", t=SEQ).unsqueeze(2).broadcast_to([KD, GI, 3, SEQ]), ACT.Copy)
                    last.then_inc(copied.sem, 1)
                    for n in range(3):
                        exp(3 * u + n, n)
                    for n in range(3 * PAIRS + 1):
                        w, b = 3 * u + n, n % 2
                        if n < 3 * PAIRS:
                            act.wait_ge(turned.sem, turned.done(w))
                            act.wait_ge(mixed.sem, mixed.freed(w))
                            nc.scalar.activation(self.pt[b], bank[0:G3, 4:6, 0:3 * P].rearrange("p k (g n) -> p k g n", n=P), ACT.Copy).then_inc(p_in.sem, 1)
                        if n + 3 < 3 * PAIRS:
                            exp(w + 3, n + 3)
                        if n and n % 3 == 0:
                            p = n // 3 - 1
                            act.wait_ge(mixed.sem, mixed.done(w - 1))
                            nc.scalar.activation(zT[0:KF, :, ds(g * GT + 2 * p * SEQ, 2 * SEQ)], bank[0:KF, 7, 0:6 * SEQ].rearrange("p (j n) -> p j n", j=3),
                                                 ACT.Copy).then_inc(o_taken.sem, 1)

        class Experts:

            def __init__(self, r, acc):
                self.r, self.acc = r, acc
                name = ("1", "2", "3f")[r]
                c = Carve()
                self.w1 = [c(KD, KT, HIDDEN) for _ in range(2)]
                self.w2 = [c(P, FT, DIM) for _ in range(2)]
                self.hid = [c(P, FT, 512) for _ in range(2)]
                self.logitsT = c(EXPERTS, TOKENS)
                small = lambda: c(P, TILES, EXPERTS)
                self.lg, self.eq, self.oh1, self.oh2, self.lg2 = (small() for _ in range(5))
                self.m1, self.m2, self.first, self.ex, self.g1, self.g2 = (c(P, TILES) for _ in range(6))
                self.router = const("router" + name).rearrange("p (k e) -> p k e", k=KT)
                self.router_bias = const("gate_b") if r == 2 else None
                self.b1 = const("b1_" + name) if r != 1 else None
                self.b2 = const("b2_" + name) if r != 1 else None
                self.w1_dram, self.w2_dram = t_in["w1_" + name], t_in["w2_" + name]
                self.chosen = zT[0:EXPERTS, 0:2, :]
                self.running = arena[0:EXPERTS, self.hid_at():self.hid_at() + 2 * TOKENS].rearrange("p (k n) -> p k n", k=2)
                self.func = ACT.Relu if r == 1 else ACT.Gelu

            def hid_at(self):
                return 2 * KT * HIDDEN + 2 * FT * DIM

            def load(self, sp, e, b):
                sp.dma_start(self.w1[b], self.w1_dram[ds(e, 1)].rearrange("a p k n -> (a p) k n")).then_inc(expert_loaded[b], 16)
                sp.dma_start(self.w2[b], self.w2_dram[ds(e, 1)].rearrange("a p f n -> (a p) f n")).then_inc(expert_loaded[b], 16)

            def sp_first(self, sp):
                for b in range(2):
                    self.load(sp, b, b)

            def sp_rest(self, sp):
                y_sum = cnt("y_sum", EXTRA["y_sum"] + self.r * EXPERTS * TILES)
                with sp.Fori(1, EXPERTS // 2) as i:
                    for b in range(2):
                        sp.wait_ge(y_sum.sem, y_sum.done((2 * i + b - 1) * TILES - 1))
                        self.load(sp, 2 * i + b, b)

            def route_pe(self, pe):
                r = self.r
                summed, taken = cnt("logit_sum", 5 * r), cnt("logit_in", 5 * r)
                for n, (at, width) in enumerate(TGROUPS):
                    pe.wait_ge(taken.sem, taken.freed(n))
                    for m in range(KT):
                        last = nc.tensor.matmul(bank[0:EXPERTS, n % 2, 0:width], self.router[:, m, :], xT[:, m, at:at + width],
                                                start=(m == 0), stop=(m == KT - 1))
                    last.then_inc(summed.sem, 1)
                pe.wait_ge(taken.sem, taken.done(4))
                for t in range(TILES):
                    last = nc.tensor.transpose(bank[:, 2, t * EXPERTS:(t + 1) * EXPERTS], self.logitsT[:, t * P:(t + 1) * P], ident[0:EXPERTS, 0:EXPERTS])
                last.then_inc(cnt("logit_turned").sem, 1)
                pe.wait_ge(cnt("routed").sem, cnt("routed", r).done(0))
                if r == 1:
                    csum, cin = cnt("choice_sum"), cnt("choice_in")
                    for k, one_hot in enumerate((self.oh1, self.oh2)):
                        for n, (at, width) in enumerate(TGROUPS):
                            v = 5 * k + n
                            pe.wait_ge(cin.sem, cin.freed(v))
                            for t in range(at // P, (at + width) // P):
                                last = nc.tensor.transpose(bank[0:EXPERTS, 4 + v % 2, t * P - at:(t + 1) * P - at], one_hot[:, t, :], ident)
                            last.then_inc(csum.sem, 1)
                    pe.wait_ge(cnt("keep_turned").sem, cnt("keep_turned").done(0))
                    for t in range(TILES):
                        last = nc.tensor.transpose(bank[:, 3, t * EXPERTS:(t + 1) * EXPERTS], self.logitsT[:, t * P:(t + 1) * P], ident[0:EXPERTS, 0:EXPERTS])
                    last.then_inc(cnt("keep_turned").sem, 1)
                    return
                turned, cin = cnt("cw_turned", 5 * (r // 2)), cnt("cw_in", 5 * (r // 2))
                for n, (at, width) in enumerate(TGROUPS):
                    pe.wait_ge(cin.sem, cin.freed(n))
                    for t in range(at // P, (at + width) // P):
                        last = nc.tensor.transpose(bank[0:EXPERTS, 4 + n % 2, t * P - at:(t + 1) * P - at], gates[:, t * EXPERTS:(t + 1) * EXPERTS], ident)
                    last.then_inc(turned.sem, 1)
                pe.wait_ge(cin.sem, cin.done(4))
                b2_sum, b2_added = cnt("b2_sum", TILES * (r // 2)), cnt("b2_added", TILES * (r // 2))
                for t in range(TILES):
                    pe.wait_ge(b2_added.sem, b2_added.freed(t))
                    nc.tensor.matmul(bank[:, 6 + t % 2, 0:DIM], self.logitsT[:, t * P:(t + 1) * P], self.b2, start=True, stop=True).then_inc(b2_sum.sem, 1)

            def route_act(self, act):
                r = self.r
                summed, taken = cnt("logit_sum", 5 * r), cnt("logit_in", 5 * r)
                for n, (at, width) in enumerate(TGROUPS):
                    act.wait_ge(summed.sem, summed.done(n))
                    nc.scalar.activation(self.logitsT[:, at:at + width], bank[0:EXPERTS, n % 2, 0:width], ACT.Identity,
                                         bias=self.router_bias if r == 2 else 0.0).then_inc(taken.sem, 1)
                act.wait_ge(cnt("exp_in").sem, cnt("exp_in", r).done(0))
                x = self.lg if r == 1 else self.ex
                nc.scalar.activation(x, x, ACT.Exp).then_inc(cnt("exp_out").sem, 1)
                if r == 1:
                    csum, cin = cnt("choice_sum"), cnt("choice_in")
                    for k in range(2):
                        for n, (at, width) in enumerate(TGROUPS):
                            v = 5 * k + n
                            act.wait_ge(csum.sem, csum.done(v))
                            nc.scalar.activation(self.chosen[:, k, at:at + width], bank[0:EXPERTS, 4 + v % 2, 0:width], ACT.Copy).then_inc(cin.sem, 1)
                    return
                turned, cin = cnt("cw_turned", 5 * (r // 2)), cnt("cw_in", 5 * (r // 2))
                for n, (at, width) in enumerate(TGROUPS):
                    act.wait_ge(turned.sem, turned.done(n))
                    nc.scalar.activation(self.logitsT[:, at:at + width], bank[0:EXPERTS, 4 + n % 2, 0:width], ACT.Copy).then_inc(cin.sem, 1)

            def route_dve(self, dve, ch):
                r = self.r
                wide = [P, TILES, EXPERTS]
                spread = lambda x: x.unsqueeze(2).broadcast_to(wide)
                order = const("descending").unsqueeze(1).broadcast_to(wide)
                V = nc.vector

                def do(ins):
                    ch.step(ins)
                    ch.settle()

                def choose(values, peak, one_hot):
                    do(V.tensor_reduce(peak, values, AX_X, ALU.max))
                    do(V.tensor_tensor(self.eq, values, spread(peak), ALU.is_equal))
                    do(V.tensor_tensor(self.eq, self.eq, order, ALU.mult))
                    do(V.tensor_reduce(self.first, self.eq, AX_X, ALU.max))
                    do(V.tensor_tensor(one_hot, self.eq, spread(self.first), ALU.is_equal))

                dve.wait_ge(cnt("logit_turned").sem, cnt("logit_turned", r).done(0))
                do(V.tensor_copy(self.lg, bank[:, 2, 0:TILES * EXPERTS].rearrange("p (t e) -> p t e", e=EXPERTS)))
                if r == 1:
                    do(V.tensor_reduce(self.m1, self.lg, AX_X, ALU.max))
                    V.tensor_tensor(self.lg, self.lg, spread(self.m1), ALU.subtract).then_inc(cnt("exp_in").sem, 1)
                    dve.wait_ge(cnt("exp_out").sem, cnt("exp_out", r).done(0))
                    do(V.tensor_reduce(self.m2, self.lg, AX_X, ALU.add))
                    do(V.reciprocal(self.m2, self.m2))
                    do(V.tensor_tensor(self.lg, self.lg, spread(self.m2), ALU.mult))
                choose(self.lg, self.m1, self.oh1)
                do(V.scalar_tensor_tensor(self.lg2, self.oh1, MASKED, self.lg, ALU.mult, ALU.add))
                choose(self.lg2, self.m2, self.oh2)
                if r == 1:
                    g1, g2 = self.m1, self.m2
                else:
                    V.tensor_tensor(self.ex, self.m2, self.m1, ALU.subtract).then_inc(cnt("exp_in").sem, 1)
                    dve.wait_ge(cnt("exp_out").sem, cnt("exp_out", r).done(0))
                    do(V.tensor_scalar(self.g1, self.ex, 1.0, None, ALU.add))
                    do(V.reciprocal(self.g1, self.g1))
                    do(V.tensor_tensor(self.g2, self.ex, self.g1, ALU.mult))
                    g1, g2 = self.g1, self.g2
                gates3 = gates[:, :].rearrange("p (t e) -> p t e", e=EXPERTS)
                do(V.tensor_tensor(gates3, self.oh1, spread(g1), ALU.mult))
                do(V.tensor_tensor(self.eq, self.oh2, spread(g2), ALU.mult))
                do(V.tensor_tensor(gates3, gates3, self.eq, ALU.add))
                dve.sem_inc(cnt("routed").sem, 1)
                if r == 1:
                    dve.wait_ge(cnt("choice_in").sem, cnt("choice_in").done(9))
                    count_on = const("ones")[0:EXPERTS, 0:1].broadcast_to([EXPERTS, GT])
                    for k in range(2):
                        for g in range(GROUPS):
                            start = 0.0 if k == 0 else self.running[:, 0, (g + 1) * GT - 1:(g + 1) * GT]
                            ch.step(V.tensor_tensor_scan(self.running[:, k, g * GT:(g + 1) * GT], count_on,
                                                         self.chosen[:, k, g * GT:(g + 1) * GT], start, ALU.mult, ALU.add))
                        ch.settle()
                    do(V.scalar_tensor_tensor(self.running, self.running, float(CAPACITY), self.chosen, ALU.is_le, ALU.mult))
                    V.tensor_tensor(self.logitsT, self.running[:, 0], self.running[:, 1], ALU.add).then_inc(cnt("keep_turned").sem, 1)
                    dve.wait_ge(cnt("keep_turned").sem, cnt("keep_turned").done(1))
                    do(V.tensor_tensor(gates[:, :], gates[:, :], bank[:, 3, 0:TILES * EXPERTS], ALU.mult))
                    return
                b2_sum, b2_added = cnt("b2_sum", TILES * (r // 2)), cnt("b2_added", TILES * (r // 2))
                for t in range(TILES):
                    dve.wait_ge(b2_sum.sem, b2_sum.done(t))
                    V.tensor_tensor(tile_h(self.acc, t), tile_h(self.acc, t), bank[:, 6 + t % 2, 0:DIM], ALU.add).then_inc(b2_added.sem, 1)

            def pe(self, pe):
                H0, Y0 = self.r * EXPERTS * 5 * FT, self.r * EXPERTS * TILES
                h_sum, h_ready = cnt("h_sum", H0), cnt("h_ready", EXTRA["h_ready"] + H0)
                y_sum, y_added = cnt("y_sum", EXTRA["y_sum"] + Y0), cnt("y_added", Y0)

                def first(e, b, j):
                    at, width = TGROUPS[j]
                    for f in range(FT):
                        n = (5 * FT) * e + FT * j + f
                        pe.wait_ge(h_ready.sem, h_ready.done(n - 4))
                        for m in range(KT):
                            last = nc.tensor.matmul(bank[:, (5 * FT * b + FT * j + f) % 4, 0:width], self.w1[b][:, m, f * P:(f + 1) * P],
                                                    xT[:, m, at:at + width], start=(m == 0), stop=(m == KT - 1))
                        last.then_inc(h_sum.sem, 1)

                def second(e, b, j):
                    at, width = TGROUPS[j]
                    pe.wait_ge(h_ready.sem, h_ready.done((5 * FT) * e + FT * j + FT - 1))
                    for t in range(at // P, (at + width) // P):
                        pe.wait_ge(y_added.sem, y_added.freed(e * TILES + t))
                        for f in range(FT):
                            last = nc.tensor.matmul(bank[:, 4 + (b + t) % 2, 0:DIM], self.hid[(b + j) % 2][:, f, t * P - at:(t + 1) * P - at],
                                                    self.w2[b][:, f, :], start=(f == 0), stop=(f == FT - 1))
                        last.then_inc(y_sum.sem, 1)

                with pe.Fori(0, EXPERTS // 2) as i:
                    for b in range(2):
                        e = 2 * i + b
                        pe.wait_ge(expert_loaded[b], 32 * i + 32 * (1 + self.r * EXPERTS // 2))
                        first(e, b, 0)
                        for j in range(5):
                            if j + 1 < 5:
                                first(e, b, j + 1)
                            second(e, b, j)

            def act(self, act):
                H0, Y0 = self.r * EXPERTS * 5 * FT, self.r * EXPERTS * TILES
                h_sum, h_ready, y_sum = cnt("h_sum", H0), cnt("h_ready", EXTRA["h_ready"] + H0), cnt("y_sum", EXTRA["y_sum"] + Y0)
                for e, b in ring(act, EXPERTS):
                    for j, (at, width) in enumerate(TGROUPS):
                        back, gone = (0, j - 2) if j >= 2 else (1, j + 3)
                        act.wait_ge(y_sum.sem, y_sum.done((e - back) * TILES + sum(TGROUPS[gone]) // P - 1))
                        for f in range(FT):
                            n = 5 * FT * e + FT * j + f
                            wait_apart(act, h_sum.sem, h_sum.done(n))
                            bias = self.b1[:, ds(e * FT + f, 1)] if self.b1 is not None else 0.0
                            nc.scalar.activation(self.hid[(b + j) % 2][:, f, 0:width], bank[:, (5 * FT * b + FT * j + f) % 4, 0:width],
                                                 self.func, bias=bias).then_inc(h_ready.sem, 1)

            def dve(self, dve):
                Y0 = self.r * EXPERTS * TILES
                y_sum, y_added = cnt("y_sum", EXTRA["y_sum"] + Y0), cnt("y_added", Y0)
                for e, b in ring(dve, EXPERTS):
                    for t in range(TILES):
                        n = e * TILES + t
                        dve.wait_ge(y_sum.sem, y_sum.done(n))
                        dve.wait_ge(y_added.sem, y_added.freed(n))
                        nc.vector.scalar_tensor_tensor(tile_h(self.acc, t), bank[:, 4 + (b + t) % 2, 0:DIM], gates[:, ds(e + t * EXPERTS, 1)],
                                                       tile_h(self.acc, t), ALU.mult, ALU.add).then_inc(y_added.sem, 1)

        def quant_dve(dve, ch):
            q = quantised
            half = TOKENS // 2
            for m in range(KT):
                for s in range(2):
                    x = xT[:, m, s * half:(s + 1) * half]
                    ch.step(nc.vector.tensor_scalar(x, x, -128.0, 127.0, ALU.max, ALU.min))
                    ch.settle()
                    ch.step(nc.vector.tensor_scalar(q[:, m, s * half:(s + 1) * half], x, MAGIC, MAGIC, ALU.add, ALU.subtract))
            ch.step(nc.vector.tensor_copy(weight_q, w_int8[:, :].bitcast(I8).rearrange("p (k n) -> p k n", k=KT)))
            ch.settle()
            dve.sem_inc(cnt("quant").sem, 1)
            done, added = cnt("proj_sum", TILES * PROJ["L0f"]), cnt("proj_added", TILES * PROJ["L0f"])
            for t, b in ring(dve, TILES, ch, 1):
                dve.wait_ge(done.sem, done.done(t))
                ch.step(nc.vector.scalar_tensor_tensor(quant_out[b], bank[:, b, 0:DIM], float(np.float32(0.02 * 0.01)), const("bias_int8"), ALU.mult, ALU.add))
                ch.settle()
                nc.vector.tensor_tensor(tile_h(h, t), tile_h(h, t), quant_out[b], ALU.add).then_inc(added.sem, 1)

        def quant_pe(pe):
            pe.wait_ge(cnt("quant").sem, cnt("quant").done(0))
            done, added = cnt("proj_sum", TILES * PROJ["L0f"]), cnt("proj_added", TILES * PROJ["L0f"])
            for t, b in ring(pe, TILES):
                pe.wait_ge(added.sem, added.freed(t))
                for m in range(KT):
                    last = nc.tensor.matmul(bank[:, b, 0:DIM], quantised[:, m, ds(t * P, P)], weight_q[:, m, :], start=(m == 0), stop=(m == KT - 1))
                last.then_inc(done.sem, 1)

        qc = Carve()
        quantised = qc(KD, TOKENS).bitcast(BF16).rearrange("p (k n) -> p k n", k=KT)
        weight_q = qc(KD, DIM).bitcast(BF16).rearrange("p (k n) -> p k n", k=KT)
        quant_out = [qc(P, DIM) for _ in range(2)]

        class StateSpace:
            def __init__(self):
                c = Carve()
                wide = lambda: c(P, CI, GT)
                self.acc, self.sig = wide(), wide()
                self.x2 = self.sig
                quarter = lambda n: kept[:, n * CI * GT:(n + 1) * CI * GT].rearrange("p (c n) -> p c n", c=CI)
                self.x, self.z, self.dt, self.tmp = (quarter(n) for n in range(4))
                self.w3, self.dt3 = c(P, CI, GI, 3, SEQ), c(P, CI, GI, 3, SEQ)
                parts3, single = c(P, GI, 3, SEQ), c(P, GT)
                r = Carve(rounded)
                low_and_q = r(P, GT)
                self.k3, self.kk3 = parts3[0:STATE], parts3[32:32 + STATE]
                self.k, self.k_squared, self.q = single[0:STATE], single[32:32 + STATE], single[64:64 + STATE]
                self.low, self.q_high, self.q_low = c(RANK, GT), low_and_q[64:64 + STATE], low_and_q[96:96 + STATE]
                self.q_parts = low_and_q[64:P]
                self.pick = r(P, STATE)[64:P]
                self.kk = normed[:, :, :].rearrange("p a b -> p (a b)")[:, 0:GT]
                self.n1, self.n2 = (wte_sum[:, n * GT:(n + 1) * GT] for n in range(2))
                spare = ztile[:, :, :].rearrange("p a b -> p (a b)")
                self.n3, self.n4 = (spare[:, n * GT:(n + 1) * GT] for n in range(2))
                at = c.at
                self.qb = c(P, STATE, GT)
                self.xp = arena[:, at:at + CI * GI * (SEQ + 3)].rearrange("p (c i t) -> p c i t", c=CI, t=SEQ + 3)
                self.lists = [r(G3, 2 * CI * P) for _ in range(2)]
                self.keys = [c(G3, 2 * STATE) for _ in range(2)]
                self.spread_k = [r(G3, STATE, SEQ) for _ in range(2)]
                self.spread_kk = [r(G3, STATE, SEQ) for _ in range(2)]
                self.decay = [c(P, STATE * SEQ) for _ in range(2)]
                self.state = [c(P, STATE * SEQ) for _ in range(STATES)]
                self.w_in = const("in_proj").rearrange("p (k n) -> p k n", k=KT)
                self.w_x = const("x_proj").rearrange("p (c n) -> p c n", c=CI)
                self.w_dt = const("dt_head")
                self.conv_w = const("conv_w").rearrange("p (c j) -> p c j", c=CI)
                self.conv_b, self.dt_b, self.d = const("conv_b"), const("dt_b"), const("d")

            def pool(self, pool, ch):
                for b in range(2):
                    ch.step(nc.gpsimd.memset(self.decay[b], 0.0))
                ch.settle()
                ch.step(nc.gpsimd.tensor_scalar(self.q_parts.bitcast(F32R), ident[64:P, 0:1].broadcast_to([64, GT]), 0.0, None, ALU.mult))
                ch.settle()
                ch.step(nc.gpsimd.tensor_tensor(self.pick.bitcast(F32R), ident[64:P, 64:64 + STATE], ident[64:P, 96:96 + STATE], ALU.add))
                ch.settle()
                pool.sem_inc(cnt("prepared").sem, 1)
                lists_in, spread = cnt("lists_in"), cnt("lists_spread")
                scanned, weighed, q_in, expanded = cnt("scanned"), cnt("weighed"), cnt("q_in"), cnt("v_expanded")
                shape = [G3, STATE, SEQ]

                def build(image, b):
                    pool.wait_ge(lists_in.sem, lists_in.done(image))
                    for n, (x, mask) in enumerate(((self.spread_k, "upto"), (self.spread_kk, "own"))):
                        nc.gpsimd.tensor_tensor(x[b].bitcast(F32R), self.keys[b][:, n * STATE:(n + 1) * STATE].unsqueeze(2).broadcast_to(shape),
                                                const(mask).unsqueeze(1).broadcast_to(shape), ALU.mult).then_inc(spread.sem, 1)

                with pool.Fori(0, GROUPS) as g:
                    first = g * GI
                    build(first, 0)
                    pool.wait_ge(q_in.sem, q_in.done(STATE * g + STATE - 1))
                    for img in range(GI):
                        for c in range(CI):
                            n = CI * img + c
                            v = CI * first + n
                            if c == 1 and img + 1 < GI:
                                build(first + img + 1, (img + 1) % 2)
                            pool.wait_ge(scanned.sem, scanned.done(v))
                            st = self.state[n % STATES].rearrange("p (n t) -> p n t", t=SEQ)
                            nc.gpsimd.tensor_tensor(st, st, self.qb[:, :, img * SEQ:(img + 1) * SEQ], ALU.mult).then_inc(weighed.sem, 1)

            def pe(self, pe):
                pe.wait_ge(cnt("prepared").sem, cnt("prepared", 1).done(0))
                C = {n: cnt(n) for n in COUNTS}
                wait = lambda n, k: pe.wait_ge(C[n].sem, C[n].done(k))
                freed = lambda n, k: pe.wait_ge(C[n].sem, C[n].freed(k))
                inc = lambda ins, n: ins.then_inc(C[n].sem, 1)
                flat = lambda x: x.rearrange("p a b -> p (a b)")

                def turn(image, img):
                    wait("lists_in", image - 1)
                    three = lambda x: x.rearrange("p a b -> p (a b)")
                    for c in range(CI):
                        nc.tensor.transpose(bank[0:G3, 6, c * P:(c + 1) * P], three(self.w3[:, c, img]), ident)
                    for c in range(CI):
                        nc.tensor.transpose(bank[0:G3, 7, c * P:(c + 1) * P], three(self.dt3[:, c, img]), ident)
                    nc.tensor.transpose(bank[0:G3, 6, CI * P:CI * P + STATE], three(self.k3[:, img]), ident[0:STATE, 0:STATE])
                    last = nc.tensor.transpose(bank[0:G3, 7, CI * P:CI * P + STATE], three(self.kk3[:, img]), ident[32:32 + STATE, 32:32 + STATE])
                    inc(last, "lists_turned")

                with pe.Fori(0, GROUPS) as g:
                    first = g * GI
                    wait("reduced", 6 * PAIRS * g - 1)
                    wait("a_in", 12 * PAIRS * g - 1)
                    for m in range(6):
                        freed("in_taken", 6 * g + m)
                        for kk in range(KT):
                            last = nc.tensor.matmul(bank[:, m % 2, 0:GT], self.w_in[:, kk, m * P:(m + 1) * P], xT[:, kk, ds(g * GT, GT)],
                                                    start=(kk == 0), stop=(kk == KT - 1))
                        inc(last, "in_sum")
                    wait("x_ready", g)
                    for j, (at, rows) in enumerate(((0, RANK), (RANK, STATE), (RANK + STATE, STATE))):
                        for c in range(CI):
                            last = nc.tensor.matmul(bank[0:rows, 2 + j, 0:GT], self.w_x[:, c, at:at + rows], self.x[:, c, :],
                                                    start=(c == 0), stop=(c == CI - 1))
                    inc(last, "low_sum")
                    wait("low_in", g)
                    wait("q_in", STATE * g - 1)
                    for c in range(CI):
                        last = nc.tensor.matmul(bank[:, 5 + c, 0:GT], self.w_dt[:, c * P:(c + 1) * P], self.low, start=True, stop=True)
                    inc(last, "dt_sum")
                    wait("in_taken", 6 * g + 5)
                    inc(nc.tensor.matmul(bank[:, 0, 0:GT], ones[32:32 + STATE, 0:P], self.k_squared, start=True, stop=True), "k2_sum")
                    wait("dt_gate", g)
                    wait("q_split", g)
                    for n in range(STATE):
                        freed("q_in", STATE * g + n)
                        inc(nc.tensor.matmul(bank[:, 6 + n % 2, 0:GT], self.pick[:, n:n + 1].broadcast_to([2 * 32, P]).bitcast(F32R), self.q_parts.bitcast(F32R), start=True, stop=True), "q_sum")
                    wait("dx_squared", g)
                    for c in range(CI):
                        last = nc.tensor.matmul(bank[:, 1, 0:GT], ones[:, 0:P], self.tmp[:, c, :], start=(c == 0), stop=(c == CI - 1))
                    inc(last, "dx_sum")
                    wait("w_ready", g)
                    wait("q_in", STATE * g + STATE - 1)
                    turn(first, 0)
                    for img in range(GI):
                        b = img % 2
                        wait("lists_spread", 2 * (first + img) + 1)
                        for c in range(CI):
                            n = CI * img + c
                            v = CI * first + n
                            wait("scanned", v - 2)
                            for half in range(2):
                                nc.tensor.matmul(bank[:, 2 * (n % 2) + half, 0:GT], self.lists[b][:, c * P:(c + 1) * P].bitcast(F32R),
                                                 flat(self.spread_k[b])[:, half * GT:(half + 1) * GT].bitcast(F32R), start=True, stop=True)
                            for half in range(2):
                                wait("a_in", 2 * v - 2 + half)
                                last = nc.tensor.matmul(bank[:, 4 + half, 0:GT], self.lists[b][:, (CI + c) * P:(CI + c + 1) * P].bitcast(F32R),
                                                        flat(self.spread_kk[b])[:, half * GT:(half + 1) * GT].bitcast(F32R), start=True, stop=True)
                                inc(last, "v_expanded")
                            if c == 0 and img + 1 < GI:
                                turn(first + img + 1, img + 1)

            def act(self, act):
                act.wait_ge(cnt("prepared").sem, cnt("prepared", 1).done(0))
                C = {n: cnt(n) for n in COUNTS}
                wait = lambda n, k: act.wait_ge(C[n].sem, C[n].done(k))
                inc = lambda ins, n: ins.then_inc(C[n].sem, 1)
                A = nc.scalar.activation
                images = lambda x: x.rearrange("p (i t) -> p i t", t=SEQ)

                def lists(image, b):
                    wait("lists_turned", image)
                    n = CI * P
                    A(self.lists[b].bitcast(F32R).rearrange("p (k n) -> p k n", k=2), bank[0:G3, 6:8, 0:n], ACT.Copy)
                    inc(A(self.keys[b].rearrange("p (k n) -> p k n", k=2), bank[0:G3, 6:8, n:n + STATE], ACT.Copy), "lists_in")

                with act.Fori(0, GROUPS) as g:
                    first = g * GI
                    for m in range(6):
                        wait("in_sum", 6 * g + m)
                        psum = bank[:, m % 2, 0:GT]
                        if m < CI:
                            inc(A(self.xp[:, m, :, 3:], images(psum), ACT.Copy), "in_taken")
                        else:
                            inc(A(self.sig[:, m - CI, :], psum, ACT.Sigmoid), "z_gate")
                    wait("conv_out", g)
                    inc(A(self.sig, self.acc, ACT.Sigmoid), "conv_gate")
                    wait("low_sum", g)
                    A(self.low, bank[0:RANK, 2, 0:GT], ACT.Copy)
                    A(self.k, bank[0:STATE, 3, 0:GT], ACT.Copy)
                    A(self.k_squared, bank[0:STATE, 3, 0:GT], ACT.Square)
                    inc(A(self.q, bank[0:STATE, 4, 0:GT], ACT.Copy), "low_in")
                    wait("dt_sum", g)
                    for c in range(CI):
                        last = A(self.dt[:, c, :], bank[:, 5 + c, 0:GT], ACT.Sigmoid, bias=self.dt_b[:, c:c + 1])
                    inc(last, "dt_gate")
                    wait("k2_sum", g)
                    inc(A(self.kk, bank[:, 0, 0:GT], ACT.Copy), "k2_in")
                    for n in range(STATE):
                        wait("q_sum", STATE * g + n)
                        if n == 0:
                            wait("weighed", 6 * PAIRS * g - 1)
                        inc(A(self.qb[:, n, :], bank[:, 6 + n % 2, 0:GT], ACT.Copy), "q_in")
                    wait("dx_ready", g)
                    inc(A(self.tmp, self.x2, ACT.Square), "dx_squared")
                    wait("norm_in", g)
                    inc(A(self.n2, self.n1, ACT.Sqrt), "norm_out")
                    lists(first, 0)
                    for img in range(GI):
                        for c in range(CI):
                            n = CI * img + c
                            v = CI * first + n
                            for half in range(2):
                                wait("v_expanded", 2 * v + half)
                                if half == 0:
                                    wait("scanned", v - 2)
                                inc(A(self.decay[n % 2].rearrange("p (k n t) -> p k n t", k=2, t=SEQ)[:, half, :, 1:],
                                      bank[:, 4 + half, 0:GT].rearrange("p (n t) -> p n t", t=SEQ)[:, :, 1:],
                                      ACT.Copy, scale=-1.0 / FADE, bias=1.0 / FADE), "a_in")
                            if c == 0 and img + 1 < GI:
                                lists(first + img + 1, (img + 1) % 2)

            def dve(self, dve, ch):
                dve.wait_ge(cnt("prepared").sem, cnt("prepared", 1).done(0))
                C = {n: cnt(n) for n in COUNTS}
                wait = lambda n, k: dve.wait_ge(C[n].sem, C[n].done(k))
                inc = lambda ins, n: ins.then_inc(C[n].sem, 1)
                V = nc.vector
                images = lambda x: x.rearrange("p (i t) -> p i t", t=SEQ)

                def do(ins):
                    ch.step(ins)
                    ch.settle()

                all_c = lambda x: x.unsqueeze(1).broadcast_to([P, CI, GT])
                def split(parts, x):
                    for dst, k in parts:
                        if k == "high":
                            ch.step(V.tensor_copy(dst.bitcast(F32R), x))
                            high = dst
                    ch.settle()
                    for dst, k in parts:
                        if k == "low":
                            ch.step(V.tensor_tensor(dst.bitcast(F32R), x, high, ALU.subtract))

                values = lambda x: [(x[:, :, 0], "high"), (x[:, :, 1], "high"), (x[:, :, 2], "low")]
                keys = lambda x: [(x[:, :, 0], "high"), (x[:, :, 1], "low"), (x[:, :, 2], "high")]

                with ch.loop(GROUPS, SSM_STEPS) as g:
                    first = g * GI
                    for c in range(CI):
                        ch.step(V.memset(self.xp[:, c, :, 0:3], 0.0))
                    for m in range(CI, 6):
                        wait("z_gate", CI * g + m - CI)
                        inc(V.tensor_tensor(self.z[:, m - CI, :], bank[:, m % 2, 0:GT], self.sig[:, m - CI, :], ALU.mult), "in_taken")
                    wait("in_taken", 6 * g + 5)
                    for j in range(4):
                        for c in range(CI):
                            src, acc, w = self.xp[:, c, :, j:j + SEQ], images(self.acc[:, c, :]), self.conv_w[:, c, j:j + 1]
                            if j == 0:
                                ch.step(V.tensor_scalar(acc, src, w, self.conv_b[:, c:c + 1], ALU.mult, ALU.add))
                            else:
                                ch.step(V.scalar_tensor_tensor(acc, src, w, acc, ALU.mult, ALU.add))
                        ch.settle()
                    dve.sem_inc(C["conv_out"].sem, 1)
                    wait("conv_gate", g)
                    inc(V.tensor_tensor(self.x, self.acc, self.sig, ALU.mult), "x_ready")
                    wait("low_in", g)
                    split(keys(self.k3), images(self.k))
                    split(keys(self.kk3), images(self.k_squared))
                    do(V.tensor_tensor(images(self.q), images(self.q), const("fall")[64:64 + STATE].unsqueeze(1).broadcast_to([STATE, GI, SEQ]), ALU.mult))
                    split([(self.q_high, "high"), (self.q_low, "low")], self.q)
                    ch.settle()
                    dve.sem_inc(C["q_split"].sem, 1)
                    wait("dt_gate", g)
                    wait("k2_in", g)
                    do(V.tensor_tensor(self.tmp, self.dt, all_c(self.kk), ALU.mult))
                    do(V.tensor_scalar(self.tmp, self.tmp, 1.0, None, ALU.add))
                    do(V.reciprocal(self.tmp, self.tmp))
                    do(V.tensor_tensor(self.dt, self.dt, self.tmp, ALU.mult))
                    do(V.tensor_tensor(self.x2, self.dt, self.x, ALU.mult))
                    dve.sem_inc(C["dx_ready"].sem, 1)
                    for c in range(CI):
                        split(values(self.dt3[:, c]), images(self.dt[:, c, :]))
                    wait("dx_sum", g)
                    inc(V.tensor_tensor(self.n1, bank[:, 1, 0:GT], self.kk, ALU.mult), "norm_in")
                    wait("norm_out", g)
                    do(V.tensor_scalar(self.n3, self.n2, 1e-7, None, ALU.add))
                    do(V.reciprocal(self.n3, self.n3))
                    do(V.tensor_tensor(self.n2, self.n2, self.n3, ALU.mult))
                    do(V.tensor_tensor(self.n2, self.n2, self.n2, ALU.mult))
                    do(V.tensor_scalar(self.n4, self.n2, 2.0315, -4.775, ALU.mult, ALU.add))
                    do(V.tensor_tensor(self.n4, self.n4, self.n2, ALU.mult))
                    do(V.scalar_tensor_tensor(self.n4, self.n4, 3.4445, self.n3, ALU.add, ALU.mult))
                    do(V.tensor_tensor(images(self.n4), images(self.n4), const("rise").unsqueeze(1).broadcast_to([P, GI, SEQ]), ALU.mult))
                    do(V.tensor_tensor(self.x2, self.x2, all_c(self.n4), ALU.mult))
                    for c in range(CI):
                        split(values(self.w3[:, c]), images(self.x2[:, c, :]))
                    ch.settle()
                    dve.sem_inc(C["w_ready"].sem, 1)

                    def reduce(v, n):
                        img, c = divmod(n, CI)
                        wait("weighed", v)
                        inc(V.tensor_reduce(self.acc[:, c, img * SEQ:(img + 1) * SEQ], self.state[n % STATES].rearrange("p (n t) -> p t n", t=SEQ), AX_X, ALU.add), "reduced")

                    for n in range(CI * GI):
                        v, b = CI * first + n, n % 2
                        wait("a_in", 2 * v + 1)
                        if n >= STATES:
                            wait("reduced", v - STATES)
                        for half in range(2):
                            last = V.tensor_tensor_scan(self.state[n % STATES][:, half * GT:(half + 1) * GT], self.decay[b][:, half * GT:(half + 1) * GT],
                                                        bank[:, 2 * b + half, 0:GT], 0.0, ALU.mult, ALU.add)
                        inc(last, "scanned")
                        if n >= 2:
                            reduce(v - 2, n - 2)
                    for n in (CI * GI - 2, CI * GI - 1):
                        reduce(CI * first + n, n)
                    wait("reduced", CI * first + CI * GI - 1)
                    for c in range(CI):
                        ch.step(V.scalar_tensor_tensor(self.acc[:, c, :], self.x[:, c, :], self.d[:, c:c + 1], self.acc[:, c, :], ALU.mult, ALU.add))
                    ch.settle()
                    do(V.tensor_tensor(zT[:, :, ds(g * GT, GT)], self.acc, self.z, ALU.mult))

        layer0, layer1, layer2, layer3 = Tokens12(), Heads16(0, "L1", True), StateSpace(), Parts8()
        layer3f = Heads16(3, "L3f", False)
        experts = [Experts(0, h), Experts(1, h), Experts(2, kept)]
        bias_of = lambda n: const(n)
        weight_of = lambda n, kt: const(n).rearrange("p (k n) -> p k n", k=kt)
        credit_share = {e: COUNTS[i::4] for i, e in enumerate(("sp", "act", "pe", "dve"))}

        def credits(eng, name):
            for n in credit_share[name]:
                eng.sem_inc(counts[n].sem, CREDITS + EXTRA.get(n, 0))

        slow_ended = sem("slow_ended")

        class Stages:

            def __init__(self, eng, slow=False):
                self.eng, self.k, self.slow = eng, 0, slow

            def end(self):
                own, k = (slow_ended if self.slow else stage_ended), self.k
                self.eng.drain().then_inc(own, 1)
                self.eng.wait_ge(stage_ended, 3 * (k + 1))
                if k == 0 or k >= SLOW_FROM:
                    self.eng.wait_ge(slow_ended, 2 if k == 0 else 2 * (k - SLOW_FROM + 2))
                self.k = SLOW_FROM if self.slow and k == 0 else k + 1

            def skip(self, n):
                for _ in range(n):
                    self.end()

        block = ctx.enter_context(nc.Block())

        @block.sync
        def _(sp):
            stage = Stages(sp, slow=True)
            credits(sp, "sp")
            sp.dma_start(w_emb, t_in["w_emb"]).then_inc(load_early, 16)
            sp.dma_start(select38, t_in["select38"]).then_inc(load_early, 16)
            sp.dma_start(rows_a[0:1, :], t_in["cls_tok"]).then_inc(load_early, 16)
            sp.dma_start(rows_a[1:SEQ, :], t_in["pos"]).then_inc(load_early, 16)
            sp.dma_start(rows_b[1:2, :], t_in["cls_token"]).then_inc(load_early, 16)
            sp.dma_start(rows_b[2:SEQ, :], t_in["b_emb"].broadcast_to([SEQ - 2, DIM])).then_inc(load_early, 16)
            stage.end()
            sp.dma_start(wte_tail, t_in["wte"][WTE_ROWS - WTE_TAIL:WTE_ROWS, :]).then_inc(load_tail, 16)
            with sp.Fori(0, TILES // 2) as i:
                for b in range(2):
                    patch_load(sp, 2 * i + b, b)
                    wte_load(sp, 2 * i + b, b)
            patch_load(sp, TILES - 1, 0)
            sp.dma_start(resident[:, :], t_in["resident"]).then_inc(load_resident, 16)
            sp.dma_start(w_int8[:, :], t_in["w_int8"]).then_inc(load_resident, 16)
            sp.wait_ge(cnt("patch_taken").sem, cnt("patch_taken").done(TILES - 1))
            sp.dma_start(layer0.wo.rearrange("p n e -> p (n e)"), t_in["wo0"]).then_inc(load_wo, 16)
            with sp.Fori(TILES // 2, WTE_CH // 2) as i:
                for b in range(2):
                    wte_load(sp, 2 * i + b, b)
            stage.skip(11 - SLOW_FROM)
            experts[0].sp_first(sp)
            stage.skip(2)
            experts[0].sp_rest(sp)
            stage.skip(4)
            experts[1].sp_first(sp)
            stage.skip(2)
            experts[1].sp_rest(sp)
            stage.skip(7)
            experts[2].sp_first(sp)
            stage.skip(2)
            experts[2].sp_rest(sp)
            stage.skip(2)
            sp.dma_start(out.rearrange("i s e -> (i s) e").rearrange("(t p) e -> p t e", p=P),
                         h[:, :].rearrange("p (t e) -> p t e", e=DIM)).then_inc(stored, 16)
            sp.wait_ge(stored, 16)

        @block.gpsimd
        def _(pool):
            ch = Chain(pool, chains["pool"])
            stage = Stages(pool, slow=True)
            stage.end()
            wte_pool(pool, ch)
            stage.skip(2)
            proj_pool(pool, PROJ["L0"], zT, KD, KT)
            stage.skip(4)
            layer1.pool(pool, ch)
            stage.end()
            proj_pool(pool, PROJ["L1"], zT, KD, KT)
            stage.skip(5)
            layer2.pool(pool, ch)
            stage.end()
            proj_pool(pool, PROJ["L2"], zT, P, CI)
            stage.skip(5)
            layer3.pool(pool, ch)
            stage.end()
            proj_pool(pool, PROJ["L3"], zT, KF, 3)
            stage.skip(2)
            layer3f.pool(pool, ch)
            stage.end()
            proj_pool(pool, PROJ["L3f"], zT, KD, KT)
            stage.skip(5)

        @block.scalar
        def _(act):
            ch = Chain(act, chains["act"])
            stage = Stages(act)
            credits(act, "act")
            stage.skip(2)
            act.wait_ge(load_resident, 32)
            ln_act(act, 0, turn=False)
            ln_act(act, 1, gain=const("ln_w"))
            stage.end()
            layer0.act(act, ch)
            stage.end()
            layer0.offset_act(act)
            stage.skip(2)
            ln_act(act, 2, scale=50.0)
            stage.skip(2)
            ln_act(act, 3)
            stage.end()
            layer1.act(act)
            stage.skip(2)
            ln_act(act, 4)
            stage.end()
            experts[0].route_act(act)
            stage.end()
            experts[0].act(act)
            stage.end()
            ln_act(act, 5)
            stage.end()
            layer2.act(act)
            stage.skip(2)
            ln_act(act, 6)
            stage.end()
            experts[1].route_act(act)
            stage.end()
            experts[1].act(act)
            stage.end()
            ln_act(act, 7)
            stage.end()
            layer3.act(act)
            stage.skip(2)
            ln_act(act, 8, turn=False)
            ln_act(act, 9, gain=const("ln1_g"), shift=const("ln1_b"))
            stage.end()
            layer3f.act(act)
            stage.skip(2)
            ln_act(act, 10, gain=const("ln2_g"), shift=const("ln2_b"))
            stage.end()
            experts[2].route_act(act)
            stage.end()
            experts[2].act(act)
            stage.skip(2)

        @block.tensor
        def _(pe):
            stage = Stages(pe)
            credits(pe, "pe")
            stage.end()
            patch_pe(pe)
            stage.end()
            pe.wait_ge(load_resident, 32)
            ln_pe(pe, 1)
            stage.end()
            layer0.pe(pe)
            stage.end()
            layer0.offset_pe(pe)
            stage.end()
            turn_pe(pe, PROJ["L0"])
            stage.end()
            ln_pe(pe, 2)
            stage.end()
            quant_pe(pe)
            stage.end()
            ln_pe(pe, 3)
            stage.end()
            layer1.pe(pe)
            stage.end()
            proj_pe(pe, PROJ["L1"], weight_of("wo1", KT), KD, KT, bias_of("bo1"))
            stage.end()
            ln_pe(pe, 4)
            stage.end()
            experts[0].route_pe(pe)
            stage.end()
            experts[0].pe(pe)
            stage.end()
            ln_pe(pe, 5)
            stage.end()
            layer2.pe(pe)
            stage.end()
            proj_pe(pe, PROJ["L2"], weight_of("out_proj", CI), P, CI)
            stage.end()
            ln_pe(pe, 6)
            stage.end()
            experts[1].route_pe(pe)
            stage.end()
            experts[1].pe(pe)
            stage.end()
            ln_pe(pe, 7)
            stage.end()
            layer3.pe(pe)
            stage.end()
            proj_pe(pe, PROJ["L3"], weight_of("wo3", 3), KF, 3, bias_of("bo3"))
            stage.end()
            ln_pe(pe, 9)
            stage.end()
            layer3f.pe(pe)
            stage.end()
            proj_pe(pe, PROJ["L3f"], weight_of("wof", KT), KD, KT, bias_of("bof"))
            stage.end()
            ln_pe(pe, 10)
            stage.end()
            experts[2].route_pe(pe)
            stage.end()
            experts[2].pe(pe)
            stage.skip(2)

        @block.vector
        def _(dve):
            ch = Chain(dve, chains["dve"])
            stage = Stages(dve)
            credits(dve, "dve")
            stage.end()
            patch_dve(dve, ch)
            stage.end()
            dve.wait_ge(load_resident, 32)
            ln_dve(dve, ch, 0, h, keep=kept, turn=False)
            ch.settle()
            ln_dve(dve, ch, 1, kept)
            stage.end()
            layer0.dve(dve, ch)
            stage.end()
            layer0.offset_dve(dve, ch)
            stage.end()
            proj_dve(dve, PROJ["L0"], h)
            stage.end()
            ln_dve(dve, ch, 2, h)
            stage.end()
            quant_dve(dve, ch)
            stage.end()
            ln_dve(dve, ch, 3, h)
            stage.end()
            layer1.dve(dve, ch)
            stage.end()
            proj_dve(dve, PROJ["L1"], h)
            stage.end()
            ln_dve(dve, ch, 4, h)
            stage.end()
            experts[0].route_dve(dve, ch)
            stage.end()
            experts[0].dve(dve)
            stage.end()
            ln_dve(dve, ch, 5, h)
            stage.end()
            layer2.dve(dve, ch)
            stage.end()
            proj_dve(dve, PROJ["L2"], h)
            stage.end()
            ln_dve(dve, ch, 6, h)
            stage.end()
            experts[1].route_dve(dve, ch)
            stage.end()
            experts[1].dve(dve)
            stage.end()
            ln_dve(dve, ch, 7, h)
            stage.end()
            layer3.dve(dve, ch)
            stage.end()
            proj_dve(dve, PROJ["L3"], h)
            stage.end()
            ln_dve(dve, ch, 8, h, keep=kept, turn=False)
            ch.settle()
            ln_dve(dve, ch, 9, kept)
            stage.end()
            layer3f.dve(dve, ch)
            stage.end()
            proj_dve(dve, PROJ["L3f"], kept)
            stage.end()
            ln_dve(dve, ch, 10, kept)
            stage.end()
            experts[2].route_dve(dve, ch)
            stage.end()
            experts[2].dve(dve)
            stage.end()
            nc.vector.tensor_tensor(h[:, :], h[:, :], kept[:, :], ALU.add)
            stage.end()


def k_major(w, kt):
    w = np.asarray(w).T
    return w.reshape(kt, w.shape[0] // kt, w.shape[1]).transpose(1, 0, 2).reshape(w.shape[0] // kt, -1)


def by_feature(v, kt):
    v = np.asarray(v)
    return v.reshape(kt, -1).T


def constants():
    f = np.float32
    c = {"ident": np.eye(P, dtype=f), "ones": np.ones((P, P), f)}
    s, t = np.arange(P)[:, None] % SLOT, np.arange(SEQ)[None, :]
    c["causal"] = np.where((s < SEQ) & (t > s), f(MASKED), f(0)).astype(f)
    c["nreg"] = np.broadcast_to((f(1) / np.arange(1, SEQ + 1, dtype=f))[None], (KD, SEQ))
    c["nreg_row"] = np.where(s < SEQ, f(1) / (s + 1).astype(f), f(0)).astype(f)
    inv = f(1) / f(10000.0) ** (np.arange(0, HD, 2, dtype=f) / f(HD))
    ang = np.arange(SEQ, dtype=f)[None, :] * inv[:, None]
    c["cos"], c["sin"] = (np.tile(np.concatenate([fn(ang)] * 2, 0), (HPK, 1)).astype(f) for fn in (np.cos, np.sin))
    c["hmask"] = (np.arange(KD)[:, None] // HD == np.arange(HPK)[None]).astype(f)
    c["hmask8"] = (np.arange(KF)[:, None] // HD3 == np.arange(NH3)[None]).astype(f)
    row = np.arange(G3)[:, None, None] // SEQ
    c["vmask"] = (np.arange(KD)[None, None] // HD == 3 * np.arange(2)[None, :, None] + row).astype(f).reshape(G3, -1)
    c["vmask8"] = (np.arange(KF)[None, None] // HD3 == 3 * np.arange(3)[None, :, None] + row).astype(f).reshape(G3, -1)
    third, when = np.arange(G3)[:, None] % SEQ, np.arange(SEQ)
    c["upto"], c["own"] = (third <= t).astype(f), (third == t).astype(f)
    c["rise"] = np.broadcast_to((FADE ** -when.astype(np.float64)).astype(f)[None], (P, SEQ))
    c["fall"] = np.broadcast_to((FADE ** when.astype(np.float64)).astype(f)[None], (P, SEQ))
    c["descending"] = np.broadcast_to(np.arange(EXPERTS, 0, -1, dtype=f)[None], (P, EXPERTS))
    c["rot_sign"] = np.where(np.arange(KD) % HD < HD // 2, f(-1), f(1)).astype(f)[:, None]
    return c


def lay_out(i):
    a = {n: np.asarray(v) for n, v in i.items()}
    rot = np.arange(DIM).reshape(HEADS, 2, HD // 2)[:, ::-1].reshape(-1)
    parts = [w * DIM + np.arange(NH3)[:, None] * 24 + s * HD3 + np.arange(HD3)[None] for w, s in
             ((0, 1), (0, 2), (1, 0), (1, 1), (1, 2), (2, 0), (2, 1), (2, 2))]
    parts = np.concatenate([x.reshape(-1) for x in parts])
    packed = constants()
    packed.update({
        "wqk": k_major(a["L0_attn_W_qk"], KT),
        "ln_w": by_feature(a["L0_attn_ln_w"], KT),
        "bias_int8": np.broadcast_to(a["L0_ffn_bias"][None], (P, DIM)),
        "qkv1": k_major(np.concatenate([a["L1_attn_Wq"], a["L1_attn_Wk"], a["L1_attn_Wv"]], 0), KT),
        "bq": by_feature(a["L1_attn_bq"], KT), "bk": by_feature(a["L1_attn_bk"], KT), "bv": by_feature(a["L1_attn_bv"], KT),
        "bq_turned": by_feature(a["L1_attn_bq"][rot], KT), "bk_turned": by_feature(a["L1_attn_bk"][rot], KT),
        "wo1": k_major(a["L1_attn_Wo"], KT), "bo1": a["L1_attn_bo"][None],
        "router1": k_major(a["L1_ffn_Wr"], KT), "b2_1": a["L1_ffn_bo"],
        "b1_1": a["L1_ffn_bi"].reshape(EXPERTS * FT, P).T,
        "in_proj": k_major(a["L2_attn_in_proj_w"], KT), "x_proj": k_major(a["L2_attn_x_proj_w"], CI),
        "dt_head": a["L2_attn_dt_head_w"].T, "dt_b": by_feature(a["L2_attn_dt_head_b"], CI),
        "conv_w": a["L2_attn_conv_w"].reshape(CI, P, 4).transpose(1, 0, 2).reshape(P, -1),
        "conv_b": by_feature(a["L2_attn_conv_b"], CI), "d": by_feature(a["L2_attn_D"], CI),
        "out_proj": k_major(a["L2_attn_out_proj_w"], CI),
        "router2": k_major(a["L2_ffn_w_router"].T, KT),
        "qkv3": k_major(a["L3_attn_w_qkv"][parts], KT), "wo3": k_major(a["L3_attn_w_proj"], 3), "bo3": a["L3_attn_b_proj"][None],
        "qkvf": k_major(a["L3_ffn_qkv_w"], KT), "wof": k_major(a["L3_ffn_proj_w"], KT), "bof": a["L3_ffn_proj_b"][None],
        "ln1_g": by_feature(a["L3_ffn_ln1_g"], KT), "ln1_b": by_feature(a["L3_ffn_ln1_b"], KT),
        "ln2_g": by_feature(a["L3_ffn_ln2_g"], KT), "ln2_b": by_feature(a["L3_ffn_ln2_b"], KT),
        "router3f": k_major(a["L3_ffn_gate_w"], KT), "gate_b": a["L3_ffn_gate_b"][:, None],
        "b1_3f": a["L3_ffn_b1"].reshape(EXPERTS * FT, P).T, "b2_3f": a["L3_ffn_b2"],
    })
    total = sum(v.shape[1] for v in packed.values())
    resident, spec, at = np.zeros((P, total), np.float32), {"resident": total}, 0
    for n, v in packed.items():
        resident[:v.shape[0], at:at + v.shape[1]] = v
        spec[n] = ("resident", v.shape[0], at, v.shape[1])
        at += v.shape[1]
    patches = a["x"].reshape(IMAGES, 3, 6, 16, 6, 16).transpose(0, 2, 4, 1, 3, 5).reshape(IMAGES, 36, PATCH_K * P)
    padded = np.zeros((IMAGES, SEQ, PATCH_K * P), np.float32)
    padded[:, 2:] = patches
    first = lambda w: np.ascontiguousarray(w.transpose(0, 2, 1).reshape(EXPERTS, KT, KD, HIDDEN).transpose(0, 2, 1, 3))
    second = lambda w: np.ascontiguousarray(w.transpose(0, 2, 1).reshape(EXPERTS, FT, P, DIM).transpose(0, 2, 1, 3))
    swap = lambda w: w.transpose(0, 2, 1)
    wo0 = a["L0_attn_W_o"].reshape(DIM, HEADS, KT, KD).transpose(3, 2, 1, 0)
    arrays = {
        "patches": padded.reshape(TILES, P, PATCH_K, P).transpose(0, 3, 2, 1),
        "w_emb": a["L0_tok_W_emb"].reshape(PATCH_K, P, DIM).transpose(1, 0, 2),
        "select38": np.tile(np.eye(SEQ, dtype=np.float32), (1, IMAGES)),
        "cls_tok": a["cls_tok"].reshape(1, DIM), "cls_token": a["L0_tok_cls_token"].reshape(1, DIM),
        "pos": a["L0_tok_pos_embedding"].reshape(SEQ - 1, DIM), "b_emb": a["L0_tok_b_emb"].reshape(1, DIM),
        "wte": a["L0_attn_wte"],
        "wo0": wo0.reshape(KD, -1),
        "w_int8": np.ascontiguousarray(a["L0_ffn_weight_t"].reshape(KT, KD, DIM).transpose(1, 0, 2).reshape(KD, -1)).view(np.int32),
        "resident": resident,
        "w1_1": first(a["L1_ffn_Wi"]), "w2_1": second(a["L1_ffn_Wo"]),
        "w1_2": first(swap(a["L2_ffn_wi"])), "w2_2": second(swap(a["L2_ffn_wo"])),
        "w1_3f": first(a["L3_ffn_w1"]), "w2_3f": second(a["L3_ffn_w2"]),
    }
    return {n: np.ascontiguousarray(v) for n, v in arrays.items()}, spec


def kernel(**inputs):
    import concourse.bacc as bacc
    from concourse.bass_utils import run_bass_kernel_spmd

    arrays, spec = lay_out(inputs)
    nc = bacc.Bacc("TRN2", target_bir_lowering=False, num_devices=1)
    t_in = {n: nc.dram_tensor(f"in_{n}", v.shape, mybir.dt.from_np(v.dtype), kind="ExternalInput").ap() for n, v in arrays.items()}
    out = nc.dram_tensor("tower_out", (IMAGES, SEQ, DIM), F32, kind="ExternalOutput").ap()
    build(nc, spec, t_in, out)
    r = run_bass_kernel_spmd(nc, [{f"in_{n}": v for n, v in arrays.items()}], core_ids=[0])
    return r.results[0]["tower_out"]
```

```python
from contextlib import ExitStack, contextmanager

import numpy as np

import concourse.bass as bass
from concourse import mybir

F32 = mybir.dt.float32
BF16 = mybir.dt.bfloat16
F32R = mybir.dt.float32r
I8 = mybir.dt.int8
I32 = mybir.dt.int32
ALU = mybir.AluOpType
ACT = mybir.ActivationFunctionType
AX_X = mybir.AxisListType.X
ds = bass.ds

P = 128
IMAGES, SEQ, DIM = 64, 38, 192
TOKENS = IMAGES * SEQ
TILES = TOKENS // P
TPAIRS = (TILES + 1) // 2
BANKS = 8
KT = 2
KD = DIM // KT
GROUPS = 8
GI = IMAGES // GROUPS
GT = GI * SEQ
GPAD = GT + 64
PAIRS = GI // 2
SLOT = 64
HEADS = 12
HPK = HEADS // KT
HD = DIM // HEADS
G3 = 3 * SEQ
PATCH_K = 6
INNER, CI, STATE, RANK = 384, 3, 16, 12
EXPERTS, HIDDEN, FT = 8, 768, 6
CAPACITY = 95
WTE_ROWS = 50257
WTE_R = 4
WTE_CH = WTE_ROWS // P // WTE_R
WTE_TAIL = WTE_ROWS - WTE_CH * WTE_R * P
NH3, HD3, KF = 8, 8, 64
EPS = 1e-5
MASKED = -1e30
MAGIC = 12582912.0
TGROUPS = [(s, min(512, TOKENS - s)) for s in range(0, TOKENS, 512)]
CREDITS = 2


class Count:

    def __init__(self, sem, base=0):
        self.sem, self.base = sem, base

    def at(self, base):
        return Count(self.sem, base)

    def done(self, k):
        return self.base + k + 1 + CREDITS

    def freed(self, k):
        return self.base + k + 1


class Chain:

    def __init__(self, eng, sem):
        self.eng, self.sem, self.n, self.reg = eng, sem, 0, 0

    def step(self, ins):
        ins.then_inc(self.sem, 1)
        self.n += 1

    def settle(self):
        self.eng.wait_ge(self.sem, self.reg + self.n)

    @contextmanager
    def loop(self, count, per):
        start, outer = self.n, self.reg
        with self.eng.Fori(0, count) as i:
            self.reg = outer + i * per
            yield i
            assert self.n - start == per, f"{self.n - start} steps in a loop body, not {per}"
        self.reg = outer
        self.n = start + per * count


def ring(eng, n, chain=None, per=0):
    with (chain.loop(n // 2, 2 * per) if chain and per else eng.Fori(0, n // 2)) as i:
        yield 2 * i, 0
        yield 2 * i + 1, 1
    if n % 2:
        yield n - 1, 0
def groups(eng, group, chain=None, per=0):
    with (chain.loop(GROUPS - 1, per) if chain else eng.Fori(0, GROUPS - 1)) as g:
        group(g, True)
    group(GROUPS - 1, False)


BASES = {
    "L0": (0, (0, 0), (0, 0)),
    "L1": (8, (32, 32), (128, 128)),
    "L3": (16, (64, 64), (160, 160)),
    "L3f": (24, (160, 96), (160, 192)),
}
PJ_BASE = {"L1": 0, "L3": 64, "L3f": 104}
HALVES = [(0, 1), (0, 2), (1, 2)]
QUERY = [0, 1, 1]
PJ_BANK = [0, 1, 2, 3, 6]
TURNING = [False, True, True, True, True, True, True, True, False, True, True]
TURNS = [sum(TURNING[:i]) for i in range(len(TURNING))]
ARENA, ROUNDED = 17400, 4288
EARLY_LOADS = 6
EXTRA = {"mixed": 4, "h_ready": 4, "y_sum": 20}
PROJ = {"L0": 0, "L0f": 1, "L1": 2, "L2": 3, "L3": 4, "L3f": 5}
SSM_STEPS = 60
IN_BANK = [0, 1, 0, 3, 4, 2]
STATES = 4
XP_AT, XP_COLS = (32, 0, 64), 64 + STATE
FADE = 0.9
AHEAD = 4
SLOW_FROM = 3


def build(nc, spec, t_in, out):
    with ExitStack() as ctx:
        def sb(name, shape, dt=F32):
            return ctx.enter_context(nc.sbuf_tensor(name, shape, dt))

        def sem(name):
            return ctx.enter_context(nc.semaphore(name))

        h = sb("h", [P, TILES * DIM])
        kept = sb("kept", [P, TILES * DIM])
        xT = sb("xT", [KD, KT, TOKENS])
        zT = sb("zT", [P, CI, TOKENS])
        resident = sb("resident", [P, spec["resident"]])
        normed = sb("normed", [P, 2, DIM])
        ztile = sb("ztile", [P, 2, CI * P])
        stats = sb("stats", [P, TILES * 6])
        mean_var = sb("mean_var", [P, TILES * 2])
        deviation = sb("deviation", [P, TILES])
        rstd = sb("rstd", [P, TILES])
        newton = sb("newton", [P, TILES])
        gates = sb("gates", [P, TILES * EXPERTS])
        wte_sum = sb("wte_sum", [P, WTE_R * DIM])
        avg_wte = sb("avg_wte", [KD, KT])
        w_int8 = sb("w_int8", [KD, KT * DIM // 4], I32)
        arena = sb("arena", [P, ARENA])
        rounded = sb("rounded", [P, ROUNDED])
        bank = ctx.enter_context(nc.psum_tensor("bank", [P, 8, 512], F32))

        def const(name):
            blob, rows, first, cols = spec[name]
            assert blob == "resident"
            return resident[0:rows, first:first + cols]

        class Carve:
            def __init__(self, memory=None):
                self.memory, self.at = arena if memory is None else memory, 0

            def __call__(self, rows, *dims):
                n = int(np.prod(dims))
                view = self.memory[0:rows, self.at:self.at + n]
                self.at += n
                assert self.at <= self.memory.shape[1], self.at
                if len(dims) > 1:
                    names = [f"d{i}" for i in range(len(dims))]
                    view = view.rearrange(f"p ({' '.join(names)}) -> p {' '.join(names)}",
                                          **{n: d for n, d in zip(names[1:], dims[1:])})
                return view

        COUNTS = ("normed_ready turned xT_ready stats_var stats_sd proj_sum proj_added rows_ready patch_sum "
                  "patch_taken wte_added prepared pj_sum pj_taken qk_ready kbd_ready scores_ready shifted exped sum_taken "
                  "probs_ready turned_probs probs_in tokens_copied tokens_split v_sum v_in o_sum o_taken "
                  "wo_sum wo_taken mean_sum mean_in offset_sum h_sum h_ready y_sum y_added "
                  "logit_sum logit_in logit_turned routed exp_in exp_out choice_sum choice_in keep_turned cw_turned cw_in b2_sum b2_added mixed quant "
                  "in_sum in_taken z_gate conv_out conv_gate x_ready low_sum low_in dt_sum dt_gate k2_sum k2_in dx_ready dx_squared dx_sum "
                  "norm_in norm_out w_ready q_split q_sum q_in lists_turned lists_in lists_spread squares_spread v_expanded a_in scanned weighed reduced").split()
        counts = {n: Count(sem(n)) for n in COUNTS}

        def cnt(name, base=0):
            return counts[name].at(base)

        load_early, load_resident, load_wo = sem("load_early"), sem("load_resident"), sem("load_wo")
        load_tail, stage_ended, stored = sem("load_tail"), sem("stage_ended"), sem("stored")
        patch_loaded = [sem(f"patch_loaded{b}") for b in range(2)]
        wte_loaded = [sem(f"wte_loaded{b}") for b in range(2)]
        expert_loaded = [sem(f"expert_loaded{b}") for b in range(2)]
        chains = {n: sem(f"chain_{n}") for n in ("pe", "dve", "act", "pool")}
        step_apart = sem("step_apart")

        def wait_apart(eng, sem_, value):
            eng.wait_ge(sem_, value)
            eng.sem_inc(step_apart, 1)

        ident = const("ident")
        tile_h = lambda x, t: x[:, t * DIM:(t + 1) * DIM] if isinstance(t, int) else x[:, ds(t * DIM, DIM)]
        staged = arena[:, ARENA - TILES * DIM:ARENA]

        def ln_dve(dve, ch, i, source, keep=None, turn=True):
            for t in range(TILES):
                ch.step(nc.vector.bn_stats(stats[:, 6 * t:6 * t + 6], tile_h(source, t)))
            ch.settle()
            for t in range(TILES):
                ch.step(nc.vector.bn_aggr(mean_var[:, 2 * t:2 * t + 2], stats[:, 6 * t:6 * t + 6]))
            ch.settle()
            var = mean_var[:, :].rearrange("p (t two) -> p two t", two=2)[:, 1, :]
            nc.vector.tensor_scalar(deviation[:, :], var, EPS, None, ALU.add).then_inc(cnt("stats_var").sem, 1)
            dve.wait_ge(cnt("stats_sd").sem, cnt("stats_sd", i).done(0))
            ch.step(nc.vector.reciprocal(rstd[:, :], newton[:, :]))
            ch.settle()
            ch.step(nc.vector.tensor_tensor(newton[:, :], rstd[:, :], rstd[:, :], ALU.mult))
            ch.settle()
            ch.step(nc.vector.tensor_tensor(newton[:, :], newton[:, :], deviation[:, :], ALU.mult))
            ch.settle()
            ch.step(nc.vector.tensor_scalar(newton[:, :], newton[:, :], -0.5, 1.5, ALU.mult, ALU.add))
            ch.settle()
            ch.step(nc.vector.tensor_tensor(rstd[:, :], rstd[:, :], newton[:, :], ALU.mult))
            ch.settle()
            normalise = lambda out_, t: nc.vector.tensor_scalar(out_, tile_h(source, t), mean_var[:, 2 * t:2 * t + 1],
                                                                rstd[:, t:t + 1], ALU.subtract, ALU.mult)
            if keep is not None:
                for t in range(TILES):
                    ch.step(normalise(tile_h(keep, t), t))
            if turn:
                for t in range(TILES):
                    normalise(tile_h(staged, t), t).then_inc(cnt("normed_ready").sem, 1)

        def ln_pe(pe, i):
            ready, turned, taken = cnt("normed_ready", TURNS[i] * TILES), cnt("turned", TURNS[i] * TPAIRS), cnt("xT_ready", TURNS[i] * TPAIRS)
            for j in range(TPAIRS):
                tiles = range(2 * j, min(2 * j + 2, TILES))
                if j >= BANKS:
                    pe.wait_ge(taken.sem, taken.done(j - BANKS))
                for t in tiles:
                    pe.wait_ge(ready.sem, ready.done(t))
                    for k in range(KT):
                        last = nc.tensor.transpose(bank[0:KD, j % BANKS, (2 * k + t % 2) * P:(2 * k + t % 2 + 1) * P],
                                                   staged[:, t * DIM + k * KD:t * DIM + (k + 1) * KD], ident)
                last.then_inc(turned.sem, 1)

        def ln_act(act, i, turn=True, gain=None, shift=None, scale=1.0):
            var = cnt("stats_var", i)
            act.wait_ge(var.sem, var.done(0))
            nc.scalar.activation(newton[:, :], deviation[:, :], ACT.Sqrt).then_inc(cnt("stats_sd").sem, 1)
            if not turn:
                return
            turned, taken = cnt("turned", TURNS[i] * TPAIRS), cnt("xT_ready", TURNS[i] * TPAIRS)
            for j in range(TPAIRS):
                n = min(2, TILES - 2 * j) * P
                psum = bank[0:KD, j % BANKS, :].rearrange("p (k n) -> p k n", k=KT)[:, :, 0:n]
                act.wait_ge(turned.sem, turned.done(j))
                if gain is None:
                    last = nc.scalar.activation(xT[:, :, 2 * j * P:2 * j * P + n], psum, ACT.Copy, scale=scale)
                else:
                    for k in range(KT):
                        last = nc.scalar.activation(xT[:, k, 2 * j * P:2 * j * P + n], psum[:, k], ACT.Identity, scale=gain[:, k:k + 1],
                                                    bias=shift[:, k:k + 1] if shift is not None else 0.0)
                last.then_inc(taken.sem, 1)

        def proj_pe(pe, i, weight, rows, kt, bias=False):
            done, added = cnt("proj_sum", TILES * i), cnt("proj_added", TILES * i)
            for t in range(TILES):
                if t >= BANKS:
                    pe.wait_ge(added.sem, added.done(t - BANKS))
                for k in range(kt):
                    n = rows + (bias and k == 0)
                    last = nc.tensor.matmul(bank[:, t % BANKS, 0:DIM], zT[0:n, k, t * P:(t + 1) * P], weight[0:n, k, :],
                                            start=(k == 0), stop=(k == kt - 1))
                last.then_inc(done.sem, 1)

        def turn_pe(pe, i):
            done, added = cnt("proj_sum", TILES * i), cnt("proj_added", TILES * i)
            for t in range(TILES):
                if t >= BANKS:
                    pe.wait_ge(added.sem, added.done(t - BANKS))
                for k in range(KT):
                    last = nc.tensor.transpose(bank[:, t % BANKS, k * KD:(k + 1) * KD], zT[0:KD, k, t * P:(t + 1) * P],
                                               ident[0:KD, 0:KD])
                last.then_inc(done.sem, 1)

        def proj_dve(dve, i, acc):
            done, added = cnt("proj_sum", TILES * i), cnt("proj_added", TILES * i)
            for t in range(TILES):
                dve.wait_ge(done.sem, done.done(t))
                nc.vector.tensor_tensor(tile_h(acc, t), tile_h(acc, t), bank[:, t % BANKS, 0:DIM], ALU.add).then_inc(added.sem, 1)

        ones = const("ones")

        early = Carve()
        w_emb = early(P, PATCH_K, DIM)
        select38 = early(SEQ, TOKENS)
        rows_a, rows_b, rows_sum = early(SEQ, DIM), early(SEQ, DIM), early(SEQ, DIM)
        patch_buf = [early(P, PATCH_K, P) for _ in range(2)]

        def patch_load(sp, t, b):
            summed = cnt("patch_sum")
            sp.wait_ge(summed.sem, summed.freed(t))
            sp.dma_start(patch_buf[b], t_in["patches"][ds(t, 1)].rearrange("a p k n -> (a p) k n")).then_inc(patch_loaded[b], 16)

        def patch_dve(dve, ch):
            ch.step(nc.vector.memset(rows_b[0:1, :], 0.0))
            ch.settle()
            dve.wait_ge(load_early, 16 * EARLY_LOADS)
            nc.vector.tensor_tensor(rows_sum, rows_a, rows_b, ALU.add).then_inc(cnt("rows_ready").sem, 1)
            summed, taken = cnt("patch_sum"), cnt("patch_taken")
            for t, b in ring(dve, TILES):
                dve.wait_ge(summed.sem, summed.done(t))
                nc.vector.tensor_copy(tile_h(h, t), bank[:, b, 0:DIM]).then_inc(taken.sem, 1)

        def patch_pe(pe):
            pe.wait_ge(load_early, 16 * EARLY_LOADS)
            pe.wait_ge(cnt("rows_ready").sem, cnt("rows_ready").done(0))
            summed, taken = cnt("patch_sum"), cnt("patch_taken")

            for t in range(TILES):
                b = t % 2
                pe.wait_ge(patch_loaded[b], 16 * (t // 2 + 1))
                pe.wait_ge(taken.sem, taken.freed(t))
                for k in range(PATCH_K):
                    nc.tensor.matmul(bank[:, b, 0:DIM], patch_buf[b][:, k, :], w_emb[:, k, :], start=(k == 0), stop=False)
                nc.tensor.matmul(bank[:, b, 0:DIM], select38[:, t * P:(t + 1) * P], rows_sum, start=False,
                                 stop=True).then_inc(summed.sem, 1)

        wte_buf = [zT[:, CI - 1, b * WTE_R * DIM:(b + 1) * WTE_R * DIM] for b in range(2)]
        wte_tail = zT[0:WTE_TAIL, CI - 1, 2 * WTE_R * DIM:(2 * WTE_R + 1) * DIM]

        def wte_load(sp, c, b):
            added = cnt("wte_added")
            view = t_in["wte"][0:WTE_ROWS - WTE_TAIL, :].rearrange("(c p r) e -> c p (r e)", p=P, r=WTE_R)
            sp.wait_ge(added.sem, added.freed(c))
            sp.dma_start(wte_buf[b], view[ds(c, 1)].rearrange("a p n -> (a p) n")).then_inc(wte_loaded[b], 16)

        def wte_pool(pool, ch):
            added = cnt("wte_added")
            ch.step(nc.gpsimd.memset(wte_sum[:, :], 0.0))
            ch.settle()
            with pool.Fori(0, WTE_CH // 2) as i:
                for b in range(2):
                    pool.wait_ge(wte_loaded[b], 16 * i + 16)
                    pool.wait_ge(added.sem, 2 * i + b + CREDITS)
                    nc.gpsimd.tensor_tensor(wte_sum[:, :], wte_sum[:, :], wte_buf[b], ALU.add).then_inc(added.sem, 1)
            if WTE_CH % 2:
                pool.wait_ge(wte_loaded[0], 16 * (WTE_CH // 2 + 1))
                pool.wait_ge(added.sem, WTE_CH - 1 + CREDITS)
                nc.gpsimd.tensor_tensor(wte_sum[:, :], wte_sum[:, :], wte_buf[0], ALU.add).then_inc(added.sem, 1)
            pool.wait_ge(added.sem, WTE_CH + CREDITS)
            pool.wait_ge(load_tail, 16)
            ch.step(nc.gpsimd.tensor_tensor(wte_sum[0:WTE_TAIL, 0:DIM], wte_sum[0:WTE_TAIL, 0:DIM], wte_tail, ALU.add))
            ch.settle()
            half = WTE_R // 2
            while half:
                ch.step(nc.gpsimd.tensor_tensor(wte_sum[:, 0:half * DIM], wte_sum[:, 0:half * DIM],
                                                wte_sum[:, half * DIM:2 * half * DIM], ALU.add))
                ch.settle()
                half //= 2

        def soft_shift(ch, psum, work, peak, mask=None):
            src = psum
            if mask is not None:
                ch.step(nc.vector.tensor_tensor(work, psum, mask.unsqueeze(1).broadcast_to(list(work.shape)), ALU.add))
                ch.settle()
                src = work
            ch.step(nc.vector.tensor_reduce(peak, src, AX_X, ALU.max))
            ch.settle()
            return nc.vector.tensor_tensor(work, src, peak.unsqueeze(2).broadcast_to(list(work.shape)), ALU.subtract)

        class Heads16:
            def __init__(self, i, name, rope):
                self.i, self.rope = i, rope
                c = Carve()
                self.q, self.k = c(KD, KT, GPAD), c(KD, KT, GPAD)
                self.rot = [c(KD, GT) for _ in range(2)]
                self.copies = c(KD, KT, GI, 3, SEQ)
                self.kbd = [c(KD, 2, KT, HPK, SEQ) for _ in range(2)]
                self.s = [c(P, HEADS, SEQ) for _ in range(PAIRS)]
                self.p = [c(P, HEADS, SEQ) for _ in range(2)]
                self.peak = [c(P, HEADS) for _ in range(PAIRS)]
                self.total = [c(P, HEADS) for _ in range(PAIRS)]
                self.inverse = [c(P, HEADS) for _ in range(PAIRS)]
                self.pt = [c(G3, 4, P) for _ in range(2)]
                self.vw = [c(G3, 2, 4, KD) for _ in range(PAIRS)]
                self.rotated = c(KD, KT, 2 * DIM) if rope else None
                self.rot_bias = c(KD, 2, KT)
                if rope:
                    self.w, self.bq, self.bk, self.rbq, self.rbk, self.bv = (const(n) for n in ("qkv1", "bq", "bk", "bq_turned", "bk_turned", "bv"))
                else:
                    self.w = const("qkvf")
                self.w = self.w.rearrange("p (k n) -> p k n", k=KT)
                self.per_group = 8 if rope else 4
                self.pj = PJ_BASE[name]
                self.g0, self.u0, self.o0 = BASES[name]

            def outputs(self):
                for dst, off in ((self.q, 0), (self.k, DIM)):
                    for m in range(KT):
                        yield dst, m, self.w[:, :, off + m * KD:off + (m + 1) * KD], False
                        if self.rope:
                            yield dst, m, self.rotated[:, :, off + m * KD:off + (m + 1) * KD], True

            def pool(self, pool, ch):
                ch.step(nc.gpsimd.memset(zT[KD:KD + 1, 0, :], 1.0))
                ch.settle()
                for x in (self.q, self.k):
                    ch.step(nc.gpsimd.memset(x[:, :, GT:GPAD], 0.0))
                if self.rope:
                    for off in (0, DIM):
                        for m in range(KT):
                            src = self.w[:, m, off:off + DIM].rearrange("p (h two d) -> p h two d", two=2, d=HD // 2)
                            dst = self.rotated[:, m, off:off + DIM].rearrange("p (h two d) -> p h two d", two=2, d=HD // 2)
                            ch.step(nc.gpsimd.tensor_scalar(dst[:, :, 0, :], src[:, :, 1, :], -1.0, None, ALU.mult))
                            ch.step(nc.gpsimd.tensor_copy(dst[:, :, 1, :], src[:, :, 0, :]))
                    for n, bias in enumerate((self.rbq, self.rbk)):
                        ch.step(nc.gpsimd.tensor_scalar(self.rot_bias[:, n, :], bias, const("rot_sign"), None, ALU.mult))
                ch.settle()
                pool.sem_inc(cnt("prepared").sem, 1)
                qk, kbd, scored = cnt("qk_ready", self.g0 - GROUPS), cnt("kbd_ready", self.u0[1]), cnt("scores_ready", self.u0[0])
                exped, probs, turned = cnt("sum_taken", self.u0[0] - GROUPS * PAIRS), cnt("probs_ready", self.u0[0]), cnt("turned_probs", self.u0[0])
                hmask = const("hmask").unsqueeze(2).broadcast_to([KD, HPK, SEQ])

                def expand(u, p, b):
                    pool.wait_ge(scored.sem, scored.freed(u))
                    for img in range(2):
                        at = (2 * p + img) * SEQ
                        for m in range(KT):
                            last = nc.gpsimd.tensor_tensor(self.kbd[b][:, img, m], self.k[:, m, at:at + SEQ].unsqueeze(1).broadcast_to([KD, HPK, SEQ]), hmask, ALU.mult)
                    last.then_inc(kbd.sem, 1)

                def norm(u, p):
                    pool.wait_ge(exped.sem, exped.done(u))
                    pool.wait_ge(turned.sem, turned.freed(u))
                    nc.gpsimd.tensor_tensor(self.p[p % 2], self.s[p], self.inverse[p].unsqueeze(2).broadcast_to([P, HEADS, SEQ]), ALU.mult).then_inc(probs.sem, 1)

                def group(g, more):
                    u = g * PAIRS
                    norm(u, 0)
                    expand(u + 3, 3, 1)
                    norm(u + 1, 1)
                    norm(u + 2, 2)
                    norm(u + 3, 3)
                    if more:
                        pool.wait_ge(qk.sem, qk.done(g + 1))
                        for p in range(3):
                            expand(u + PAIRS + p, p, p % 2)

                pool.wait_ge(qk.sem, qk.done(0))
                for p in range(3):
                    expand(p, p, p % 2)
                groups(pool, group)

            def pe(self, pe):
                pe.wait_ge(cnt("prepared").sem, cnt("prepared", self.i).done(0))
                pj, pj_taken = cnt("pj_sum", self.pj), cnt("pj_taken", self.pj)
                kbd, scored, s_taken = cnt("kbd_ready", self.u0[1]), cnt("scores_ready", self.u0[0]), cnt("shifted", self.u0[0])
                copies, v_sum, v_in = cnt("tokens_copied", self.g0), cnt("v_sum", self.u0[1]), cnt("v_in", self.u0[1])
                probs, turned, p_in = cnt("probs_ready", self.u0[0]), cnt("turned_probs", self.u0[0]), cnt("probs_in", self.u0[0])
                o_sum, o_taken = cnt("o_sum", self.o0[0]), cnt("o_taken", self.o0[1])

                def scores(u, p, b):
                    pe.wait_ge(kbd.sem, kbd.done(u))
                    pe.wait_ge(s_taken.sem, s_taken.freed(u))
                    for img in range(2):
                        at = (2 * p + img) * SEQ
                        for m in range(KT):
                            last = nc.tensor.matmul(bank[img * SLOT:(img + 1) * SLOT, 2 + b, m * HPK * SEQ:(m + 1) * HPK * SEQ],
                                                    self.q[:, m, at:at + SLOT], self.kbd[b][:, img, m].rearrange("p h t -> p (h t)"),
                                                    start=True, stop=True)
                    last.then_inc(scored.sem, 1)

                def values(u, p):
                    pe.wait_ge(v_in.sem, v_in.done(u - 1))
                    for img in range(2):
                        for m in range(KT):
                            last = nc.tensor.matmul(bank[0:G3, 6, img * DIM:(img + 1) * DIM],
                                                    self.copies[:, m, 2 * p + img].rearrange("p c t -> p (c t)"),
                                                    self.w[:, m, 2 * DIM:3 * DIM], start=(m == 0), stop=(m == KT - 1))
                    last.then_inc(v_sum.sem, 1)

                def turn(u, b):
                    pe.wait_ge(probs.sem, probs.done(u))
                    pe.wait_ge(p_in.sem, p_in.freed(u))
                    flat = self.p[b].rearrange("p h t -> p (h t)")
                    for j in range(4):
                        last = nc.tensor.transpose(bank[0:G3, 4 + b, j * P:(j + 1) * P], flat[:, j * G3:(j + 1) * G3], ident)
                    last.then_inc(turned.sem, 1)

                def mix(u, p):
                    b = p % 2
                    pe.wait_ge(p_in.sem, p_in.done(u))
                    pe.wait_ge(v_in.sem, v_in.done(u))
                    pe.wait_ge(o_taken.sem, o_taken.done(u - 1))
                    for m in range(KT):
                        for img in range(2):
                            for j in range(2):
                                last = nc.tensor.matmul(bank[0:KD, 7, (2 * m + img) * SEQ:(2 * m + img + 1) * SEQ],
                                                        self.vw[p][:, img, 2 * m + j, :],
                                                        self.pt[b][:, 2 * m + j, img * SLOT:img * SLOT + SEQ],
                                                        start=(j == 0), stop=(j == 1))
                    last.then_inc(o_sum.sem, 1)

                def project(g, first, last_):
                    for n, (_, m, w, _) in list(enumerate(self.outputs()))[first:last_]:
                        pe.wait_ge(pj_taken.sem, pj_taken.freed(g * self.per_group + n))
                        for kk in range(KT):
                            last = nc.tensor.matmul(bank[0:KD, n % 2, 0:GT], w[:, kk, :], xT[:, kk, ds(g * GT, GT)],
                                                    start=(kk == 0), stop=(kk == KT - 1))
                        last.then_inc(pj.sem, 1)

                def open_(g):
                    u = g * PAIRS
                    scores(u, 0, 0)
                    scores(u + 1, 1, 1)
                    pe.wait_ge(copies.sem, copies.done(g))
                    values(u, 0)
                    scores(u + 2, 2, 0)

                def group(g, more):
                    u, half = g * PAIRS, self.per_group // 2
                    turn(u, 0)
                    scores(u + 3, 3, 1)
                    values(u + 1, 1)
                    for p in (1, 2):
                        turn(u + p, p % 2)
                        mix(u + p - 1, p - 1)
                        values(u + p + 1, p + 1)
                        if more:
                            project(g + 1, (p - 1) * half, p * half)
                    turn(u + 3, 1)
                    mix(u + 2, 2)
                    mix(u + 3, 3)
                    if more:
                        open_(g + 1)

                project(0, 0, self.per_group)
                open_(0)
                groups(pe, group)

            def dve(self, dve, ch):
                pj, pj_taken = cnt("pj_sum", self.pj), cnt("pj_taken", self.pj)
                qk = cnt("qk_ready", self.g0 - GROUPS)
                scored, shifted = cnt("scores_ready", self.u0[0]), cnt("shifted", self.u0[0])
                exped, summed, probs = cnt("exped", self.u0[0]), cnt("sum_taken", self.u0[0] - GROUPS * PAIRS), cnt("probs_ready", self.u0[0])
                v_sum, v_in, o_sum = cnt("v_sum", self.u0[1]), cnt("v_in", self.u0[1]), cnt("o_sum", self.o0[0])
                cos, sin = (const(n).unsqueeze(1).broadcast_to([KD, GI, SEQ]) for n in ("cos", "sin"))
                mask = const("causal") if self.rope else None
                images = lambda x: x.rearrange("p (i t) -> p i t", t=SEQ)
                dve.wait_ge(cnt("prepared").sem, cnt("prepared", self.i).done(0))

                def part1(u, b):
                    dve.wait_ge(scored.sem, scored.done(u))
                    dve.wait_ge(probs.sem, probs.done(u - PAIRS))
                    psum = bank[:, 2 + b % 2, 0:HEADS * SEQ].rearrange("p (h t) -> p h t", t=SEQ)
                    soft_shift(ch, psum, self.s[b], self.peak[b], mask).then_inc(shifted.sem, 1)

                def value(u, b):
                    dve.wait_ge(v_sum.sem, v_sum.done(u))
                    dve.wait_ge(o_sum.sem, o_sum.done(u - PAIRS))
                    for img in range(2):
                        psum = bank[0:G3, 6, img * DIM:(img + 1) * DIM].rearrange("p (m n) -> p m n", m=KT).unsqueeze(2).broadcast_to([G3, KT, 2, KD])
                        msk = const("vmask").rearrange("p (j n) -> p j n", j=2).unsqueeze(1).broadcast_to([G3, KT, 2, KD])
                        out_ = self.vw[b][:, img].rearrange("p (m j) n -> p m j n", j=2)
                        last = nc.vector.tensor_tensor(out_, psum, msk, ALU.mult)
                    last.then_inc(v_in.sem, 1)

                def part2(u, b):
                    dve.wait_ge(exped.sem, exped.done(u))
                    ch.step(nc.vector.tensor_reduce(self.total[b], self.s[b], AX_X, ALU.add))
                    ch.settle()
                    nc.vector.reciprocal(self.inverse[b], self.total[b]).then_inc(summed.sem, 1)

                def take(g, first, last_):
                    for n, (dst, m, _, rotated) in list(enumerate(self.outputs()))[first:last_]:
                        v = g * self.per_group + n
                        dve.wait_ge(pj.sem, pj.done(v))
                        psum = bank[0:KD, n % 2, 0:GT]
                        if not self.rope:
                            nc.vector.tensor_copy(dst[:, m, 0:GT], psum).then_inc(pj_taken.sem, 1)
                            continue
                        bias = {(0, False): self.bq, (0, True): self.rot_bias[:, 0], (1, False): self.bk, (1, True): self.rot_bias[:, 1]}[(0 if dst is self.q else 1, rotated)]
                        if n >= 2:
                            ch.settle()
                        nc.vector.scalar_tensor_tensor(images(self.rot[int(rotated)]), images(psum), bias[:, m:m + 1],
                                                       sin if rotated else cos, ALU.add, ALU.mult).then_inc(pj_taken.sem, 1)
                        if rotated:
                            dve.wait_ge(pj_taken.sem, pj_taken.done(v))
                            ch.step(nc.vector.tensor_tensor(dst[:, m, 0:GT], self.rot[0], self.rot[1], ALU.add))
                    if last_ == self.per_group:
                        dve.wait_ge(pj_taken.sem, pj_taken.done(g * self.per_group + self.per_group - 1))
                        ch.settle()
                        dve.sem_inc(qk.sem, 1)

                def open_(g):
                    u = g * PAIRS
                    part1(u, 0)
                    part1(u + 1, 1)
                    value(u, 0)

                def group(g, more):
                    u, half = g * PAIRS, self.per_group // 2
                    part2(u, 0)
                    part1(u + 2, 2)
                    part2(u + 1, 1)
                    part1(u + 3, 3)
                    value(u + 1, 1)
                    part2(u + 2, 2)
                    value(u + 2, 2)
                    part2(u + 3, 3)
                    if more:
                        take(g + 1, 0, half)
                    value(u + 3, 3)
                    if more:
                        take(g + 1, half, 2 * half)
                        open_(g + 1)

                take(0, 0, self.per_group)
                open_(0)
                groups(dve, group, ch, 4 + 3 * PAIRS if self.rope else 2 * PAIRS)

            def act(self, act):
                copies, v_sum = cnt("tokens_copied", self.g0), cnt("v_sum", self.u0[1])
                shifted, exped = cnt("shifted", self.u0[0]), cnt("exped", self.u0[0])
                turned, p_in, o_sum, o_taken = cnt("turned_probs", self.u0[0]), cnt("probs_in", self.u0[0]), cnt("o_sum", self.o0[0]), cnt("o_taken", self.o0[1])

                def exp(u, b):
                    act.wait_ge(shifted.sem, shifted.done(u))
                    nc.scalar.activation(self.s[b], self.s[b], ACT.Exp, scale=HD ** -0.5).then_inc(exped.sem, 1)

                def copy(g):
                    act.wait_ge(v_sum.sem, v_sum.done(g * PAIRS - 1))
                    for m in range(KT):
                        last = nc.scalar.activation(self.copies[:, m], xT[:, m, ds(g * GT, GT)].rearrange("p (i t) -> p i t", t=SEQ).unsqueeze(2).broadcast_to([KD, GI, 3, SEQ]), ACT.Copy)
                    last.then_inc(copies.sem, 1)

                def output(g, p):
                    act.wait_ge(o_sum.sem, o_sum.done(g * PAIRS + p))
                    for m in range(KT):
                        last = nc.scalar.activation(zT[0:KD, m, ds(g * GT + 2 * p * SEQ, 2 * SEQ)],
                                                    bank[0:KD, 7, 2 * m * SEQ:2 * (m + 1) * SEQ], ACT.Identity,
                                                    bias=self.bv[:, m:m + 1] if self.rope else 0.0)
                    last.then_inc(o_taken.sem, 1)

                def group(g, more):
                    u = g * PAIRS
                    exp(u + 2, 2)
                    for p in range(PAIRS):
                        b = p % 2
                        act.wait_ge(turned.sem, turned.done(u + p))
                        act.wait_ge(o_sum.sem, o_sum.freed(u + p))
                        nc.scalar.activation(self.pt[b].rearrange("p j n -> p (j n)"), bank[0:G3, 4 + b, :], ACT.Copy).then_inc(p_in.sem, 1)
                        if p == 0:
                            exp(u + 3, 3)
                        else:
                            output(g, p - 1)
                    if more:
                        copy(g + 1)
                    output(g, PAIRS - 1)
                    if more:
                        exp(u + PAIRS, 0)
                        exp(u + PAIRS + 1, 1)

                copy(0)
                exp(0, 0)
                exp(1, 1)
                groups(act, group)

        class Tokens12:
            def __init__(self):
                c, r = Carve(), Carve(rounded)
                self.wo = c(KD, KT * HEADS, DIM)
                self.a = c(KD, KT, GPAD)
                self.w2 = c(KD, KT, HEADS)
                self.kx = [c(KD, 2, KT, HEADS, SEQ) for _ in range(2)]
                self.s = [c(P, HEADS, SEQ) for _ in range(2)]
                self.p = c(P, HEADS, 3, SEQ)
                self.a_parts = c(KD, KT, GI, 3, SEQ)
                self.peak, self.total, self.inverse = ([c(P, HEADS) for _ in range(2)] for _ in range(3))
                self.pt = [r(G3, 2, HEADS, SEQ) for _ in range(2)]
                self.v = [r(G3, 2, DIM) for _ in range(2)]
                self.att = [kept[0:KD, :].rearrange("p (m h n) -> p m h n", m=KT, h=HEADS), c(KD, KT, HEADS, 4 * SEQ)]
                self.offset = c(KD, KT)

            def pe(self, pe):
                kx, scored, shifted = cnt("kbd_ready"), cnt("scores_ready"), cnt("shifted")
                copied, v_sum, v_in = cnt("tokens_copied"), cnt("v_sum"), cnt("v_in")
                probs, turned, p_in = cnt("probs_ready"), cnt("turned_probs"), cnt("probs_in")
                o_sum, o_taken, wo_sum, wo_taken = cnt("o_sum"), cnt("o_taken"), cnt("wo_sum"), cnt("wo_taken")

                def scores(u, p, b):
                    pe.wait_ge(kx.sem, kx.done(u))
                    pe.wait_ge(shifted.sem, shifted.done(u - 1))
                    for img in range(2):
                        at = (2 * p + img) * SEQ
                        for m in range(KT):
                            last = nc.tensor.matmul(bank[img * SLOT:(img + 1) * SLOT, 0, 0:HEADS * SEQ], self.a[:, m, at:at + SLOT],
                                                    self.kx[b][:, img, m].rearrange("p h t -> p (h t)"),
                                                    start=(m == 0), stop=(m == KT - 1))
                    last.then_inc(scored.sem, 1)

                def values(u, p):
                    wait_apart(pe, v_in.sem, v_in.done(u - 1))
                    for img in range(2):
                        for m in range(KT):
                            last = nc.tensor.transpose(bank[0:G3, 4, img * DIM + m * KD:img * DIM + (m + 1) * KD],
                                                       self.a_parts[:, m, 2 * p + img].rearrange("p c t -> p (c t)"), ident[0:KD, 0:KD])
                    last.then_inc(v_sum.sem, 1)

                def turn(u, b):
                    pe.wait_ge(p_in.sem, p_in.done(u - 1))
                    wait_apart(pe, probs.sem, probs.done(u))
                    for hh in range(HEADS):
                        last = nc.tensor.transpose(bank[0:G3, 1 + hh // 4, hh % 4 * P:(hh % 4 + 1) * P], self.p[:, hh].rearrange("p c t -> p (c t)"), ident)
                    last.then_inc(turned.sem, 1)

                def mix(u, b):
                    pe.wait_ge(p_in.sem, p_in.done(u))
                    pe.wait_ge(v_in.sem, v_in.done(u))
                    for n in range(4):
                        img, m = divmod(n, 2)
                        pe.wait_ge(o_taken.sem, o_taken.freed(4 * u + n))
                        nc.tensor.matmul(bank[0:KD, 5 + n % 2, 0:HEADS * SEQ], self.v[b][:, img, m * KD:(m + 1) * KD].bitcast(F32R),
                                         self.pt[b][:, img].rearrange("p h t -> p (h t)").bitcast(F32R), start=True, stop=True).then_inc(o_sum.sem, 1)

                def project(g, quad):
                    q = 2 * g + quad
                    pe.wait_ge(o_taken.sem, o_taken.done(4 * PAIRS * g + 8 * quad + 7))
                    pe.wait_ge(wo_taken.sem, wo_taken.done(q - 1))
                    for mt in range(KT):
                        for n in range(KT * HEADS):
                            last = nc.tensor.matmul(bank[0:KD, 7, mt * 4 * SEQ:(mt + 1) * 4 * SEQ], self.wo[:, n, mt * KD:(mt + 1) * KD],
                                                    self.att[quad][:, n // HEADS, n % HEADS, :], start=(n == 0), stop=(n == KT * HEADS - 1))
                    last.then_inc(wo_sum.sem, 1)

                pe.wait_ge(load_wo, 16)
                def open_(g):
                    u = g * PAIRS
                    pe.wait_ge(copied.sem, copied.done(g))
                    scores(u, 0, 0)
                    pe.wait_ge(cnt("tokens_split").sem, cnt("tokens_split").done(g))
                    values(u, 0)
                    scores(u + 1, 1, 1)

                def group(g, more):
                    u = g * PAIRS
                    for p in range(PAIRS):
                        turn(u + p, p % 2)
                        if p + 2 < PAIRS:
                            scores(u + p + 2, p + 2, p % 2)
                        if p + 1 < PAIRS:
                            values(u + p + 1, p + 1)
                        if p:
                            mix(u + p - 1, (p - 1) % 2)
                    project(g, 0)
                    mix(u + PAIRS - 1, (PAIRS - 1) % 2)
                    if more:
                        open_(g + 1)
                    project(g, 1)

                open_(0)
                groups(pe, group)

            def dve(self, dve, ch):
                kx, scored, shifted, exped = cnt("kbd_ready"), cnt("scores_ready"), cnt("shifted"), cnt("exped")
                copied, probs, turned = cnt("tokens_copied"), cnt("probs_ready"), cnt("turned_probs")
                wqk = const("wqk").rearrange("p (k h) -> p k h", k=KT)
                ch.step(nc.vector.tensor_tensor(self.w2, wqk, wqk, ALU.mult))
                ch.settle()

                def expand(u, p, b):
                    dve.wait_ge(scored.sem, scored.freed(u))
                    for img in range(2):
                        at = (2 * p + img) * SEQ
                        shape = [KD, KT, HEADS, SEQ]
                        last = nc.vector.tensor_tensor(self.kx[b][:, img], self.a[:, :, at:at + SEQ].unsqueeze(2).broadcast_to(shape),
                                                       self.w2.unsqueeze(3).broadcast_to(shape), ALU.mult)
                    last.then_inc(kx.sem, 1)

                def part1(u, b):
                    dve.wait_ge(scored.sem, scored.done(u))
                    dve.wait_ge(probs.sem, probs.freed(u))
                    soft_shift(ch, bank[:, 0, 0:HEADS * SEQ].rearrange("p (h t) -> p h t", t=SEQ), self.s[b], self.peak[b],
                               const("causal")).then_inc(shifted.sem, 1)

                def part2(u, b):
                    dve.wait_ge(exped.sem, exped.done(u))
                    ch.step(nc.vector.tensor_reduce(self.total[b], self.s[b], AX_X, ALU.add))
                    ch.settle()
                    ch.step(nc.vector.reciprocal(self.inverse[b], self.total[b]))
                    ch.settle()
                    ch.step(nc.vector.scalar_tensor_tensor(self.s[b], self.s[b], const("nreg_row"), self.inverse[b].unsqueeze(2).broadcast_to([P, HEADS, SEQ]),
                                                           ALU.mult, ALU.mult))
                    ch.settle()
                    dve.wait_ge(turned.sem, turned.done(u - 1))
                    ch.step(nc.vector.tensor_copy(self.p[:, :, 0:2].bitcast(F32R), self.s[b].unsqueeze(2).broadcast_to([P, HEADS, 2, SEQ])))
                    ch.settle()
                    nc.vector.tensor_tensor(self.p[:, :, 2].bitcast(F32R), self.s[b], self.p[:, :, 0], ALU.subtract).then_inc(probs.sem, 1)

                def split(g):
                    v_sum = cnt("v_sum")
                    dve.wait_ge(v_sum.sem, v_sum.done(g * PAIRS - 1))
                    tokens = [self.a[:, m, 0:GT].rearrange("p (i t) -> p i t", t=SEQ) for m in range(KT)]
                    for part in (0, 2):
                        for m in range(KT):
                            ch.step(nc.vector.tensor_copy(self.a_parts[:, m, :, part].bitcast(F32R), tokens[m]))
                    ch.settle()
                    for m in range(KT):
                        ch.step(nc.vector.tensor_tensor(self.a_parts[:, m, :, 1].bitcast(F32R), tokens[m], self.a_parts[:, m, :, 0], ALU.subtract))
                    ch.settle()
                    dve.sem_inc(cnt("tokens_split").sem, 1)

                def open_(g):
                    u = g * PAIRS
                    dve.wait_ge(copied.sem, copied.done(g))
                    expand(u, 0, 0)
                    split(g)
                    expand(u + 1, 1, 1)
                    part1(u, 0)
                    part1(u + 1, 1)
                    part2(u, 0)

                def group(g, more):
                    u = g * PAIRS
                    for p in range(1, PAIRS):
                        if p + 1 < PAIRS:
                            expand(u + p + 1, p + 1, (p + 1) % 2)
                        part2(u + p, p % 2)
                        if p + 1 < PAIRS:
                            part1(u + p + 1, (p + 1) % 2)
                    if more:
                        open_(g + 1)

                open_(0)
                groups(dve, group, ch, 6 * PAIRS + 6)

            def act(self, act, ch):
                copied, v_sum, v_in, scored = cnt("tokens_copied"), cnt("v_sum"), cnt("v_in"), cnt("scores_ready")
                shifted, exped, turned, p_in = cnt("shifted"), cnt("exped"), cnt("turned_probs"), cnt("probs_in")
                wo_sum, wo_taken, o_sum, o_taken = cnt("wo_sum"), cnt("wo_taken"), cnt("o_sum"), cnt("o_taken")
                ch.step(nc.scalar.activation(self.a[:, :, GT:GPAD], xT[:, :, 0:GPAD - GT], ACT.Copy))
                ch.settle()

                def exp(u, b):
                    act.wait_ge(shifted.sem, shifted.done(u))
                    nc.scalar.activation(self.s[b], self.s[b], ACT.Exp, scale=float(DIM) ** -0.5).then_inc(exped.sem, 1)

                def value(u, b):
                    act.wait_ge(v_sum.sem, v_sum.done(u))
                    nc.scalar.activation(self.v[b].bitcast(F32R), bank[0:G3, 4, 0:2 * DIM].rearrange("p (i n) -> p i n", i=2), ACT.Copy).then_inc(v_in.sem, 1)

                def take(u, p, g):
                    if p % 2 == 0:
                        act.wait_ge(wo_sum.sem, wo_sum.freed(2 * g + p // 2))
                    for n in range(4):
                        img, m = divmod(n, 2)
                        at = (2 * (p % 2) + img) * SEQ
                        act.wait_ge(o_sum.sem, o_sum.done(4 * u + n))
                        nc.scalar.activation(self.att[p // 2][:, m, :, at:at + SEQ],
                                             bank[0:KD, 5 + n % 2, 0:HEADS * SEQ].rearrange("p (h t) -> p h t", t=SEQ), ACT.Copy).then_inc(o_taken.sem, 1)

                def output(g, quad):
                    q = 2 * g + quad
                    act.wait_ge(wo_sum.sem, wo_sum.done(q))
                    nc.scalar.activation(zT[0:KD, 0:KT, ds(g * GT + quad * 4 * SEQ, 4 * SEQ)],
                                         bank[0:KD, 7, 0:KT * 4 * SEQ].rearrange("p (m n) -> p m n", m=KT), ACT.Copy).then_inc(wo_taken.sem, 1)

                def copy(g):
                    u = g * PAIRS
                    act.wait_ge(v_sum.sem, v_sum.done(u - 1))
                    act.wait_ge(scored.sem, scored.done(u - 1))
                    nc.scalar.activation(self.a[:, :, 0:GT], xT[:, :, ds(g * GT, GT)], ACT.Copy).then_inc(copied.sem, 1)

                def open_(g):
                    u = g * PAIRS
                    exp(u, 0)
                    value(u, 0)
                    exp(u + 1, 1)

                def group(g, more):
                    u = g * PAIRS
                    for p in range(PAIRS):
                        b = p % 2
                        act.wait_ge(turned.sem, turned.done(u + p))
                        if p >= 2:
                            act.wait_ge(o_sum.sem, o_sum.done(4 * (u + p) - 5))
                        for img in range(2):
                            last = nc.scalar.activation(self.pt[b][:, img].bitcast(F32R), bank[0:G3, 1:4, :].rearrange("p k (h n) -> p (k h) n", n=P)[:, :, img * SLOT:img * SLOT + SEQ], ACT.Copy)
                        last.then_inc(p_in.sem, 1)
                        if p + 2 < PAIRS:
                            exp(u + p + 2, b)
                        if p:
                            take(u + p - 1, p - 1, g)
                        if p + 1 < PAIRS:
                            value(u + p + 1, (p + 1) % 2)
                        if more and p == 2:
                            copy(g + 1)
                    output(g, 0)
                    take(u + PAIRS - 1, PAIRS - 1, g)
                    if more:
                        open_(g + 1)
                    output(g, 1)

                copy(0)
                open_(0)
                groups(act, group)

            def offset_pe(self, pe):
                for m in range(KT):
                    last = nc.tensor.matmul(bank[0:KD, 0, m:m + 1], wte_sum[:, m * KD:(m + 1) * KD], ones[:, 0:1], start=True, stop=True)
                last.then_inc(cnt("mean_sum").sem, 1)
                pe.wait_ge(cnt("mean_in").sem, cnt("mean_in").done(0))
                for mt in range(KT):
                    for n in range(KT * HEADS):
                        last = nc.tensor.matmul(bank[0:KD, 1, mt:mt + 1], self.wo[:, n, mt * KD:(mt + 1) * KD],
                                                avg_wte[:, n // HEADS:n // HEADS + 1], start=(n == 0), stop=(n == KT * HEADS - 1))
                last.then_inc(cnt("offset_sum").sem, 1)

            def offset_act(self, act):
                act.wait_ge(cnt("mean_sum").sem, cnt("mean_sum").done(0))
                nc.scalar.activation(avg_wte[:, :], bank[0:KD, 0, 0:KT], ACT.Copy, scale=1.0 / WTE_ROWS).then_inc(cnt("mean_in").sem, 1)

            def offset_dve(self, dve, ch):
                dve.wait_ge(cnt("offset_sum").sem, cnt("offset_sum").done(0))
                ch.step(nc.vector.tensor_scalar(self.offset, bank[0:KD, 1, 0:KT], -1.0, None, ALU.mult))
                ch.settle()
                for m in range(KT):
                    z = zT[0:KD, m, :].rearrange("p (i t) -> p i t", t=SEQ)
                    ch.step(nc.vector.scalar_tensor_tensor(z, const("nreg").unsqueeze(1).broadcast_to([KD, IMAGES, SEQ]),
                                                           self.offset[:, m:m + 1], z, ALU.mult, ALU.add))

        class Parts8:
            def __init__(self):
                c = Carve()
                self.qk = c(KF, 5, GPAD)
                self.copies = c(KD, KT, GI, 3, SEQ)
                self.kbd = [c(KF, 2, 3, NH3, SEQ) for _ in range(2)]
                self.s = [c(P, 2, NH3, SEQ) for _ in range(AHEAD)]
                self.p = [c(P, 2, NH3 + 1, SEQ) for _ in range(2)]
                self.peak2, self.total2 = ([c(P, 2, NH3) for _ in range(AHEAD)] for _ in range(2))
                self.peak, self.total, self.inverse = ([c(P, NH3) for _ in range(AHEAD)] for _ in range(3))
                self.pt = [c(G3, 2, 3, P) for _ in range(2)]
                self.vw = [c(G3, 2, 3, 3, KF) for _ in range(2)]
                self.w = const("qkv3").rearrange("p (k n) -> p k n", k=KT)
                (self.g0, (self.w0, self.u0), self.o0), self.pj = BASES["L3"], PJ_BASE["L3"]

            def pool(self, pool, ch):
                ch.step(nc.gpsimd.memset(zT[KF:KF + 1, 0, :], 1.0))
                ch.settle()
                ch.step(nc.gpsimd.memset(self.qk[:, :, GT:GPAD], 0.0))
                for b in range(2):
                    ch.step(nc.gpsimd.memset(self.p[b][:, :, NH3, :], 0.0))
                ch.settle()
                pool.sem_inc(cnt("prepared").sem, 1)
                qk, kbd, scored = cnt("qk_ready", self.g0 - GROUPS), cnt("kbd_ready", self.u0), cnt("scores_ready", self.w0)
                probs, turned = (cnt(n, self.w0) for n in ("probs_ready", "turned_probs"))
                summed = cnt("sum_taken", self.w0 - GROUPS * PAIRS)

                def expand(u, p, b):
                    pool.wait_ge(scored.sem, scored.done(3 * u - 4))
                    for img in range(2):
                        at = (2 * p + img) * SEQ
                        shape = [KF, 3, NH3, SEQ]
                        last = nc.gpsimd.tensor_tensor(self.kbd[b][:, img], self.qk[:, 2:5, at:at + SEQ].unsqueeze(2).broadcast_to(shape),
                                                       const("hmask8").unsqueeze(1).unsqueeze(3).broadcast_to(shape), ALU.mult)
                    last.then_inc(kbd.sem, 1)

                def group(g, more):
                    u = g * PAIRS
                    for p in range(PAIRS):
                        if p + 1 < PAIRS:
                            expand(u + p + 1, p + 1, (p + 1) % 2)
                        for j in range(3):
                            w, b, a = 3 * (u + p) + j, (3 * p + j) % 2, (3 * p + j) % AHEAD
                            pool.wait_ge(summed.sem, summed.done(w))
                            pool.wait_ge(turned.sem, turned.freed(w))
                            shape = [P, 2, NH3, SEQ]
                            nc.gpsimd.tensor_tensor(self.p[b][:, :, 0:NH3, :], self.s[a],
                                                    self.inverse[a].unsqueeze(1).unsqueeze(3).broadcast_to(shape), ALU.mult).then_inc(probs.sem, 1)
                    if more:
                        pool.wait_ge(qk.sem, qk.done(g + 1))
                        expand(u + PAIRS, 0, 0)

                pool.wait_ge(qk.sem, qk.done(0))
                expand(0, 0, 0)
                groups(pool, group)

            def pe(self, pe):
                pe.wait_ge(cnt("prepared").sem, cnt("prepared", 2).done(0))
                pj = cnt("pj_sum", self.pj)
                kbd, v_sum, v_in = (cnt(n, self.u0) for n in ("kbd_ready", "v_sum", "v_in"))
                copied = cnt("tokens_copied", self.g0)
                scored, shifted, probs, turned, p_in = (cnt(n, self.w0) for n in ("scores_ready", "shifted", "probs_ready", "turned_probs", "probs_in"))
                o_taken, mixed = cnt("o_taken", self.o0[1]), cnt("mixed", EXTRA["mixed"])

                def scores(u, n):
                    p, j = divmod(n, 3)
                    b, w = n % 2, 3 * u + n
                    pe.wait_ge(kbd.sem, kbd.done(u + p))
                    wait_apart(pe, shifted.sem, shifted.freed(w))
                    for img in range(2):
                        at = (2 * p + img) * SEQ
                        for half, part in enumerate(HALVES[j]):
                            last = nc.tensor.matmul(bank[img * SLOT:(img + 1) * SLOT, 2 * b + half, 0:NH3 * SEQ], self.qk[:, QUERY[j], at:at + SLOT],
                                                    self.kbd[p % 2][:, img, part].rearrange("p h t -> p (h t)"), start=True, stop=True)
                    last.then_inc(scored.sem, 1)

                def values(u, p):
                    pe.wait_ge(v_in.sem, v_in.done(u - 1))
                    for img in range(2):
                        for m in range(KT):
                            last = nc.tensor.matmul(bank[0:G3, 6, img * DIM:(img + 1) * DIM],
                                                    self.copies[:, m, 2 * p + img].rearrange("p c t -> p (c t)"),
                                                    self.w[:, m, 5 * KF:8 * KF], start=(m == 0), stop=(m == KT - 1))
                    last.then_inc(v_sum.sem, 1)

                def turn(w, b):
                    pe.wait_ge(probs.sem, probs.done(w))
                    pe.wait_ge(p_in.sem, p_in.done(w - 1))
                    for half in range(2):
                        flat = self.p[b][:, half].rearrange("p h t -> p (h t)")
                        for gr in range(3):
                            last = nc.tensor.transpose(bank[0:G3, 4 + half, gr * P:(gr + 1) * P], flat[:, gr * G3:(gr + 1) * G3], ident)
                    last.then_inc(turned.sem, 1)

                def mix(u, p, j, w, b):
                    pe.wait_ge(p_in.sem, p_in.done(w))
                    if j == 0:
                        pe.wait_ge(v_in.sem, v_in.done(u))
                        pe.wait_ge(o_taken.sem, o_taken.done(u - 1))
                    for img in range(2):
                        for half, part in enumerate(HALVES[j]):
                            for gr in range(3):
                                last = nc.tensor.matmul(bank[0:KF, 7, (2 * j + img) * SEQ:(2 * j + img + 1) * SEQ], self.vw[p % 2][:, img, part, gr, :],
                                                        self.pt[b][:, half, gr, img * SLOT:img * SLOT + SEQ],
                                                        start=(half == 0 and gr == 0), stop=(half == 1 and gr == 2))
                    last.then_inc(mixed.sem, 1)

                def mix_unit(u, n):
                    p, j = divmod(n, 3)
                    mix(u + p, p, j, 3 * u + n, n % 2)

                def project(g):
                    wait_apart(pe, shifted.sem, shifted.done(3 * PAIRS * g - 1))
                    for n in range(5):
                        if n == 4:
                            wait_apart(pe, v_in.sem, v_in.done(PAIRS * g - 1))
                        for kk in range(KT):
                            last = nc.tensor.matmul(bank[0:KF, PJ_BANK[n], 0:GT], self.w[:, kk, n * KF:(n + 1) * KF], xT[:, kk, ds(g * GT, GT)],
                                                    start=(kk == 0), stop=(kk == KT - 1))
                        last.then_inc(pj.sem, 1)

                def open_(g):
                    u = g * PAIRS
                    scores(u, 0)
                    scores(u, 1)
                    pe.wait_ge(copied.sem, copied.done(g))
                    values(u, 0)
                    scores(u, 2)

                def group(g, more):
                    u, units = g * PAIRS, 3 * PAIRS
                    for n in range(units):
                        p, j = divmod(n, 3)
                        turn(3 * u + n, n % 2)
                        if n + 3 < units:
                            scores(u, n + 3)
                        if n:
                            mix_unit(u, n - 1)
                        if j == 0 and p + 1 < PAIRS:
                            values(u + p + 1, p + 1)
                        if more and n == units - 2:
                            project(g + 1)
                    mix_unit(u, units - 1)
                    if more:
                        open_(g + 1)

                project(0)
                open_(0)
                groups(pe, group)

            def dve(self, dve, ch):
                dve.wait_ge(cnt("prepared").sem, cnt("prepared", 2).done(0))
                pj, pj_taken, qk = cnt("pj_sum", self.pj), cnt("pj_taken", self.pj), cnt("qk_ready", self.g0 - GROUPS)
                scored, shifted, exped, probs = (cnt(n, self.w0) for n in ("scores_ready", "shifted", "exped", "probs_ready"))
                summed = cnt("sum_taken", self.w0 - GROUPS * PAIRS)
                v_sum, v_in, mixed = cnt("v_sum", self.u0), cnt("v_in", self.u0), cnt("mixed", EXTRA["mixed"])

                def part1(w, n):
                    b = n % AHEAD
                    dve.wait_ge(scored.sem, scored.done(w))
                    dve.wait_ge(probs.sem, probs.done(w - AHEAD))
                    psum = bank[:, 2 * (n % 2):2 * (n % 2) + 2, 0:NH3 * SEQ].rearrange("p k (h t) -> p k h t", t=SEQ)
                    ch.step(nc.vector.tensor_reduce(self.peak2[b], psum, AX_X, ALU.max))
                    ch.settle()
                    ch.step(nc.vector.tensor_tensor(self.peak[b], self.peak2[b][:, 0], self.peak2[b][:, 1], ALU.max))
                    ch.settle()
                    nc.vector.tensor_tensor(self.s[b], psum, self.peak[b].unsqueeze(1).unsqueeze(3).broadcast_to([P, 2, NH3, SEQ]),
                                            ALU.subtract).then_inc(shifted.sem, 1)

                def part2(w, n):
                    b = n % AHEAD
                    dve.wait_ge(exped.sem, exped.done(w))
                    ch.step(nc.vector.tensor_reduce(self.total2[b], self.s[b], AX_X, ALU.add))
                    ch.settle()
                    ch.step(nc.vector.tensor_tensor(self.total[b], self.total2[b][:, 0], self.total2[b][:, 1], ALU.add))
                    ch.settle()
                    nc.vector.reciprocal(self.inverse[b], self.total[b]).then_inc(summed.sem, 1)

                def value(u, b):
                    dve.wait_ge(v_sum.sem, v_sum.done(u))
                    dve.wait_ge(mixed.sem, mixed.done(3 * u - 4))
                    for img in range(2):
                        shape = [G3, 3, 3, KF]
                        last = nc.vector.tensor_tensor(self.vw[b][:, img],
                                                       bank[0:G3, 6, img * DIM:(img + 1) * DIM].rearrange("p (v n) -> p v n", v=3).unsqueeze(2).broadcast_to(shape),
                                                       const("vmask8").rearrange("p (g n) -> p g n", g=3).unsqueeze(1).broadcast_to(shape), ALU.mult)
                    last.then_inc(v_in.sem, 1)

                def take(g):
                    for n in range(5):
                        dve.wait_ge(pj.sem, pj.done(5 * g + n))
                        nc.vector.tensor_copy(self.qk[:, n, 0:GT], bank[0:KF, PJ_BANK[n], 0:GT]).then_inc(pj_taken.sem, 1)
                    dve.wait_ge(pj_taken.sem, pj_taken.done(5 * g + 4))
                    dve.sem_inc(qk.sem, 1)

                def open_(g):
                    u = g * PAIRS
                    part1(3 * u, 0)
                    part1(3 * u + 1, 1)
                    value(u, 0)

                def group(g, more):
                    u, units = g * PAIRS, 3 * PAIRS
                    part2(3 * u, 0)
                    part1(3 * u + 2, 2)
                    for n in range(1, units):
                        p, j = divmod(n, 3)
                        part2(3 * u + n, n)
                        if n + 2 < units:
                            part1(3 * u + n + 2, n + 2)
                        if j == 1 and p + 1 < PAIRS:
                            value(u + p + 1, (p + 1) % 2)
                    if more:
                        take(g + 1)
                    if more:
                        open_(g + 1)

                take(0)
                open_(0)
                groups(dve, group, ch, 4 * 3 * PAIRS)

            def act(self, act):
                copied, v_sum = cnt("tokens_copied", self.g0), cnt("v_sum", self.u0)
                shifted, exped, turned, p_in = (cnt(n, self.w0) for n in ("shifted", "exped", "turned_probs", "probs_in"))
                o_taken, mixed = cnt("o_taken", self.o0[1]), cnt("mixed", EXTRA["mixed"])

                def exp(w, n):
                    b = n % AHEAD
                    act.wait_ge(shifted.sem, shifted.done(w))
                    nc.scalar.activation(self.s[b], self.s[b], ACT.Exp, scale=float(3 * HD3) ** -0.5).then_inc(exped.sem, 1)

                def copy(g):
                    act.wait_ge(v_sum.sem, v_sum.done(g * PAIRS - 1))
                    for m in range(KT):
                        last = nc.scalar.activation(self.copies[:, m], xT[:, m, ds(g * GT, GT)].rearrange("p (i t) -> p i t", t=SEQ).unsqueeze(2).broadcast_to([KD, GI, 3, SEQ]), ACT.Copy)
                    last.then_inc(copied.sem, 1)

                def group(g, more):
                    u, units = g * PAIRS, 3 * PAIRS
                    exp(3 * u + 2, 2)
                    for n in range(units + 1):
                        w, b = 3 * u + n, n % 2
                        if n < units:
                            act.wait_ge(turned.sem, turned.done(w))
                            act.wait_ge(mixed.sem, mixed.freed(w))
                            nc.scalar.activation(self.pt[b], bank[0:G3, 4:6, 0:3 * P].rearrange("p k (g n) -> p k g n", n=P), ACT.Copy).then_inc(p_in.sem, 1)
                        if n + 3 < units:
                            exp(w + 3, n + 3)
                        if more and n == units:
                            copy(g + 1)
                        if n and n % 3 == 0:
                            p = n // 3 - 1
                            act.wait_ge(mixed.sem, mixed.done(w - 1))
                            nc.scalar.activation(zT[0:KF, :, ds(g * GT + 2 * p * SEQ, 2 * SEQ)], bank[0:KF, 7, 0:6 * SEQ].rearrange("p (j n) -> p j n", j=3),
                                                 ACT.Copy).then_inc(o_taken.sem, 1)
                    if more:
                        exp(3 * u + units, 0)
                        exp(3 * u + units + 1, 1)

                copy(0)
                exp(0, 0)
                exp(1, 1)
                groups(act, group)

        class Experts:

            def __init__(self, r, acc):
                self.r, self.acc = r, acc
                name = ("1", "2", "3f")[r]
                c = Carve()
                self.w1 = [c(KD, KT, HIDDEN) for _ in range(2)]
                self.w2 = [c(P, FT, DIM) for _ in range(2)]
                self.hid = [c(P, FT, 512) for _ in range(2)]
                self.logitsT = c(EXPERTS, TOKENS)
                small = lambda: c(P, TILES, EXPERTS)
                self.lg, self.eq, self.oh1, self.oh2, self.lg2 = (small() for _ in range(5))
                self.m1, self.m2, self.first, self.ex, self.g1, self.g2 = (c(P, TILES) for _ in range(6))
                self.router = const("router" + name).rearrange("p (k e) -> p k e", k=KT)
                self.router_bias = const("gate_b") if r == 2 else None
                self.b1 = const("b1_" + name) if r != 1 else None
                self.b2 = const("b2_" + name) if r != 1 else None
                self.w1_dram, self.w2_dram = t_in["w1_" + name], t_in["w2_" + name]
                self.chosen = zT[0:EXPERTS, 0:2, :]
                self.running = arena[0:EXPERTS, self.hid_at():self.hid_at() + 2 * TOKENS].rearrange("p (k n) -> p k n", k=2)
                self.func = ACT.Relu if r == 1 else ACT.Gelu

            def hid_at(self):
                return 2 * KT * HIDDEN + 2 * FT * DIM

            def load(self, sp, e, b):
                sp.dma_start(self.w1[b], self.w1_dram[ds(e, 1)].rearrange("a p k n -> (a p) k n")).then_inc(expert_loaded[b], 16)
                sp.dma_start(self.w2[b], self.w2_dram[ds(e, 1)].rearrange("a p f n -> (a p) f n")).then_inc(expert_loaded[b], 16)

            def sp_first(self, sp):
                for b in range(2):
                    self.load(sp, b, b)

            def sp_rest(self, sp):
                y_sum = cnt("y_sum", EXTRA["y_sum"] + self.r * EXPERTS * TILES)
                with sp.Fori(1, EXPERTS // 2) as i:
                    for b in range(2):
                        sp.wait_ge(y_sum.sem, y_sum.done((2 * i + b - 1) * TILES - 1))
                        self.load(sp, 2 * i + b, b)

            def route_pe(self, pe):
                r = self.r
                summed, taken = cnt("logit_sum", 5 * r), cnt("logit_in", 5 * r)
                for n, (at, width) in enumerate(TGROUPS):
                    pe.wait_ge(taken.sem, taken.freed(n))
                    for m in range(KT):
                        last = nc.tensor.matmul(bank[0:EXPERTS, n % 2, 0:width], self.router[:, m, :], xT[:, m, at:at + width],
                                                start=(m == 0), stop=(m == KT - 1))
                    last.then_inc(summed.sem, 1)
                pe.wait_ge(taken.sem, taken.done(4))
                for t in range(TILES):
                    last = nc.tensor.transpose(bank[:, 2, t * EXPERTS:(t + 1) * EXPERTS], self.logitsT[:, t * P:(t + 1) * P], ident[0:EXPERTS, 0:EXPERTS])
                last.then_inc(cnt("logit_turned").sem, 1)
                pe.wait_ge(cnt("routed").sem, cnt("routed", r).done(0))
                if r == 1:
                    csum, cin = cnt("choice_sum"), cnt("choice_in")
                    for k, one_hot in enumerate((self.oh1, self.oh2)):
                        for n, (at, width) in enumerate(TGROUPS):
                            v = 5 * k + n
                            pe.wait_ge(cin.sem, cin.freed(v))
                            for t in range(at // P, (at + width) // P):
                                last = nc.tensor.transpose(bank[0:EXPERTS, 4 + v % 2, t * P - at:(t + 1) * P - at], one_hot[:, t, :], ident)
                            last.then_inc(csum.sem, 1)
                    pe.wait_ge(cnt("keep_turned").sem, cnt("keep_turned").done(0))
                    for t in range(TILES):
                        last = nc.tensor.transpose(bank[:, 3, t * EXPERTS:(t + 1) * EXPERTS], self.logitsT[:, t * P:(t + 1) * P], ident[0:EXPERTS, 0:EXPERTS])
                    last.then_inc(cnt("keep_turned").sem, 1)
                    return
                turned, cin = cnt("cw_turned", 5 * (r // 2)), cnt("cw_in", 5 * (r // 2))
                for n, (at, width) in enumerate(TGROUPS):
                    pe.wait_ge(cin.sem, cin.freed(n))
                    for t in range(at // P, (at + width) // P):
                        last = nc.tensor.transpose(bank[0:EXPERTS, 4 + n % 2, t * P - at:(t + 1) * P - at], gates[:, t * EXPERTS:(t + 1) * EXPERTS], ident)
                    last.then_inc(turned.sem, 1)
                pe.wait_ge(cin.sem, cin.done(4))
                b2_sum, b2_added = cnt("b2_sum", TILES * (r // 2)), cnt("b2_added", TILES * (r // 2))
                for t in range(TILES):
                    pe.wait_ge(b2_added.sem, b2_added.freed(t))
                    nc.tensor.matmul(bank[:, 6 + t % 2, 0:DIM], self.logitsT[:, t * P:(t + 1) * P], self.b2, start=True, stop=True).then_inc(b2_sum.sem, 1)

            def route_act(self, act):
                r = self.r
                summed, taken = cnt("logit_sum", 5 * r), cnt("logit_in", 5 * r)
                for n, (at, width) in enumerate(TGROUPS):
                    act.wait_ge(summed.sem, summed.done(n))
                    nc.scalar.activation(self.logitsT[:, at:at + width], bank[0:EXPERTS, n % 2, 0:width], ACT.Identity,
                                         bias=self.router_bias if r == 2 else 0.0).then_inc(taken.sem, 1)
                act.wait_ge(cnt("exp_in").sem, cnt("exp_in", r).done(0))
                x = self.lg if r == 1 else self.ex
                nc.scalar.activation(x, x, ACT.Exp).then_inc(cnt("exp_out").sem, 1)
                if r == 1:
                    csum, cin = cnt("choice_sum"), cnt("choice_in")
                    for k in range(2):
                        for n, (at, width) in enumerate(TGROUPS):
                            v = 5 * k + n
                            act.wait_ge(csum.sem, csum.done(v))
                            nc.scalar.activation(self.chosen[:, k, at:at + width], bank[0:EXPERTS, 4 + v % 2, 0:width], ACT.Copy).then_inc(cin.sem, 1)
                    return
                turned, cin = cnt("cw_turned", 5 * (r // 2)), cnt("cw_in", 5 * (r // 2))
                for n, (at, width) in enumerate(TGROUPS):
                    act.wait_ge(turned.sem, turned.done(n))
                    nc.scalar.activation(self.logitsT[:, at:at + width], bank[0:EXPERTS, 4 + n % 2, 0:width], ACT.Copy).then_inc(cin.sem, 1)

            def route_dve(self, dve, ch):
                r = self.r
                wide = [P, TILES, EXPERTS]
                spread = lambda x: x.unsqueeze(2).broadcast_to(wide)
                order = const("descending").unsqueeze(1).broadcast_to(wide)
                V = nc.vector

                def do(ins):
                    ch.step(ins)
                    ch.settle()

                def choose(values, peak, one_hot):
                    do(V.tensor_reduce(peak, values, AX_X, ALU.max))
                    do(V.tensor_tensor(self.eq, values, spread(peak), ALU.is_equal))
                    do(V.tensor_tensor(self.eq, self.eq, order, ALU.mult))
                    do(V.tensor_reduce(self.first, self.eq, AX_X, ALU.max))
                    do(V.tensor_tensor(one_hot, self.eq, spread(self.first), ALU.is_equal))

                dve.wait_ge(cnt("logit_turned").sem, cnt("logit_turned", r).done(0))
                do(V.tensor_copy(self.lg, bank[:, 2, 0:TILES * EXPERTS].rearrange("p (t e) -> p t e", e=EXPERTS)))
                if r == 1:
                    do(V.tensor_reduce(self.m1, self.lg, AX_X, ALU.max))
                    V.tensor_tensor(self.lg, self.lg, spread(self.m1), ALU.subtract).then_inc(cnt("exp_in").sem, 1)
                    dve.wait_ge(cnt("exp_out").sem, cnt("exp_out", r).done(0))
                    do(V.tensor_reduce(self.m2, self.lg, AX_X, ALU.add))
                    do(V.reciprocal(self.m2, self.m2))
                    do(V.tensor_tensor(self.lg, self.lg, spread(self.m2), ALU.mult))
                choose(self.lg, self.m1, self.oh1)
                do(V.scalar_tensor_tensor(self.lg2, self.oh1, MASKED, self.lg, ALU.mult, ALU.add))
                choose(self.lg2, self.m2, self.oh2)
                if r == 1:
                    g1, g2 = self.m1, self.m2
                else:
                    V.tensor_tensor(self.ex, self.m2, self.m1, ALU.subtract).then_inc(cnt("exp_in").sem, 1)
                    dve.wait_ge(cnt("exp_out").sem, cnt("exp_out", r).done(0))
                    do(V.tensor_scalar(self.g1, self.ex, 1.0, None, ALU.add))
                    do(V.reciprocal(self.g1, self.g1))
                    do(V.tensor_tensor(self.g2, self.ex, self.g1, ALU.mult))
                    g1, g2 = self.g1, self.g2
                gates3 = gates[:, :].rearrange("p (t e) -> p t e", e=EXPERTS)
                do(V.tensor_tensor(gates3, self.oh1, spread(g1), ALU.mult))
                do(V.tensor_tensor(self.eq, self.oh2, spread(g2), ALU.mult))
                do(V.tensor_tensor(gates3, gates3, self.eq, ALU.add))
                dve.sem_inc(cnt("routed").sem, 1)
                if r == 1:
                    dve.wait_ge(cnt("choice_in").sem, cnt("choice_in").done(9))
                    count_on = const("ones")[0:EXPERTS, 0:1].broadcast_to([EXPERTS, GT])
                    for k in range(2):
                        for g in range(GROUPS):
                            start = 0.0 if k == 0 else self.running[:, 0, (g + 1) * GT - 1:(g + 1) * GT]
                            ch.step(V.tensor_tensor_scan(self.running[:, k, g * GT:(g + 1) * GT], count_on,
                                                         self.chosen[:, k, g * GT:(g + 1) * GT], start, ALU.mult, ALU.add))
                        ch.settle()
                    do(V.scalar_tensor_tensor(self.running, self.running, float(CAPACITY), self.chosen, ALU.is_le, ALU.mult))
                    V.tensor_tensor(self.logitsT, self.running[:, 0], self.running[:, 1], ALU.add).then_inc(cnt("keep_turned").sem, 1)
                    dve.wait_ge(cnt("keep_turned").sem, cnt("keep_turned").done(1))
                    do(V.tensor_tensor(gates[:, :], gates[:, :], bank[:, 3, 0:TILES * EXPERTS], ALU.mult))
                    return
                b2_sum, b2_added = cnt("b2_sum", TILES * (r // 2)), cnt("b2_added", TILES * (r // 2))
                for t in range(TILES):
                    dve.wait_ge(b2_sum.sem, b2_sum.done(t))
                    V.tensor_tensor(tile_h(self.acc, t), tile_h(self.acc, t), bank[:, 6 + t % 2, 0:DIM], ALU.add).then_inc(b2_added.sem, 1)

            def pe(self, pe):
                H0, Y0 = self.r * EXPERTS * 5 * FT, self.r * EXPERTS * TILES
                h_sum, h_ready = cnt("h_sum", H0), cnt("h_ready", EXTRA["h_ready"] + H0)
                y_sum, y_added = cnt("y_sum", EXTRA["y_sum"] + Y0), cnt("y_added", Y0)

                def first(e, b, j):
                    at, width = TGROUPS[j]
                    for f in range(FT):
                        n = (5 * FT) * e + FT * j + f
                        pe.wait_ge(h_ready.sem, h_ready.done(n - 4))
                        for m in range(KT):
                            last = nc.tensor.matmul(bank[:, (5 * FT * b + FT * j + f) % 4, 0:width], self.w1[b][:, m, f * P:(f + 1) * P],
                                                    xT[:, m, at:at + width], start=(m == 0), stop=(m == KT - 1))
                        last.then_inc(h_sum.sem, 1)

                def second(e, b, j):
                    at, width = TGROUPS[j]
                    pe.wait_ge(h_ready.sem, h_ready.done((5 * FT) * e + FT * j + FT - 1))
                    for t in range(at // P, (at + width) // P):
                        pe.wait_ge(y_added.sem, y_added.freed(e * TILES + t))
                        for f in range(FT):
                            last = nc.tensor.matmul(bank[:, 4 + (b + t) % 2, 0:DIM], self.hid[(b + j) % 2][:, f, t * P - at:(t + 1) * P - at],
                                                    self.w2[b][:, f, :], start=(f == 0), stop=(f == FT - 1))
                        last.then_inc(y_sum.sem, 1)

                with pe.Fori(0, EXPERTS // 2) as i:
                    for b in range(2):
                        e = 2 * i + b
                        pe.wait_ge(expert_loaded[b], 32 * i + 32 * (1 + self.r * EXPERTS // 2))
                        first(e, b, 0)
                        for j in range(5):
                            if j + 1 < 5:
                                first(e, b, j + 1)
                            second(e, b, j)

            def act(self, act):
                H0, Y0 = self.r * EXPERTS * 5 * FT, self.r * EXPERTS * TILES
                h_sum, h_ready, y_sum = cnt("h_sum", H0), cnt("h_ready", EXTRA["h_ready"] + H0), cnt("y_sum", EXTRA["y_sum"] + Y0)
                for e, b in ring(act, EXPERTS):
                    for j, (at, width) in enumerate(TGROUPS):
                        back, gone = (0, j - 2) if j >= 2 else (1, j + 3)
                        act.wait_ge(y_sum.sem, y_sum.done((e - back) * TILES + sum(TGROUPS[gone]) // P - 1))
                        for f in range(FT):
                            n = 5 * FT * e + FT * j + f
                            wait_apart(act, h_sum.sem, h_sum.done(n))
                            bias = self.b1[:, ds(e * FT + f, 1)] if self.b1 is not None else 0.0
                            nc.scalar.activation(self.hid[(b + j) % 2][:, f, 0:width], bank[:, (5 * FT * b + FT * j + f) % 4, 0:width],
                                                 self.func, bias=bias).then_inc(h_ready.sem, 1)

            def dve(self, dve):
                Y0 = self.r * EXPERTS * TILES
                y_sum, y_added = cnt("y_sum", EXTRA["y_sum"] + Y0), cnt("y_added", Y0)
                for e, b in ring(dve, EXPERTS):
                    for t in range(TILES):
                        n = e * TILES + t
                        dve.wait_ge(y_sum.sem, y_sum.done(n))
                        dve.wait_ge(y_added.sem, y_added.freed(n))
                        nc.vector.scalar_tensor_tensor(tile_h(self.acc, t), bank[:, 4 + (b + t) % 2, 0:DIM], gates[:, ds(e + t * EXPERTS, 1)],
                                                       tile_h(self.acc, t), ALU.mult, ALU.add).then_inc(y_added.sem, 1)

        def quant_dve(dve, ch):
            q = quantised
            half = TOKENS // 2
            for m in range(KT):
                for s in range(2):
                    x = xT[:, m, s * half:(s + 1) * half]
                    ch.step(nc.vector.tensor_scalar(x, x, -128.0, 127.0, ALU.max, ALU.min))
                    ch.settle()
                    ch.step(nc.vector.tensor_scalar(q[:, m, s * half:(s + 1) * half], x, MAGIC, MAGIC, ALU.add, ALU.subtract))
            ch.step(nc.vector.tensor_copy(weight_q, w_int8[:, :].bitcast(I8).rearrange("p (k n) -> p k n", k=KT)))
            ch.settle()
            dve.sem_inc(cnt("quant").sem, 1)
            done, added = cnt("proj_sum", TILES * PROJ["L0f"]), cnt("proj_added", TILES * PROJ["L0f"])
            for t, b in ring(dve, TILES, ch, 1):
                dve.wait_ge(done.sem, done.done(t))
                ch.step(nc.vector.scalar_tensor_tensor(quant_out[b], bank[:, b, 0:DIM], float(np.float32(0.02 * 0.01)), const("bias_int8"), ALU.mult, ALU.add))
                ch.settle()
                nc.vector.tensor_tensor(tile_h(h, t), tile_h(h, t), quant_out[b], ALU.add).then_inc(added.sem, 1)

        def quant_pe(pe):
            pe.wait_ge(cnt("quant").sem, cnt("quant").done(0))
            done, added = cnt("proj_sum", TILES * PROJ["L0f"]), cnt("proj_added", TILES * PROJ["L0f"])
            for t, b in ring(pe, TILES):
                pe.wait_ge(added.sem, added.freed(t))
                for m in range(KT):
                    last = nc.tensor.matmul(bank[:, b, 0:DIM], quantised[:, m, ds(t * P, P)], weight_q[:, m, :], start=(m == 0), stop=(m == KT - 1))
                last.then_inc(done.sem, 1)

        qc = Carve()
        quantised = qc(KD, TOKENS).bitcast(BF16).rearrange("p (k n) -> p k n", k=KT)
        weight_q = qc(KD, DIM).bitcast(BF16).rearrange("p (k n) -> p k n", k=KT)
        quant_out = [qc(P, DIM) for _ in range(2)]

        class StateSpace:
            def __init__(self):
                c = Carve()
                wide = lambda: c(P, CI, GT)
                self.acc, self.sig = wide(), wide()
                self.x2 = self.sig
                quarter = lambda n: kept[:, n * CI * GT:(n + 1) * CI * GT].rearrange("p (c n) -> p c n", c=CI)
                self.x, self.z, self.dt, self.tmp = (quarter(n) for n in range(4))
                self.w3, self.dt3 = c(P, CI, GI, 3, SEQ), c(P, CI, GI, 3, SEQ)
                parts3, single = c(P, GI, 3, SEQ), c(P, GT)
                r = Carve(rounded)
                low_and_q = r(P, GT)
                self.k3, self.kk3 = parts3[0:STATE], parts3[32:32 + STATE]
                self.k, self.k_squared, self.q = single[0:STATE], single[32:32 + STATE], single[64:64 + STATE]
                self.low, self.q_high, self.q_low = c(RANK, GT), low_and_q[64:64 + STATE], low_and_q[96:96 + STATE]
                self.q_parts = low_and_q[64:P]
                self.pick = r(P, STATE)[64:P]
                self.kk = normed[:, :, :].rearrange("p a b -> p (a b)")[:, 0:GT]
                self.n1, self.n2 = (wte_sum[:, n * GT:(n + 1) * GT] for n in range(2))
                spare = ztile[:, :, :].rearrange("p a b -> p (a b)")
                self.n3, self.n4 = (spare[:, n * GT:(n + 1) * GT] for n in range(2))
                at = c.at
                self.qb = c(P, STATE, GT)
                self.xp = arena[:, at:at + CI * GI * (SEQ + 3)].rearrange("p (c i t) -> p c i t", c=CI, t=SEQ + 3)
                self.lists = [r(G3, 2 * CI * P) for _ in range(2)]
                self.keys = [c(G3, 2 * STATE) for _ in range(2)]
                self.spread_k = [r(G3, STATE, SEQ) for _ in range(2)]
                self.spread_kk = [r(G3, STATE, SEQ) for _ in range(2)]
                self.decay = [c(P, STATE * SEQ) for _ in range(2)]
                self.state = [c(P, STATE * SEQ) for _ in range(STATES)]
                self.w_in = const("in_proj").rearrange("p (k n) -> p k n", k=KT)
                self.w_x = const("x_proj").rearrange("p (c n) -> p c n", c=CI)
                self.w_dt = const("dt_head")
                self.conv_w = const("conv_w").rearrange("p (c j) -> p c j", c=CI)
                self.conv_b, self.dt_b, self.d = const("conv_b"), const("dt_b"), const("d")

            def pool(self, pool, ch):
                for b in range(2):
                    ch.step(nc.gpsimd.memset(self.decay[b], 0.0))
                ch.settle()
                ch.step(nc.gpsimd.tensor_scalar(self.q_parts.bitcast(F32R), ident[64:P, 0:1].broadcast_to([64, GT]), 0.0, None, ALU.mult))
                ch.settle()
                ch.step(nc.gpsimd.tensor_tensor(self.pick.bitcast(F32R), ident[64:P, 64:64 + STATE], ident[64:P, 96:96 + STATE], ALU.add))
                ch.settle()
                pool.sem_inc(cnt("prepared").sem, 1)
                lists_in, spread = cnt("lists_in"), cnt("lists_spread")
                scanned, weighed, q_in = cnt("scanned"), cnt("weighed"), cnt("q_in")
                shape = [G3, STATE, SEQ]

                def build(image, b):
                    pool.wait_ge(lists_in.sem, lists_in.done(image))
                    nc.gpsimd.tensor_tensor(self.spread_k[b].bitcast(F32R), self.keys[b][:, 0:STATE].unsqueeze(2).broadcast_to(shape),
                                            const("upto").unsqueeze(1).broadcast_to(shape), ALU.mult).then_inc(spread.sem, 1)

                with pool.Fori(0, GROUPS) as g:
                    first = g * GI
                    build(first, 0)
                    pool.wait_ge(q_in.sem, q_in.done(STATE * g + STATE - 1))
                    for img in range(GI):
                        for c in range(CI):
                            n = CI * img + c
                            v = CI * first + n
                            if c == 1 and img + 1 < GI:
                                build(first + img + 1, (img + 1) % 2)
                            pool.wait_ge(scanned.sem, scanned.done(v))
                            st = self.state[n % STATES].rearrange("p (n t) -> p n t", t=SEQ)
                            nc.gpsimd.tensor_tensor(st, st, self.qb[:, :, img * SEQ:(img + 1) * SEQ], ALU.mult).then_inc(weighed.sem, 1)

            def pe(self, pe):
                pe.wait_ge(cnt("prepared").sem, cnt("prepared", 1).done(0))
                C = {n: cnt(n) for n in COUNTS}
                wait = lambda n, k: pe.wait_ge(C[n].sem, C[n].done(k))
                freed = lambda n, k: pe.wait_ge(C[n].sem, C[n].freed(k))
                inc = lambda ins, n: ins.then_inc(C[n].sem, 1)
                flat = lambda x: x.rearrange("p a b -> p (a b)")

                def turn(image, img):
                    wait("lists_in", image - 1)
                    three = lambda x: x.rearrange("p a b -> p (a b)")
                    for c in range(CI):
                        nc.tensor.transpose(bank[0:G3, 6, c * P:(c + 1) * P], three(self.w3[:, c, img]), ident)
                    for c in range(CI):
                        nc.tensor.transpose(bank[0:G3, 7, c * P:(c + 1) * P], three(self.dt3[:, c, img]), ident)
                    nc.tensor.transpose(bank[0:G3, 6, CI * P:CI * P + STATE], three(self.k3[:, img]), ident[0:STATE, 0:STATE])
                    last = nc.tensor.transpose(bank[0:G3, 7, CI * P:CI * P + STATE], three(self.kk3[:, img]), ident[32:32 + STATE, 32:32 + STATE])
                    inc(last, "lists_turned")

                with pe.Fori(0, GROUPS) as g:
                    first = g * GI
                    wait("reduced", 6 * PAIRS * g - 1)
                    wait("a_in", 12 * PAIRS * g - 1)
                    for m in range(6):
                        if m == 2:
                            wait("in_taken", 6 * g)
                        for kk in range(KT):
                            last = nc.tensor.matmul(bank[:, IN_BANK[m], 0:GT], self.w_in[:, kk, m * P:(m + 1) * P], xT[:, kk, ds(g * GT, GT)],
                                                    start=(kk == 0), stop=(kk == KT - 1))
                        inc(last, "in_sum")
                    wait("x_ready", g)
                    for c in range(CI):
                        last = nc.tensor.matmul(bank[0:XP_COLS, 1, 0:GT], self.w_x[:, c, :], self.x[:, c, :], start=(c == 0), stop=(c == CI - 1))
                    inc(last, "low_sum")
                    wait("low_in", g)
                    wait("q_in", STATE * g - 1)
                    for c in range(CI):
                        last = nc.tensor.matmul(bank[:, 5 + c, 0:GT], self.w_dt[:, c * P:(c + 1) * P], self.low, start=True, stop=True)
                    inc(last, "dt_sum")
                    wait("in_taken", 6 * g + 5)
                    inc(nc.tensor.matmul(bank[:, 0, 0:GT], ones[32:32 + STATE, 0:P], self.k_squared, start=True, stop=True), "k2_sum")
                    wait("dt_gate", g)
                    wait("q_split", g)
                    for n in range(STATE):
                        freed("q_in", STATE * g + n)
                        inc(nc.tensor.matmul(bank[:, 6 + n % 2, 0:GT], self.pick[:, n:n + 1].broadcast_to([2 * 32, P]).bitcast(F32R), self.q_parts.bitcast(F32R), start=True, stop=True), "q_sum")
                    wait("dx_squared", g)
                    for c in range(CI):
                        last = nc.tensor.matmul(bank[:, 1, 0:GT], ones[:, 0:P], self.tmp[:, c, :], start=(c == 0), stop=(c == CI - 1))
                    inc(last, "dx_sum")
                    wait("w_ready", g)
                    wait("q_in", STATE * g + STATE - 1)
                    turn(first, 0)
                    for img in range(GI):
                        b = img % 2
                        wait("lists_spread", first + img)
                        wait("squares_spread", first + img)
                        for c in range(CI):
                            n = CI * img + c
                            v = CI * first + n
                            wait("scanned", v - 2)
                            for half in range(2):
                                nc.tensor.matmul(bank[:, 2 * (n % 2) + half, 0:GT], self.lists[b][:, c * P:(c + 1) * P].bitcast(F32R),
                                                 flat(self.spread_k[b])[:, half * GT:(half + 1) * GT].bitcast(F32R), start=True, stop=True)
                            for half in range(2):
                                wait("a_in", 2 * v - 2 + half)
                                last = nc.tensor.matmul(bank[:, 4 + half, 0:GT], self.lists[b][:, (CI + c) * P:(CI + c + 1) * P].bitcast(F32R),
                                                        flat(self.spread_kk[b])[:, half * GT:(half + 1) * GT].bitcast(F32R), start=True, stop=True)
                                inc(last, "v_expanded")
                            if c == 0 and img + 1 < GI:
                                turn(first + img + 1, img + 1)

            def act(self, act):
                act.wait_ge(cnt("prepared").sem, cnt("prepared", 1).done(0))
                C = {n: cnt(n) for n in COUNTS}
                wait = lambda n, k: act.wait_ge(C[n].sem, C[n].done(k))
                inc = lambda ins, n: ins.then_inc(C[n].sem, 1)
                A = nc.scalar.activation
                images = lambda x: x.rearrange("p (i t) -> p i t", t=SEQ)

                def lists(image, b):
                    wait("lists_turned", image)
                    n = CI * P
                    A(self.lists[b].bitcast(F32R).rearrange("p (k n) -> p k n", k=2), bank[0:G3, 6:8, 0:n], ACT.Copy)
                    inc(A(self.keys[b].rearrange("p (k n) -> p k n", k=2), bank[0:G3, 6:8, n:n + STATE], ACT.Copy), "lists_in")

                with act.Fori(0, GROUPS) as g:
                    first = g * GI
                    for m in range(6):
                        wait("in_sum", 6 * g + m)
                        psum = bank[:, IN_BANK[m], 0:GT]
                        if m < CI:
                            inc(A(self.xp[:, m, :, 3:], images(psum), ACT.Copy), "in_taken")
                        else:
                            inc(A(self.tmp[:, m - CI, :], psum, ACT.Sigmoid), "z_gate")
                    wait("conv_out", g)
                    inc(A(self.sig, self.acc, ACT.Sigmoid), "conv_gate")
                    wait("low_sum", g)
                    A(self.low, bank[XP_AT[0]:XP_AT[0] + RANK, 1, 0:GT], ACT.Copy)
                    A(self.k, bank[XP_AT[1]:XP_AT[1] + STATE, 1, 0:GT], ACT.Copy)
                    A(self.k_squared, bank[XP_AT[1]:XP_AT[1] + STATE, 1, 0:GT], ACT.Square)
                    inc(A(self.q, bank[XP_AT[2]:XP_AT[2] + STATE, 1, 0:GT], ACT.Copy), "low_in")
                    wait("dt_sum", g)
                    for c in range(CI):
                        last = A(self.dt[:, c, :], bank[:, 5 + c, 0:GT], ACT.Sigmoid, bias=self.dt_b[:, c:c + 1])
                    inc(last, "dt_gate")
                    wait("k2_sum", g)
                    inc(A(self.kk, bank[:, 0, 0:GT], ACT.Copy), "k2_in")
                    for n in range(STATE):
                        wait("q_sum", STATE * g + n)
                        if n == 0:
                            wait("weighed", 6 * PAIRS * g - 1)
                        inc(A(self.qb[:, n, :], bank[:, 6 + n % 2, 0:GT], ACT.Copy), "q_in")
                    wait("dx_ready", g)
                    inc(A(self.tmp, self.x2, ACT.Square), "dx_squared")
                    wait("norm_in", g)
                    inc(A(self.n2, self.n1, ACT.Sqrt), "norm_out")
                    lists(first, 0)
                    for img in range(GI):
                        for c in range(CI):
                            n = CI * img + c
                            v = CI * first + n
                            for half in range(2):
                                wait("v_expanded", 2 * v + half)
                                if half == 0:
                                    wait("scanned", v - 2)
                                inc(A(self.decay[n % 2].rearrange("p (k n t) -> p k n t", k=2, t=SEQ)[:, half, :, 1:],
                                      bank[:, 4 + half, 0:GT].rearrange("p (n t) -> p n t", t=SEQ)[:, :, 1:],
                                      ACT.Copy, scale=-1.0 / FADE, bias=1.0 / FADE), "a_in")
                            if c == 0 and img + 1 < GI:
                                lists(first + img + 1, (img + 1) % 2)

            def dve(self, dve, ch):
                dve.wait_ge(cnt("prepared").sem, cnt("prepared", 1).done(0))
                C = {n: cnt(n) for n in COUNTS}
                wait = lambda n, k: dve.wait_ge(C[n].sem, C[n].done(k))
                inc = lambda ins, n: ins.then_inc(C[n].sem, 1)
                V = nc.vector
                images = lambda x: x.rearrange("p (i t) -> p i t", t=SEQ)

                def do(ins):
                    ch.step(ins)
                    ch.settle()

                all_c = lambda x: x.unsqueeze(1).broadcast_to([P, CI, GT])
                def split(parts, x):
                    for dst, k in parts:
                        if k == "high":
                            ch.step(V.tensor_copy(dst.bitcast(F32R), x))
                            high = dst
                    ch.settle()
                    for dst, k in parts:
                        if k == "low":
                            ch.step(V.tensor_tensor(dst.bitcast(F32R), x, high, ALU.subtract))

                values = lambda x: [(x[:, :, 0], "high"), (x[:, :, 1], "high"), (x[:, :, 2], "low")]
                keys = lambda x: [(x[:, :, 0], "high"), (x[:, :, 1], "low"), (x[:, :, 2], "high")]

                with ch.loop(GROUPS, SSM_STEPS) as g:
                    first = g * GI
                    for c in range(CI):
                        ch.step(V.memset(self.xp[:, c, :, 0:3], 0.0))
                    ch.settle()
                    wait("in_taken", 6 * g + 2)
                    for j in range(4):
                        for c in range(CI):
                            src, acc, w = self.xp[:, c, :, j:j + SEQ], images(self.acc[:, c, :]), self.conv_w[:, c, j:j + 1]
                            if j == 0:
                                ch.step(V.tensor_scalar(acc, src, w, self.conv_b[:, c:c + 1], ALU.mult, ALU.add))
                            else:
                                ch.step(V.scalar_tensor_tensor(acc, src, w, acc, ALU.mult, ALU.add))
                        ch.settle()
                    dve.sem_inc(C["conv_out"].sem, 1)
                    wait("conv_gate", g)
                    inc(V.tensor_tensor(self.x, self.acc, self.sig, ALU.mult), "x_ready")
                    for m in range(CI, 6):
                        wait("z_gate", CI * g + m - CI)
                        inc(V.tensor_tensor(self.z[:, m - CI, :], bank[:, IN_BANK[m], 0:GT], self.tmp[:, m - CI, :], ALU.mult), "in_taken")
                    wait("low_in", g)
                    split(keys(self.k3), images(self.k))
                    split(keys(self.kk3), images(self.k_squared))
                    do(V.tensor_tensor(images(self.q), images(self.q), const("fall")[64:64 + STATE].unsqueeze(1).broadcast_to([STATE, GI, SEQ]), ALU.mult))
                    split([(self.q_high, "high"), (self.q_low, "low")], self.q)
                    ch.settle()
                    dve.sem_inc(C["q_split"].sem, 1)
                    wait("dt_gate", g)
                    wait("k2_in", g)
                    wait("in_taken", 6 * g + 5)
                    do(V.tensor_tensor(self.tmp, self.dt, all_c(self.kk), ALU.mult))
                    do(V.tensor_scalar(self.tmp, self.tmp, 1.0, None, ALU.add))
                    do(V.reciprocal(self.tmp, self.tmp))
                    do(V.tensor_tensor(self.dt, self.dt, self.tmp, ALU.mult))
                    do(V.tensor_tensor(self.x2, self.dt, self.x, ALU.mult))
                    dve.sem_inc(C["dx_ready"].sem, 1)
                    for c in range(CI):
                        split(values(self.dt3[:, c]), images(self.dt[:, c, :]))
                    wait("dx_sum", g)
                    inc(V.tensor_tensor(self.n1, bank[:, 1, 0:GT], self.kk, ALU.mult), "norm_in")
                    wait("norm_out", g)
                    do(V.tensor_scalar(self.n3, self.n2, 1e-7, None, ALU.add))
                    do(V.reciprocal(self.n3, self.n3))
                    do(V.tensor_tensor(self.n2, self.n2, self.n3, ALU.mult))
                    do(V.tensor_tensor(self.n2, self.n2, self.n2, ALU.mult))
                    do(V.tensor_scalar(self.n4, self.n2, 2.0315, -4.775, ALU.mult, ALU.add))
                    do(V.tensor_tensor(self.n4, self.n4, self.n2, ALU.mult))
                    do(V.scalar_tensor_tensor(self.n4, self.n4, 3.4445, self.n3, ALU.add, ALU.mult))
                    do(V.tensor_tensor(images(self.n4), images(self.n4), const("rise").unsqueeze(1).broadcast_to([P, GI, SEQ]), ALU.mult))
                    do(V.tensor_tensor(self.x2, self.x2, all_c(self.n4), ALU.mult))
                    for c in range(CI):
                        split(values(self.w3[:, c]), images(self.x2[:, c, :]))
                    ch.settle()
                    dve.sem_inc(C["w_ready"].sem, 1)

                    def reduce(v, n):
                        img, c = divmod(n, CI)
                        wait("weighed", v)
                        inc(V.tensor_reduce(self.acc[:, c, img * SEQ:(img + 1) * SEQ], self.state[n % STATES].rearrange("p (n t) -> p t n", t=SEQ), AX_X, ALU.add), "reduced")

                    def build(img):
                        shape = [G3, STATE, SEQ]
                        wait("lists_in", first + img)
                        inc(V.tensor_tensor(self.spread_kk[img % 2].bitcast(F32R), self.keys[img % 2][:, STATE:].unsqueeze(2).broadcast_to(shape),
                                            const("own").unsqueeze(1).broadcast_to(shape), ALU.mult), "squares_spread")

                    build(0)
                    for n in range(CI * GI):
                        v, b = CI * first + n, n % 2
                        if n % CI == 1 and n // CI + 1 < GI:
                            build(n // CI + 1)
                        wait("a_in", 2 * v + 1)
                        if n >= STATES:
                            wait("reduced", v - STATES)
                        for half in range(2):
                            last = V.tensor_tensor_scan(self.state[n % STATES][:, half * GT:(half + 1) * GT], self.decay[b][:, half * GT:(half + 1) * GT],
                                                        bank[:, 2 * b + half, 0:GT], 0.0, ALU.mult, ALU.add)
                        inc(last, "scanned")
                        if n >= 2:
                            reduce(v - 2, n - 2)
                    for n in (CI * GI - 2, CI * GI - 1):
                        reduce(CI * first + n, n)
                    wait("reduced", CI * first + CI * GI - 1)
                    for c in range(CI):
                        ch.step(V.scalar_tensor_tensor(self.acc[:, c, :], self.x[:, c, :], self.d[:, c:c + 1], self.acc[:, c, :], ALU.mult, ALU.add))
                    ch.settle()
                    do(V.tensor_tensor(zT[:, :, ds(g * GT, GT)], self.acc, self.z, ALU.mult))

        layer0, layer1, layer2, layer3 = Tokens12(), Heads16(0, "L1", True), StateSpace(), Parts8()
        layer3f = Heads16(3, "L3f", False)
        experts = [Experts(0, h), Experts(1, h), Experts(2, kept)]
        weight_of = lambda n, kt: const(n).rearrange("p (k n) -> p k n", k=kt)
        credit_share = {e: COUNTS[i::4] for i, e in enumerate(("sp", "act", "pe", "dve"))}

        def credits(eng, name):
            for n in credit_share[name]:
                eng.sem_inc(counts[n].sem, CREDITS + EXTRA.get(n, 0))

        slow_ended = sem("slow_ended")

        class Stages:

            def __init__(self, eng, slow=False):
                self.eng, self.k, self.slow = eng, 0, slow

            def end(self):
                own, k = (slow_ended if self.slow else stage_ended), self.k
                self.eng.drain().then_inc(own, 1)
                self.eng.wait_ge(stage_ended, 3 * (k + 1))
                if k == 0 or k >= SLOW_FROM:
                    self.eng.wait_ge(slow_ended, 2 if k == 0 else 2 * (k - SLOW_FROM + 2))
                self.k = SLOW_FROM if self.slow and k == 0 else k + 1

            def skip(self, n):
                for _ in range(n):
                    self.end()

        block = ctx.enter_context(nc.Block())

        @block.sync
        def _(sp):
            stage = Stages(sp, slow=True)
            credits(sp, "sp")
            sp.dma_start(w_emb, t_in["w_emb"]).then_inc(load_early, 16)
            sp.dma_start(select38, t_in["select38"]).then_inc(load_early, 16)
            sp.dma_start(rows_a[0:1, :], t_in["cls_tok"]).then_inc(load_early, 16)
            sp.dma_start(rows_a[1:SEQ, :], t_in["pos"]).then_inc(load_early, 16)
            sp.dma_start(rows_b[1:2, :], t_in["cls_token"]).then_inc(load_early, 16)
            sp.dma_start(rows_b[2:SEQ, :], t_in["b_emb"].broadcast_to([SEQ - 2, DIM])).then_inc(load_early, 16)
            stage.end()
            sp.dma_start(wte_tail, t_in["wte"][WTE_ROWS - WTE_TAIL:WTE_ROWS, :]).then_inc(load_tail, 16)
            with sp.Fori(0, TILES // 2) as i:
                for b in range(2):
                    patch_load(sp, 2 * i + b, b)
                    wte_load(sp, 2 * i + b, b)
            patch_load(sp, TILES - 1, 0)
            sp.dma_start(resident[:, :], t_in["resident"]).then_inc(load_resident, 16)
            sp.dma_start(w_int8[:, :], t_in["w_int8"]).then_inc(load_resident, 16)
            sp.wait_ge(cnt("patch_taken").sem, cnt("patch_taken").done(TILES - 1))
            sp.dma_start(layer0.wo.rearrange("p n e -> p (n e)"), t_in["wo0"]).then_inc(load_wo, 16)
            with sp.Fori(TILES // 2, WTE_CH // 2) as i:
                for b in range(2):
                    wte_load(sp, 2 * i + b, b)
            stage.skip(11 - SLOW_FROM)
            experts[0].sp_first(sp)
            stage.skip(2)
            experts[0].sp_rest(sp)
            stage.skip(4)
            experts[1].sp_first(sp)
            stage.skip(2)
            experts[1].sp_rest(sp)
            stage.skip(7)
            experts[2].sp_first(sp)
            stage.skip(2)
            experts[2].sp_rest(sp)
            stage.skip(2)
            sp.dma_start(out.rearrange("i s e -> (i s) e").rearrange("(t p) e -> p t e", p=P),
                         h[:, :].rearrange("p (t e) -> p t e", e=DIM)).then_inc(stored, 16)
            sp.wait_ge(stored, 16)

        @block.gpsimd
        def _(pool):
            ch = Chain(pool, chains["pool"])
            stage = Stages(pool, slow=True)
            stage.end()
            wte_pool(pool, ch)
            stage.skip(2)
            stage.skip(4)
            layer1.pool(pool, ch)
            stage.end()
            stage.skip(5)
            layer2.pool(pool, ch)
            stage.end()
            stage.skip(5)
            layer3.pool(pool, ch)
            stage.end()
            stage.skip(2)
            layer3f.pool(pool, ch)
            stage.end()
            stage.skip(5)

        @block.scalar
        def _(act):
            ch = Chain(act, chains["act"])
            stage = Stages(act)
            credits(act, "act")
            stage.skip(2)
            act.wait_ge(load_resident, 32)
            ln_act(act, 0, turn=False)
            ln_act(act, 1, gain=const("ln_w"))
            stage.end()
            layer0.act(act, ch)
            stage.end()
            layer0.offset_act(act)
            stage.skip(2)
            ln_act(act, 2, scale=50.0)
            stage.skip(2)
            ln_act(act, 3)
            stage.end()
            layer1.act(act)
            stage.skip(2)
            ln_act(act, 4)
            stage.end()
            experts[0].route_act(act)
            stage.end()
            experts[0].act(act)
            stage.end()
            ln_act(act, 5)
            stage.end()
            layer2.act(act)
            stage.skip(2)
            ln_act(act, 6)
            stage.end()
            experts[1].route_act(act)
            stage.end()
            experts[1].act(act)
            stage.end()
            ln_act(act, 7)
            stage.end()
            layer3.act(act)
            stage.skip(2)
            ln_act(act, 8, turn=False)
            ln_act(act, 9, gain=const("ln1_g"), shift=const("ln1_b"))
            stage.end()
            layer3f.act(act)
            stage.skip(2)
            ln_act(act, 10, gain=const("ln2_g"), shift=const("ln2_b"))
            stage.end()
            experts[2].route_act(act)
            stage.end()
            experts[2].act(act)
            stage.skip(2)

        @block.tensor
        def _(pe):
            stage = Stages(pe)
            credits(pe, "pe")
            stage.end()
            patch_pe(pe)
            stage.end()
            pe.wait_ge(load_resident, 32)
            ln_pe(pe, 1)
            stage.end()
            layer0.pe(pe)
            stage.end()
            layer0.offset_pe(pe)
            stage.end()
            turn_pe(pe, PROJ["L0"])
            stage.end()
            ln_pe(pe, 2)
            stage.end()
            quant_pe(pe)
            stage.end()
            ln_pe(pe, 3)
            stage.end()
            layer1.pe(pe)
            stage.end()
            proj_pe(pe, PROJ["L1"], weight_of("wo1", KT), KD, KT, bias=True)
            stage.end()
            ln_pe(pe, 4)
            stage.end()
            experts[0].route_pe(pe)
            stage.end()
            experts[0].pe(pe)
            stage.end()
            ln_pe(pe, 5)
            stage.end()
            layer2.pe(pe)
            stage.end()
            proj_pe(pe, PROJ["L2"], weight_of("out_proj", CI), P, CI)
            stage.end()
            ln_pe(pe, 6)
            stage.end()
            experts[1].route_pe(pe)
            stage.end()
            experts[1].pe(pe)
            stage.end()
            ln_pe(pe, 7)
            stage.end()
            layer3.pe(pe)
            stage.end()
            proj_pe(pe, PROJ["L3"], weight_of("wo3", 3), KF, 3, bias=True)
            stage.end()
            ln_pe(pe, 9)
            stage.end()
            layer3f.pe(pe)
            stage.end()
            proj_pe(pe, PROJ["L3f"], weight_of("wof", KT), KD, KT, bias=True)
            stage.end()
            ln_pe(pe, 10)
            stage.end()
            experts[2].route_pe(pe)
            stage.end()
            experts[2].pe(pe)
            stage.skip(2)

        @block.vector
        def _(dve):
            ch = Chain(dve, chains["dve"])
            stage = Stages(dve)
            credits(dve, "dve")
            stage.end()
            patch_dve(dve, ch)
            stage.end()
            dve.wait_ge(load_resident, 32)
            ln_dve(dve, ch, 0, h, keep=kept, turn=False)
            ch.settle()
            ln_dve(dve, ch, 1, kept)
            stage.end()
            layer0.dve(dve, ch)
            stage.end()
            layer0.offset_dve(dve, ch)
            stage.end()
            proj_dve(dve, PROJ["L0"], h)
            stage.end()
            ln_dve(dve, ch, 2, h)
            stage.end()
            quant_dve(dve, ch)
            stage.end()
            ln_dve(dve, ch, 3, h)
            stage.end()
            layer1.dve(dve, ch)
            stage.end()
            proj_dve(dve, PROJ["L1"], h)
            stage.end()
            ln_dve(dve, ch, 4, h)
            stage.end()
            experts[0].route_dve(dve, ch)
            stage.end()
            experts[0].dve(dve)
            stage.end()
            ln_dve(dve, ch, 5, h)
            stage.end()
            layer2.dve(dve, ch)
            stage.end()
            proj_dve(dve, PROJ["L2"], h)
            stage.end()
            ln_dve(dve, ch, 6, h)
            stage.end()
            experts[1].route_dve(dve, ch)
            stage.end()
            experts[1].dve(dve)
            stage.end()
            ln_dve(dve, ch, 7, h)
            stage.end()
            layer3.dve(dve, ch)
            stage.end()
            proj_dve(dve, PROJ["L3"], h)
            stage.end()
            ln_dve(dve, ch, 8, h, keep=kept, turn=False)
            ch.settle()
            ln_dve(dve, ch, 9, kept)
            stage.end()
            layer3f.dve(dve, ch)
            stage.end()
            proj_dve(dve, PROJ["L3f"], kept)
            stage.end()
            ln_dve(dve, ch, 10, kept)
            stage.end()
            experts[2].route_dve(dve, ch)
            stage.end()
            experts[2].dve(dve)
            stage.end()
            nc.vector.tensor_tensor(h[:, :], h[:, :], kept[:, :], ALU.add)
            stage.end()


def k_major(w, kt):
    w = np.asarray(w).T
    return w.reshape(kt, w.shape[0] // kt, w.shape[1]).transpose(1, 0, 2).reshape(w.shape[0] // kt, -1)


def with_bias(w, kt, bias):
    w = k_major(w, kt)
    row = np.zeros((1, w.shape[1]), w.dtype)
    row[0, :len(bias)] = np.asarray(bias)
    return np.concatenate([w, row], 0)


def by_feature(v, kt):
    v = np.asarray(v)
    return v.reshape(kt, -1).T


def constants():
    f = np.float32
    c = {"ident": np.eye(P, dtype=f), "ones": np.ones((P, P), f)}
    s, t = np.arange(P)[:, None] % SLOT, np.arange(SEQ)[None, :]
    c["causal"] = np.where((s < SEQ) & (t > s), f(MASKED), f(0)).astype(f)
    c["nreg"] = np.broadcast_to((f(1) / np.arange(1, SEQ + 1, dtype=f))[None], (KD, SEQ))
    c["nreg_row"] = np.where(s < SEQ, f(1) / (s + 1).astype(f), f(0)).astype(f)
    inv = f(1) / f(10000.0) ** (np.arange(0, HD, 2, dtype=f) / f(HD))
    ang = np.arange(SEQ, dtype=f)[None, :] * inv[:, None]
    c["cos"], c["sin"] = (np.tile(np.concatenate([fn(ang)] * 2, 0), (HPK, 1)).astype(f) for fn in (np.cos, np.sin))
    c["hmask"] = (np.arange(KD)[:, None] // HD == np.arange(HPK)[None]).astype(f)
    c["hmask8"] = (np.arange(KF)[:, None] // HD3 == np.arange(NH3)[None]).astype(f)
    row = np.arange(G3)[:, None, None] // SEQ
    c["vmask"] = (np.arange(KD)[None, None] // HD == 3 * np.arange(2)[None, :, None] + row).astype(f).reshape(G3, -1)
    c["vmask8"] = (np.arange(KF)[None, None] // HD3 == 3 * np.arange(3)[None, :, None] + row).astype(f).reshape(G3, -1)
    third, when = np.arange(G3)[:, None] % SEQ, np.arange(SEQ)
    c["upto"], c["own"] = (third <= t).astype(f), (third == t).astype(f)
    c["rise"] = np.broadcast_to((FADE ** -when.astype(np.float64)).astype(f)[None], (P, SEQ))
    c["fall"] = np.broadcast_to((FADE ** when.astype(np.float64)).astype(f)[None], (P, SEQ))
    c["descending"] = np.broadcast_to(np.arange(EXPERTS, 0, -1, dtype=f)[None], (P, EXPERTS))
    c["rot_sign"] = np.where(np.arange(KD) % HD < HD // 2, f(-1), f(1)).astype(f)[:, None]
    return c


def lay_out(i):
    a = {n: np.asarray(v) for n, v in i.items()}
    rot = np.arange(DIM).reshape(HEADS, 2, HD // 2)[:, ::-1].reshape(-1)
    parts = [w * DIM + np.arange(NH3)[:, None] * 24 + s * HD3 + np.arange(HD3)[None] for w, s in
             ((0, 1), (0, 2), (1, 0), (1, 1), (1, 2), (2, 0), (2, 1), (2, 2))]
    parts = np.concatenate([x.reshape(-1) for x in parts])
    x_proj = np.zeros((XP_COLS, INNER), np.float32)
    for at, (start, n) in zip(XP_AT, ((0, RANK), (RANK, STATE), (RANK + STATE, STATE))):
        x_proj[at:at + n] = a["L2_attn_x_proj_w"][start:start + n]
    x_proj = k_major(x_proj, CI)
    packed = constants()
    packed.update({
        "wqk": k_major(a["L0_attn_W_qk"], KT),
        "ln_w": by_feature(a["L0_attn_ln_w"], KT),
        "bias_int8": np.broadcast_to(a["L0_ffn_bias"][None], (P, DIM)),
        "qkv1": k_major(np.concatenate([a["L1_attn_Wq"], a["L1_attn_Wk"], a["L1_attn_Wv"]], 0), KT),
        "bq": by_feature(a["L1_attn_bq"], KT), "bk": by_feature(a["L1_attn_bk"], KT), "bv": by_feature(a["L1_attn_bv"], KT),
        "bq_turned": by_feature(a["L1_attn_bq"][rot], KT), "bk_turned": by_feature(a["L1_attn_bk"][rot], KT),
        "wo1": with_bias(a["L1_attn_Wo"], KT, a["L1_attn_bo"]),
        "router1": k_major(a["L1_ffn_Wr"], KT), "b2_1": a["L1_ffn_bo"],
        "b1_1": a["L1_ffn_bi"].reshape(EXPERTS * FT, P).T,
        "in_proj": k_major(a["L2_attn_in_proj_w"], KT), "x_proj": x_proj,
        "dt_head": a["L2_attn_dt_head_w"].T, "dt_b": by_feature(a["L2_attn_dt_head_b"], CI),
        "conv_w": a["L2_attn_conv_w"].reshape(CI, P, 4).transpose(1, 0, 2).reshape(P, -1),
        "conv_b": by_feature(a["L2_attn_conv_b"], CI), "d": by_feature(a["L2_attn_D"], CI),
        "out_proj": k_major(a["L2_attn_out_proj_w"], CI),
        "router2": k_major(a["L2_ffn_w_router"].T, KT),
        "qkv3": k_major(a["L3_attn_w_qkv"][parts], KT), "wo3": with_bias(a["L3_attn_w_proj"], 3, a["L3_attn_b_proj"]),
        "qkvf": k_major(a["L3_ffn_qkv_w"], KT), "wof": with_bias(a["L3_ffn_proj_w"], KT, a["L3_ffn_proj_b"]),
        "ln1_g": by_feature(a["L3_ffn_ln1_g"], KT), "ln1_b": by_feature(a["L3_ffn_ln1_b"], KT),
        "ln2_g": by_feature(a["L3_ffn_ln2_g"], KT), "ln2_b": by_feature(a["L3_ffn_ln2_b"], KT),
        "router3f": k_major(a["L3_ffn_gate_w"], KT), "gate_b": a["L3_ffn_gate_b"][:, None],
        "b1_3f": a["L3_ffn_b1"].reshape(EXPERTS * FT, P).T, "b2_3f": a["L3_ffn_b2"],
    })
    total = sum(v.shape[1] for v in packed.values())
    resident, spec, at = np.zeros((P, total), np.float32), {"resident": total}, 0
    for n, v in packed.items():
        resident[:v.shape[0], at:at + v.shape[1]] = v
        spec[n] = ("resident", v.shape[0], at, v.shape[1])
        at += v.shape[1]
    patches = a["x"].reshape(IMAGES, 3, 6, 16, 6, 16).transpose(0, 2, 4, 1, 3, 5).reshape(IMAGES, 36, PATCH_K * P)
    padded = np.zeros((IMAGES, SEQ, PATCH_K * P), np.float32)
    padded[:, 2:] = patches
    first = lambda w: np.ascontiguousarray(w.transpose(0, 2, 1).reshape(EXPERTS, KT, KD, HIDDEN).transpose(0, 2, 1, 3))
    second = lambda w: np.ascontiguousarray(w.transpose(0, 2, 1).reshape(EXPERTS, FT, P, DIM).transpose(0, 2, 1, 3))
    swap = lambda w: w.transpose(0, 2, 1)
    wo0 = a["L0_attn_W_o"].reshape(DIM, HEADS, KT, KD).transpose(3, 2, 1, 0)
    arrays = {
        "patches": padded.reshape(TILES, P, PATCH_K, P).transpose(0, 3, 2, 1),
        "w_emb": a["L0_tok_W_emb"].reshape(PATCH_K, P, DIM).transpose(1, 0, 2),
        "select38": np.tile(np.eye(SEQ, dtype=np.float32), (1, IMAGES)),
        "cls_tok": a["cls_tok"].reshape(1, DIM), "cls_token": a["L0_tok_cls_token"].reshape(1, DIM),
        "pos": a["L0_tok_pos_embedding"].reshape(SEQ - 1, DIM), "b_emb": a["L0_tok_b_emb"].reshape(1, DIM),
        "wte": a["L0_attn_wte"],
        "wo0": wo0.reshape(KD, -1),
        "w_int8": np.ascontiguousarray(a["L0_ffn_weight_t"].reshape(KT, KD, DIM).transpose(1, 0, 2).reshape(KD, -1)).view(np.int32),
        "resident": resident,
        "w1_1": first(a["L1_ffn_Wi"]), "w2_1": second(a["L1_ffn_Wo"]),
        "w1_2": first(swap(a["L2_ffn_wi"])), "w2_2": second(swap(a["L2_ffn_wo"])),
        "w1_3f": first(a["L3_ffn_w1"]), "w2_3f": second(a["L3_ffn_w2"]),
    }
    return {n: np.ascontiguousarray(v) for n, v in arrays.items()}, spec


def kernel(**inputs):
    import concourse.bacc as bacc
    from concourse.bass_utils import run_bass_kernel_spmd

    arrays, spec = lay_out(inputs)
    nc = bacc.Bacc("TRN2", target_bir_lowering=False, num_devices=1)
    t_in = {n: nc.dram_tensor(f"in_{n}", v.shape, mybir.dt.from_np(v.dtype), kind="ExternalInput").ap() for n, v in arrays.items()}
    out = nc.dram_tensor("tower_out", (IMAGES, SEQ, DIM), F32, kind="ExternalOutput").ap()
    build(nc, spec, t_in, out)
    r = run_bass_kernel_spmd(nc, [{f"in_{n}": v for n, v in arrays.items()}], core_ids=[0])
    return r.results[0]["tower_out"]
```
